# Optimizing a Trainium2 kernel written in Bass

```python
import numpy as np
import jax
import jax.numpy as jnp

def _softmax(x, axis=-1):
    return jax.nn.softmax(x, axis=axis)

def _gelu(x):
    return jax.nn.gelu(x, approximate=True)

def _silu(x):
    return jax.nn.silu(x)

def _sigmoid(x):
    return jax.nn.sigmoid(x)

def _layernorm(x, axis=-1, eps=1e-05):
    m = jnp.mean(x, axis=axis, keepdims=True)
    v = jnp.var(x, axis=axis, keepdims=True)
    return (x - m) / jnp.sqrt(v + eps)

def _scatter_add(tgt, idx, src, axis=0):
    return tgt.at[idx].add(src)

def _segment_sum(src, seg, n):
    return jax.ops.segment_sum(src, seg, n)
kernel_name = 'mk_decoder_postln_d2_seqx_r8_c00919'

def setup_inputs(seed: int=0):
    np.random.seed(seed)
    _w = jnp.asarray

    def _rec_inputs():
        import jax
        import jax.numpy as jnp
        _rk = jax.random.key(seed)
        x = 7.22e-05 + 1 * jax.random.normal(jax.random.fold_in(_rk, 1), (32, 64, 256), jnp.float32)
        _lenS = 64 - jax.random.randint(jax.random.fold_in(_rk, 7), (32,), 0, max(1, 64 // 4) + 1, jnp.int32)
        _lenS2 = 64 - jax.random.randint(jax.random.fold_in(_rk, 8), (32,), 0, max(1, 64 // 4) + 1, jnp.int32)
        _ctx_2048P = jax.random.normal(jax.random.fold_in(_rk, 11), (32, 16, 256), jnp.float32)
        _ctx_2048c = jax.random.dirichlet(jax.random.fold_in(_rk, 511), 0.3 * jnp.ones((16,), jnp.float32), (32, 64))
        _ctx_2048t = jnp.einsum('bsk,bkd->bsd', _ctx_2048c, _ctx_2048P)
        _ctx_2048t = _ctx_2048t * jax.lax.rsqrt(jnp.mean(jnp.square(_ctx_2048t)) + 1e-12) * 0.953939
        ctx_2048 = 4.13588e-05 + 0.999923 * (_ctx_2048t + 0.3 * jax.random.normal(jax.random.fold_in(_rk, 611), (32, 64, 256), jnp.float32))
        _validS = jnp.arange(64)[None, :] < _lenS[:, None]
        _validS2 = jnp.arange(64)[None, :] < _lenS2[:, None]
        _causal = jnp.tril(jnp.ones((64, 64), dtype=bool))
        mask_BxS2_bk0 = jnp.logical_not(jnp.broadcast_to(_validS2[:, :], (32, 64)))
        return (x, ctx_2048, mask_BxS2_bk0)
    x, ctx_2048, mask_BxS2_bk0 = _rec_inputs()

    def _L0_attn_setup():
        import jax, jax.numpy as jnp
        import numpy as np
        import math
        N_EMBED = 256
        N_HEAD = 16
        KV_PER_HEAD = 4
        N_GROUPS = N_HEAD // KV_PER_HEAD
        HEAD_DIM = N_EMBED // N_HEAD
        EPS = 1e-06
        ROPE_BASE = 10000.0

        def rope_tables(seq_len, dim):
            inv_freq = 1.0 / ROPE_BASE ** (jnp.arange(0, dim, 2, dtype=jnp.float32) / dim)
            pos = jnp.arange(seq_len, dtype=jnp.float32)
            freqs = pos[:, None] * inv_freq[None, :]
            return (jnp.cos(freqs), jnp.sin(freqs))

        def apply_rope(x, cos, sin):
            x1 = x[..., ::2]
            x2 = x[..., 1::2]
            c = cos[None, None, :, :]
            s = sin[None, None, :, :]
            r1 = x1 * c - x2 * s
            r2 = x1 * s + x2 * c
            return jnp.stack([r1, r2], axis=-1).reshape(x.shape)
        key = jax.random.key(seed)
        ks = jax.random.split(key, 10)
        B, T, C = (2, 256, N_EMBED)
        kv_dim = N_GROUPS * HEAD_DIM
        std = 0.02
        x = jax.random.normal(ks[0], (B, T, C), dtype=jnp.float32)
        Wq = jax.random.normal(ks[1], (C, C), dtype=jnp.float32) * std
        bq = jnp.zeros((C,), dtype=jnp.float32)
        Wk = jax.random.normal(ks[2], (C, kv_dim), dtype=jnp.float32) * std
        bk = jnp.zeros((kv_dim,), dtype=jnp.float32)
        Wv = jax.random.normal(ks[3], (C, kv_dim), dtype=jnp.float32) * std
        bv = jnp.zeros((kv_dim,), dtype=jnp.float32)
        Wo = jax.random.normal(ks[4], (C, C), dtype=jnp.float32) * std
        bo = jnp.zeros((C,), dtype=jnp.float32)
        alpha = jnp.ones((N_HEAD,), dtype=jnp.float32)
        return {'x': x, 'Wq': Wq, 'bq': bq, 'Wk': Wk, 'bk': bk, 'Wv': Wv, 'bv': bv, 'Wo': Wo, 'bo': bo, 'alpha': alpha}
    _L0_attn_all = _L0_attn_setup()
    _L0_attn_in = {k: v for k, v in _L0_attn_all.items() if k in ('Wq', 'bq', 'Wk', 'bk', 'Wv', 'bv', 'Wo', 'bo', 'alpha')}
    del _L0_attn_all

    def _L0_xattn_setup():
        import jax, jax.numpy as jnp
        import numpy as np
        N_HEAD = 8
        key = jax.random.key(seed)
        k1, k2, k3 = jax.random.split(key, 3)
        B, D, L = (4, 128, 256)
        q = jax.random.normal(k1, (B, D, L), dtype=jnp.float32)
        k = jax.random.normal(k2, (B, D, L), dtype=jnp.float32)
        v = jax.random.normal(k3, (B, D, L), dtype=jnp.float32)
        gamma = jnp.ones((), dtype=jnp.float32)
        return {'q': q, 'k': k, 'v': v, 'gamma': gamma}
    _L0_xattn_all = _L0_xattn_setup()
    _L0_xattn_in = {k: v for k, v in _L0_xattn_all.items() if k in ('gamma',)}
    del _L0_xattn_all

    def _L0_ffn_setup():
        import jax, jax.numpy as jnp
        import numpy as np
        D = 256
        F = 176
        E = 8
        K = 2
        FS = 352
        B, S = (2, 128)
        key = jax.random.key(seed)
        ks = jax.random.split(key, 9)
        sc = 0.02
        return {'x': jax.random.normal(ks[0], (B, S, D), dtype=jnp.float32), 'Wr': jax.random.normal(ks[1], (E, D), dtype=jnp.float32) * sc, 'Wg': jax.random.normal(ks[2], (E, F, D), dtype=jnp.float32) * sc, 'Wu': jax.random.normal(ks[3], (E, F, D), dtype=jnp.float32) * sc, 'Wd': jax.random.normal(ks[4], (E, D, F), dtype=jnp.float32) * sc, 'Wsg': jax.random.normal(ks[5], (FS, D), dtype=jnp.float32) * sc, 'Wsu': jax.random.normal(ks[6], (FS, D), dtype=jnp.float32) * sc, 'Wsd': jax.random.normal(ks[7], (D, FS), dtype=jnp.float32) * sc}
    _L0_ffn_all = _L0_ffn_setup()
    _L0_ffn_in = {k: v for k, v in _L0_ffn_all.items() if k in ('Wr', 'Wg', 'Wu', 'Wd', 'Wsg', 'Wsu', 'Wsd')}
    del _L0_ffn_all

    def _L1_attn_setup():
        import jax, jax.numpy as jnp
        import numpy as np
        D_MODEL = 256
        D_INNER = 512
        D_XB = 128
        D_STATE = 128
        HEADDIM = 64
        NHEADS = D_INNER // HEADDIM
        NGROUPS = D_INNER // D_STATE
        HPG = NHEADS // NGROUPS
        REPEAT = D_INNER // D_XB
        XB_GROUPS = D_XB // D_STATE
        CHUNK = 32
        D_CONV = 4
        CONV_DIM = D_INNER + 2 * D_XB
        D_IN_PROJ = D_INNER + 2 * D_XB + D_INNER + NHEADS
        NORM_GS = D_INNER // NGROUPS
        EPS = 1e-05

        def _segsum(x):
            T = x.shape[-1]
            cs = jnp.cumsum(x, axis=-1)
            seg = cs[..., :, None] - cs[..., None, :]
            mask = jnp.tril(jnp.ones((T, T), bool))
            return jnp.where(mask, seg, -jnp.inf)

        def _chunked_scan(x, dt, A, Bh, Ch, D):
            b, l, h, p = x.shape
            c = l // CHUNK
            xc = x.reshape(b, c, CHUNK, h, p)
            dtc = dt.reshape(b, c, CHUNK, h)
            Bc = Bh.reshape(b, c, CHUNK, h, D_STATE)
            Cc = Ch.reshape(b, c, CHUNK, h, D_STATE)
            dA = jnp.transpose(dtc * A, (0, 3, 1, 2))
            dA_cs = jnp.cumsum(dA, axis=-1)
            L = jnp.exp(_segsum(dA))
            xdt = xc * dtc[..., None]
            G = jnp.einsum('bclhn,bcshn->bhcls', Cc, Bc)
            Y_diag = jnp.einsum('bhcls,bcshp->bclhp', G * L, xdt)
            decay_states = jnp.exp(dA_cs[..., -1:] - dA_cs)
            states = jnp.einsum('bcshn,bhcs,bcshp->bchpn', Bc, decay_states, xdt)
            chunk_decay = jnp.exp(dA_cs[..., -1])
            states_t = jnp.moveaxis(states, 1, 0)
            decay_t = jnp.moveaxis(chunk_decay, -1, 0)

            def step(carry, inp):
                s, d = inp
                return (carry * d[..., None, None] + s, carry)
            _, prev = jax.lax.scan(step, jnp.zeros_like(states_t[0]), (states_t, decay_t))
            prev = jnp.moveaxis(prev, 0, 1)
            Y_off = jnp.einsum('bclhn,bchpn,bhcl->bclhp', Cc, prev, jnp.exp(dA_cs))
            y = Y_diag + Y_off + xc * D[:, None]
            return y.reshape(b, l, h, p)
        key = jax.random.key(seed)
        ks = jax.random.split(key, 8)
        u = jax.random.normal(ks[0], (2, 256, D_MODEL), jnp.float32)
        W_in = jax.random.normal(ks[1], (D_IN_PROJ, D_MODEL), jnp.float32) * 0.02
        conv_w = jax.random.normal(ks[2], (CONV_DIM, D_CONV), jnp.float32) * 0.2
        conv_b = jnp.zeros((CONV_DIM,), jnp.float32)
        dt = jnp.exp(jax.random.uniform(ks[3], (NHEADS,), jnp.float32) * (np.log(0.1) - np.log(0.001)) + np.log(0.001))
        dt_bias = dt + jnp.log(-jnp.expm1(-dt))
        A_log = jnp.log(jax.random.uniform(ks[4], (NHEADS,), jnp.float32, minval=1.0, maxval=16.0))
        D = jnp.ones((NHEADS,), jnp.float32)
        norm_weight = jnp.ones((D_INNER,), jnp.float32)
        W_out = jax.random.normal(ks[5], (D_MODEL, D_INNER), jnp.float32) * 0.02
        return dict(u=u, W_in=W_in, conv_w=conv_w, conv_b=conv_b, dt_bias=dt_bias, A_log=A_log, D=D, norm_weight=norm_weight, W_out=W_out)
    _L1_attn_all = _L1_attn_setup()
    _L1_attn_in = {k: v for k, v in _L1_attn_all.items() if k in ('W_in', 'conv_w', 'conv_b', 'dt_bias', 'A_log', 'D', 'norm_weight', 'W_out')}
    del _L1_attn_all

    def _L1_xattn_setup():
        import jax, jax.numpy as jnp
        import numpy as np
        H = 256
        NH = 16
        HD = H // NH
        EPS = 1e-06

        def rmsnorm(x, w, eps=EPS):
            var = jnp.mean(x * x, axis=-1, keepdims=True)
            return x * jax.lax.rsqrt(var + eps) * w
        key = jax.random.key(seed)
        ks = jax.random.split(key, 9)
        B, L, M = (4, 512, 32)
        s = 1.0 / np.sqrt(H)
        return {'hidden_states': jax.random.normal(ks[0], (B, L, H), dtype=jnp.float32), 'memory_tokens': jax.random.normal(ks[1], (B, M, H), dtype=jnp.float32), 'memory_mask': jax.random.randint(ks[2], (B, M), 0, 2).astype(bool), 'norm_w': jnp.ones((H,), dtype=jnp.float32), 'wq': jax.random.normal(ks[3], (H, H), dtype=jnp.float32) * s, 'wk': jax.random.normal(ks[4], (H, H), dtype=jnp.float32) * s, 'wv': jax.random.normal(ks[5], (H, H), dtype=jnp.float32) * s, 'wo': jax.random.normal(ks[6], (H, H), dtype=jnp.float32) * s, 'wg': jax.random.normal(ks[7], (H, H), dtype=jnp.float32) * s}
    _L1_xattn_all = _L1_xattn_setup()
    _L1_xattn_in = {k: v for k, v in _L1_xattn_all.items() if k in ('norm_w', 'wq', 'wk', 'wv', 'wo', 'wg')}
    del _L1_xattn_all

    def _L1_ffn_setup():
        import jax, jax.numpy as jnp
        import numpy as np
        TOP_K = 2
        LORA_SCALE = 32.0 / 16.0
        key = jax.random.key(seed)
        ks = jax.random.split(key, 11)
        B, S, D, F, E, R = (4, 128, 256, 704, 8, 16)
        sd, sf = (1.0 / np.sqrt(D), 1.0 / np.sqrt(F))
        return {'x': jax.random.normal(ks[0], (B, S, D), jnp.float32), 'gate_w': jax.random.normal(ks[1], (E, D), jnp.float32) * 0.02, 'w1': jax.random.normal(ks[2], (F, D), jnp.float32) * sd, 'w3': jax.random.normal(ks[3], (F, D), jnp.float32) * sd, 'w2': jax.random.normal(ks[4], (D, F), jnp.float32) * sf, 'a1': jax.random.normal(ks[5], (E, R, D), jnp.float32) * sd, 'b1': jax.random.normal(ks[6], (E, F, R), jnp.float32) * 0.01, 'a3': jax.random.normal(ks[7], (E, R, D), jnp.float32) * sd, 'b3': jax.random.normal(ks[8], (E, F, R), jnp.float32) * 0.01, 'a2': jax.random.normal(ks[9], (E, R, F), jnp.float32) * sf, 'b2': jax.random.normal(ks[10], (E, D, R), jnp.float32) * 0.01}
    _L1_ffn_all = _L1_ffn_setup()
    _L1_ffn_in = {k: v for k, v in _L1_ffn_all.items() if k in ('gate_w', 'w1', 'w3', 'w2', 'a1', 'b1', 'a3', 'b3', 'a2', 'b2')}
    del _L1_ffn_all
    return {'x': x, 'ctx_2048': ctx_2048, 'mask_BxS2_bk0': mask_BxS2_bk0, 'L0_attn_Wq': _L0_attn_in['Wq'], 'L0_attn_bq': _L0_attn_in['bq'], 'L0_attn_Wk': _L0_attn_in['Wk'], 'L0_attn_bk': _L0_attn_in['bk'], 'L0_attn_Wv': _L0_attn_in['Wv'], 'L0_attn_bv': _L0_attn_in['bv'], 'L0_attn_Wo': _L0_attn_in['Wo'], 'L0_attn_bo': _L0_attn_in['bo'], 'L0_attn_alpha': _L0_attn_in['alpha'], 'L0_xattn_gamma': _L0_xattn_in['gamma'], 'L0_ffn_Wr': _L0_ffn_in['Wr'], 'L0_ffn_Wg': _L0_ffn_in['Wg'], 'L0_ffn_Wu': _L0_ffn_in['Wu'], 'L0_ffn_Wd': _L0_ffn_in['Wd'], 'L0_ffn_Wsg': _L0_ffn_in['Wsg'], 'L0_ffn_Wsu': _L0_ffn_in['Wsu'], 'L0_ffn_Wsd': _L0_ffn_in['Wsd'], 'L1_attn_W_in': _L1_attn_in['W_in'], 'L1_attn_conv_w': _L1_attn_in['conv_w'], 'L1_attn_conv_b': _L1_attn_in['conv_b'], 'L1_attn_dt_bias': _L1_attn_in['dt_bias'], 'L1_attn_A_log': _L1_attn_in['A_log'], 'L1_attn_D': _L1_attn_in['D'], 'L1_attn_norm_weight': _L1_attn_in['norm_weight'], 'L1_attn_W_out': _L1_attn_in['W_out'], 'L1_xattn_norm_w': _L1_xattn_in['norm_w'], 'L1_xattn_wq': _L1_xattn_in['wq'], 'L1_xattn_wk': _L1_xattn_in['wk'], 'L1_xattn_wv': _L1_xattn_in['wv'], 'L1_xattn_wo': _L1_xattn_in['wo'], 'L1_xattn_wg': _L1_xattn_in['wg'], 'L1_ffn_gate_w': _L1_ffn_in['gate_w'], 'L1_ffn_w1': _L1_ffn_in['w1'], 'L1_ffn_w3': _L1_ffn_in['w3'], 'L1_ffn_w2': _L1_ffn_in['w2'], 'L1_ffn_a1': _L1_ffn_in['a1'], 'L1_ffn_b1': _L1_ffn_in['b1'], 'L1_ffn_a3': _L1_ffn_in['a3'], 'L1_ffn_b3': _L1_ffn_in['b3'], 'L1_ffn_a2': _L1_ffn_in['a2'], 'L1_ffn_b2': _L1_ffn_in['b2']}

def reference(x, ctx_2048, mask_BxS2_bk0, L0_attn_Wq, L0_attn_bq, L0_attn_Wk, L0_attn_bk, L0_attn_Wv, L0_attn_bv, L0_attn_Wo, L0_attn_bo, L0_attn_alpha, L0_xattn_gamma, L0_ffn_Wr, L0_ffn_Wg, L0_ffn_Wu, L0_ffn_Wd, L0_ffn_Wsg, L0_ffn_Wsu, L0_ffn_Wsd, L1_attn_W_in, L1_attn_conv_w, L1_attn_conv_b, L1_attn_dt_bias, L1_attn_A_log, L1_attn_D, L1_attn_norm_weight, L1_attn_W_out, L1_xattn_norm_w, L1_xattn_wq, L1_xattn_wk, L1_xattn_wv, L1_xattn_wo, L1_xattn_wg, L1_ffn_gate_w, L1_ffn_w1, L1_ffn_w3, L1_ffn_w2, L1_ffn_a1, L1_ffn_b1, L1_ffn_a3, L1_ffn_b3, L1_ffn_a2, L1_ffn_b2):
    import jax
    import jax.numpy as jnp

    def _L0_attn_ref(x, Wq, bq, Wk, bk, Wv, bv, Wo, bo, alpha):
        import jax, jax.numpy as jnp
        import numpy as np
        import math
        N_EMBED = 256
        N_HEAD = 16
        KV_PER_HEAD = 4
        N_GROUPS = N_HEAD // KV_PER_HEAD
        HEAD_DIM = N_EMBED // N_HEAD
        EPS = 1e-06
        ROPE_BASE = 10000.0

        def rope_tables(seq_len, dim):
            inv_freq = 1.0 / ROPE_BASE ** (jnp.arange(0, dim, 2, dtype=jnp.float32) / dim)
            pos = jnp.arange(seq_len, dtype=jnp.float32)
            freqs = pos[:, None] * inv_freq[None, :]
            return (jnp.cos(freqs), jnp.sin(freqs))

        def apply_rope(x, cos, sin):
            x1 = x[..., ::2]
            x2 = x[..., 1::2]
            c = cos[None, None, :, :]
            s = sin[None, None, :, :]
            r1 = x1 * c - x2 * s
            r2 = x1 * s + x2 * c
            return jnp.stack([r1, r2], axis=-1).reshape(x.shape)
        B, T, C = x.shape
        hd = HEAD_DIM
        q = (x @ Wq + bq).reshape(B, T, N_HEAD, hd).transpose(0, 2, 1, 3)
        k = (x @ Wk + bk).reshape(B, T, N_GROUPS, hd).transpose(0, 2, 1, 3)
        v = (x @ Wv + bv).reshape(B, T, N_GROUPS, hd).transpose(0, 2, 1, 3)
        k = jnp.repeat(k, KV_PER_HEAD, axis=1)
        v = jnp.repeat(v, KV_PER_HEAD, axis=1)
        q_hat = q / (jnp.linalg.norm(q, axis=-1, keepdims=True) + EPS)
        k_hat = k / (jnp.linalg.norm(k, axis=-1, keepdims=True) + EPS)
        factor = (alpha * math.sqrt(hd)).reshape(1, N_HEAD, 1, 1)
        q_scaled = q_hat * factor
        cos, sin = rope_tables(T, hd)
        q_r = apply_rope(q_scaled, cos, sin)
        k_r = apply_rope(k_hat, cos, sin)
        scores = jnp.einsum('bhtd,bhsd->bhts', q_r, k_r) / math.sqrt(hd)
        causal = jnp.tril(jnp.ones((T, T), dtype=bool))
        scores = jnp.where(causal[None, None], scores, -jnp.inf)
        attn = jax.nn.softmax(scores, axis=-1)
        y = jnp.einsum('bhts,bhsd->bhtd', attn, v)
        y = y.transpose(0, 2, 1, 3).reshape(B, T, C)
        return y @ Wo + bo

    def _L0_xattn_ref(q, k, v, gamma):
        import jax, jax.numpy as jnp
        import numpy as np
        N_HEAD = 8
        B, Dq, Lq = q.shape
        Dv, Lk = (v.shape[-2], v.shape[-1])
        h = N_HEAD
        dq = Dq // h
        dv = Dv // h
        qh = q.reshape(B, h, dq, Lq)
        kh = k.reshape(B, h, dq, Lk)
        vh = v.reshape(B, h, dv, Lk)
        scale = 1.0 / jnp.sqrt(jnp.asarray(dq, dtype=q.dtype))
        qk = jnp.einsum('bhdq,bhdl->bhql', qh, kh) * scale
        sm = jax.nn.softmax(qk, axis=-1)
        ret = jnp.einsum('bhql,bhdl->bhdq', sm, vh)
        ret = ret.reshape(B, Dv, Lq)
        return gamma * ret

    def _L0_ffn_ref(x, Wr, Wg, Wu, Wd, Wsg, Wsu, Wsd):
        import jax, jax.numpy as jnp
        import numpy as np
        D = 256
        F = 176
        E = 8
        K = 2
        FS = 352
        B, S = (2, 128)
        silu = jax.nn.silu
        sg = silu(jnp.einsum('bsd,fd->bsf', x, Wsg))
        su = jnp.einsum('bsd,fd->bsf', x, Wsu)
        shared_out = jnp.einsum('bsf,df->bsd', sg * su, Wsd)
        logits = jnp.einsum('bsd,ed->bse', x, Wr)
        scores = jax.nn.softmax(logits, axis=-1)
        topk_scores, topk_idx = jax.lax.top_k(scores, K)
        w_full = jnp.sum(jax.nn.one_hot(topk_idx, E, dtype=x.dtype) * topk_scores[..., None], axis=-2)
        g = silu(jnp.einsum('bsd,efd->bsef', x, Wg))
        u = jnp.einsum('bsd,efd->bsef', x, Wu)
        out_e = jnp.einsum('bsef,edf->bsed', g * u, Wd)
        routed_out = jnp.einsum('bsed,bse->bsd', out_e, w_full)
        return routed_out + shared_out

    def _L1_attn_ref(u, W_in, conv_w, conv_b, dt_bias, A_log, D, norm_weight, W_out):
        import jax, jax.numpy as jnp
        import numpy as np
        D_MODEL = 256
        D_INNER = 512
        D_XB = 128
        D_STATE = 128
        HEADDIM = 64
        NHEADS = D_INNER // HEADDIM
        NGROUPS = D_INNER // D_STATE
        HPG = NHEADS // NGROUPS
        REPEAT = D_INNER // D_XB
        XB_GROUPS = D_XB // D_STATE
        CHUNK = 32
        D_CONV = 4
        CONV_DIM = D_INNER + 2 * D_XB
        D_IN_PROJ = D_INNER + 2 * D_XB + D_INNER + NHEADS
        NORM_GS = D_INNER // NGROUPS
        EPS = 1e-05

        def _segsum(x):
            T = x.shape[-1]
            cs = jnp.cumsum(x, axis=-1)
            seg = cs[..., :, None] - cs[..., None, :]
            mask = jnp.tril(jnp.ones((T, T), bool))
            return jnp.where(mask, seg, -jnp.inf)

        def _chunked_scan(x, dt, A, Bh, Ch, D):
            b, l, h, p = x.shape
            c = l // CHUNK
            xc = x.reshape(b, c, CHUNK, h, p)
            dtc = dt.reshape(b, c, CHUNK, h)
            Bc = Bh.reshape(b, c, CHUNK, h, D_STATE)
            Cc = Ch.reshape(b, c, CHUNK, h, D_STATE)
            dA = jnp.transpose(dtc * A, (0, 3, 1, 2))
            dA_cs = jnp.cumsum(dA, axis=-1)
            L = jnp.exp(_segsum(dA))
            xdt = xc * dtc[..., None]
            G = jnp.einsum('bclhn,bcshn->bhcls', Cc, Bc)
            Y_diag = jnp.einsum('bhcls,bcshp->bclhp', G * L, xdt)
            decay_states = jnp.exp(dA_cs[..., -1:] - dA_cs)
            states = jnp.einsum('bcshn,bhcs,bcshp->bchpn', Bc, decay_states, xdt)
            chunk_decay = jnp.exp(dA_cs[..., -1])
            states_t = jnp.moveaxis(states, 1, 0)
            decay_t = jnp.moveaxis(chunk_decay, -1, 0)

            def step(carry, inp):
                s, d = inp
                return (carry * d[..., None, None] + s, carry)
            _, prev = jax.lax.scan(step, jnp.zeros_like(states_t[0]), (states_t, decay_t))
            prev = jnp.moveaxis(prev, 0, 1)
            Y_off = jnp.einsum('bclhn,bchpn,bhcl->bclhp', Cc, prev, jnp.exp(dA_cs))
            y = Y_diag + Y_off + xc * D[:, None]
            return y.reshape(b, l, h, p)
        b, l, _ = u.shape
        zxbcdt = u @ W_in.T
        z, xBC, dt = jnp.split(zxbcdt, [D_INNER, D_INNER + CONV_DIM], axis=-1)
        xp = jnp.pad(xBC, ((0, 0), (D_CONV - 1, 0), (0, 0)))
        conv = conv_b
        for k in range(D_CONV):
            conv = conv + xp[:, k:k + l, :] * conv_w[:, k]
        xBC = jax.nn.silu(conv)
        x, B, C = jnp.split(xBC, [D_XB, 2 * D_XB], axis=-1)
        x = jnp.repeat(x.reshape(b, l, XB_GROUPS, D_STATE), REPEAT, axis=2).reshape(b, l, D_INNER)
        B = jnp.repeat(B.reshape(b, l, XB_GROUPS, D_STATE), REPEAT, axis=2)
        C = C.reshape(b, l, NGROUPS, D_STATE)
        Bh = jnp.repeat(B, HPG, axis=2)
        Ch = jnp.repeat(C, HPG, axis=2)
        xh = x.reshape(b, l, NHEADS, HEADDIM)
        dt = jax.nn.softplus(dt + dt_bias)
        A = -jnp.exp(A_log)
        y = _chunked_scan(xh, dt, A, Bh, Ch, D).reshape(b, l, D_INNER)
        y = y * jax.nn.silu(z)
        yg = y.reshape(b, l, NGROUPS, NORM_GS)
        rstd = jax.lax.rsqrt(jnp.mean(yg * yg, axis=-1, keepdims=True) + EPS)
        y = (yg * rstd).reshape(b, l, D_INNER) * norm_weight
        return y @ W_out.T

    def _L1_xattn_ref(hidden_states, memory_tokens, memory_mask, norm_w, wq, wk, wv, wo, wg):
        import jax, jax.numpy as jnp
        import numpy as np
        H = 256
        NH = 16
        HD = H // NH
        EPS = 1e-06

        def rmsnorm(x, w, eps=EPS):
            var = jnp.mean(x * x, axis=-1, keepdims=True)
            return x * jax.lax.rsqrt(var + eps) * w
        B, L, C = hidden_states.shape
        M = memory_tokens.shape[1]
        scale = HD ** (-0.5)
        x = rmsnorm(hidden_states, norm_w)
        q = (x @ wq.T).reshape(B, L, NH, HD)
        k = (memory_tokens @ wk.T).reshape(B, M, NH, HD)
        v = (memory_tokens @ wv.T).reshape(B, M, NH, HD)
        attn = jnp.einsum('blhd,bmhd->bhlm', q, k) * scale
        attn = jnp.where(memory_mask[:, None, None, :], attn, -jnp.inf)
        attn = jax.nn.softmax(attn, axis=-1)
        attn = jnp.nan_to_num(attn, nan=0.0)
        out = jnp.einsum('bhlm,bmhd->blhd', attn, v).reshape(B, L, C)
        out = out @ wo.T
        gate = jax.nn.sigmoid(x @ wg.T)
        return gate * out

    def _L1_ffn_ref(x, gate_w, w1, w3, w2, a1, b1, a3, b3, a2, b2):
        import jax, jax.numpy as jnp
        import numpy as np
        TOP_K = 2
        LORA_SCALE = 32.0 / 16.0
        B, S, D = x.shape
        E = gate_w.shape[0]
        xf = x.reshape(B * S, D)
        N = xf.shape[0]
        logits = xf @ gate_w.T
        top_w, top_i = jax.lax.top_k(logits, TOP_K)
        routing = jax.nn.softmax(top_w, axis=-1)
        w_full = jnp.zeros((N, E), x.dtype).at[jnp.arange(N)[:, None], top_i].add(routing)
        base1 = xf @ w1.T
        base3 = xf @ w3.T

        def expert_step(acc, p):
            A1, B1, A3, B3, A2, B2, we = p
            h1 = base1 + xf @ A1.T @ B1.T * LORA_SCALE
            h3 = base3 + xf @ A3.T @ B3.T * LORA_SCALE
            act = jax.nn.silu(h1) * h3
            out = act @ w2.T + act @ A2.T @ B2.T * LORA_SCALE
            return (acc + we[:, None] * out, None)
        init = jnp.zeros((N, D), x.dtype)
        out, _ = jax.lax.scan(expert_step, init, (a1, b1, a3, b3, a2, b2, w_full.T))
        return out.reshape(B, S, D)
    x = _layernorm(x + _L0_attn_ref(x, L0_attn_Wq, L0_attn_bq, L0_attn_Wk, L0_attn_bk, L0_attn_Wv, L0_attn_bv, L0_attn_Wo, L0_attn_bo, L0_attn_alpha), axis=-1)
    x = _layernorm(x + _L0_xattn_ref(x, ctx_2048, ctx_2048, L0_xattn_gamma), axis=-1)
    x = _layernorm(x + _L0_ffn_ref(x, L0_ffn_Wr, L0_ffn_Wg, L0_ffn_Wu, L0_ffn_Wd, L0_ffn_Wsg, L0_ffn_Wsu, L0_ffn_Wsd), axis=-1)
    x = _layernorm(x + _L1_attn_ref(x, L1_attn_W_in, L1_attn_conv_w, L1_attn_conv_b, L1_attn_dt_bias, L1_attn_A_log, L1_attn_D, L1_attn_norm_weight, L1_attn_W_out), axis=-1)
    x = _layernorm(x + _L1_xattn_ref(x, ctx_2048, mask_BxS2_bk0, L1_xattn_norm_w, L1_xattn_wq, L1_xattn_wk, L1_xattn_wv, L1_xattn_wo, L1_xattn_wg), axis=-1)
    x = _layernorm(x + _L1_ffn_ref(x, L1_ffn_gate_w, L1_ffn_w1, L1_ffn_w3, L1_ffn_w2, L1_ffn_a1, L1_ffn_b1, L1_ffn_a3, L1_ffn_b3, L1_ffn_a2, L1_ffn_b2), axis=-1)
    return x

_drawn_inputs = setup_inputs


def setup_inputs(seed=0):
    import zlib

    import numpy as np

    out = dict(_drawn_inputs(seed))
    spreads = {'L0_attn_bq': (0.0, 0.8),
     'L0_attn_bk': (0.0, 0.8),
     'L0_attn_bv': (0.0, 0.1),
     'L0_attn_bo': (0.0, 0.1),
     'L0_attn_alpha': (1.0, 0.6),
     'L1_attn_conv_b': (0.0, 0.1),
     'L1_attn_D': (1.0, 0.2),
     'L1_attn_norm_weight': (1.0, 0.2),
     'L1_xattn_norm_w': (1.0, 0.2)}
    factors = {'L0_attn_Wq': 7.085,
     'L0_attn_Wk': 6.716,
     'L0_ffn_Wr': 8.0,
     'L0_ffn_Wg': 8.0,
     'L0_ffn_Wu': 8.0,
     'L0_ffn_Wd': 8.0,
     'L1_attn_dt_bias': 8.0,
     'L1_attn_A_log': 8.0}
    for name, (base, spread) in spreads.items():
        noise = np.random.default_rng([zlib.crc32(name.encode()), seed]).standard_normal(out[name].shape)
        drawn = base * np.exp(spread * noise) if base else spread * noise
        out[name] = jnp.asarray(drawn.astype(out[name].dtype))
    for name, factor in factors.items():
        out[name] = (out[name] * factor).astype(out[name].dtype)
    return out
```

```python
from contextlib import ExitStack

import numpy as np

import concourse.bass as bass
from concourse import mybir

F32 = mybir.dt.float32
BF16 = mybir.dt.bfloat16
ALU = mybir.AluOpType
ACT = mybir.ActivationFunctionType
AX = mybir.AxisListType
ds = bass.ds

P = 128
B, T, D = 32, 64, 256
NTOK = B * T
TILES = NTOK // P
SEQS = P // T
KD = D // P
CHUNK = 512
NCHUNK = NTOK // CHUNK
TPC = CHUNK // P
EPS = 1e-5
BIG = 1e30

HEADS, HD = 16, 16
GROUPS = 4
HALF = HD // 2


class Steps:

    def __init__(self, eng, sem, per, it=0):
        self.eng, self.sem, self.per, self.it, self.n = eng, sem, per, it, 0

    def done(self, ins):
        self.n += 1
        return ins.then_inc(self.sem, 1)

    def wait(self, back=0):
        self.eng.wait_ge(self.sem, self.it * self.per + self.n - back)

    def close(self):
        assert self.n == self.per, (self.n, self.per)


class Kernel:

    def __init__(self, nc, ctx, io):
        self.nc, self.ctx, self.io, self.sems = nc, ctx, io, []
        self.resid = self.sb("resid", [P, TILES, D])
        self.residT = self.sb("residT", [P, KD, NTOK])
        self.ctxT = self.sb("ctxT_all", [P, KD, NTOK])
        self.ident = self.sb("ident", [P, P])
        self.identb = self.sb("identb", [P, P], BF16)
        self.mhalf = self.sb("mhalf", [P, 64])
        self.phalf = self.sb("phalf", [P, 32])
        self.ones = self.sb("ones", [P, P])
        self.built = ctx.enter_context(nc.semaphore("consts_built"))
        self.passed = ctx.enter_context(nc.semaphore("passed"))
        self.headmask = self.sb("headmask", [P, 4])

    def sb(self, name, shape, dt=F32, ctx=None):
        return (ctx or self.ctx).enter_context(self.nc.sbuf_tensor(name, shape, dt))

    def ps(self, name, shape, dt=F32, ctx=None):
        return (ctx or self.ctx).enter_context(self.nc.psum_tensor(name, shape, dt))

    def sem(self, name):
        self.sems.append(self.nc.alloc_semaphore(name=name))
        return self.sems[-1]

    def recycle(self):
        self.nc.all_engine_barrier()
        self.nc.clear_and_free_semaphores(self.sems)
        self.nc.all_engine_barrier()
        self.sems = []


class LayerNorm:

    def __init__(self, k, name, sb, W=2):
        self.k, self.W = k, W
        self.r = [sb(f"r{u}", [P, D]) for u in range(W)]
        self.stats = [sb(f"stats{u}", [P, 6]) for u in range(W)]
        self.mv = [sb(f"mv{u}", [P, 2]) for u in range(W)]
        self.rstd = [sb(f"rstd{u}", [P, 1]) for u in range(W)]
        self.rn = [sb(f"rn{u}", [P, D]) for u in range(W)]
        self.mv_done, self.rstd_done = k.sem(name + "_mv_done"), k.sem(name + "_rstd_done")
        self.rn_done, self.stored = k.sem(name + "_rn_done"), k.sem(name + "_resid_stored")
        self.gp_steps = k.sem(name + "_gp_steps")

    def statistics(self, dve, st, u):
        st.done(dve.bn_stats(self.stats[u][:], self.r[u][:]))

    def aggregate(self, dve, u):
        dve.bn_aggr(self.mv[u][:], self.stats[u][:]).then_inc(self.mv_done, 1)

    def variance_power(self, gp, i):
        for u in range(self.W):
            gp.wait_ge(self.mv_done, self.W * i + u + 1)
            gp.sem_inc(self.k.passed, 1)
            gp.tensor_scalar(self.rstd[u][:], self.mv[u][:, 1:2], EPS, None, ALU.add).then_inc(self.gp_steps, 1)
        for u in range(self.W):
            gp.wait_ge(self.gp_steps, self.W * i + u + 1)
            gp.tensor_tensor(self.rstd[u][:], self.rstd[u][:], self.k.mhalf[:, 0:1], ALU.pow).then_inc(self.rstd_done, 1)

    def apply(self, dve, i, u):
        if u == 0:
            dve.wait_ge(self.stored, 16 * self.W * i)
        dve.wait_ge(self.rstd_done, self.W * i + u + 1)
        dve.tensor_scalar(self.rn[u][:], self.r[u][:], self.mv[u][:, 0:1], self.rstd[u][:], ALU.subtract,
                          ALU.mult).then_inc(self.rn_done, 1)

    def store(self, sp, i):
        for u in range(self.W):
            sp.wait_ge(self.rn_done, self.W * i + u + 1)
            sp.dma_start(self.k.resid[:, ds(self.W * i + u, 1), :], self.rn[u][:].unsqueeze(1)).then_inc(self.stored, 16)

    def transpose(self, pe, i, u, tr):
        pe.wait_ge(self.rn_done, self.W * i + u + 1)
        for kd in range(KD):
            ins = pe.transpose(tr[:, kd, :], self.rn[u][:, kd * P:(kd + 1) * P], self.k.ident[:])
        return ins


def setup(k):
    with k.nc.Block() as block:
        @block.gpsimd
        def _(gp):
            gp.memset(k.ident[:], 0.0).then_inc(k.built, 1)
            gp.memset(k.identb[:], 0.0).then_inc(k.built, 1)
            gp.memset(k.mhalf[:], -0.5).then_inc(k.built, 1)
            gp.memset(k.phalf[:], 0.5).then_inc(k.built, 1)
            gp.memset(k.ones[:], 1.0).then_inc(k.built, 1)
            gp.wait_ge(k.built, 2)
            for m in (k.ident, k.identb):
                gp.affine_select(out=m[:], in_=m[:], compare_op=ALU.not_equal, fill=1.0, base=0,
                                 pattern=[[-1, P]], channel_multiplier=1).then_inc(k.built, 1)


def layer0_attention(k):
    nc, io, sem = k.nc, k.io, k.sem
    with ExitStack() as ctx:
        def sb(name, shape, dt=F32):
            return k.sb("a_" + name, shape, dt, ctx)

        def pair(name, shape, dt=F32):
            return [sb(f"{name}{u}", shape, dt) for u in range(2)]

        NQK, NV, H20 = (HEADS + GROUPS) * HD, GROUPS * HD, HEADS + GROUPS
        wqkv, wo = sb("wqkv", [P, KD, NQK + NV]), sb("wo", [P, KD, D])
        biasrow, borow = sb("biasrow", [1, NQK + 2 * NV]), sb("borow", [1, D])
        factor, cos, sin = sb("factor", [P, H20]), sb("cos", [P, HD]), sb("sin", [P, HD])
        causal = sb("causal", [P, T])
        x, twice = pair("x", [P, KD, P]), pair("twice", [P, KD, 2, 2, T])
        qk, sq = pair("qk", [P, H20, HD]), pair("sq", [P, H20, HD])
        ss, nrm, sc = pair("ss", [P, H20]), pair("nrm", [P, H20]), pair("sc", [P, H20])
        turned, rot = pair("turned", [P, H20, HD]), pair("rot", [P, H20, HD])
        krep, qkT, kbd = pair("krep", [P, GROUPS, 4, HD]), pair("qkT", [P, 4, P]), pair("kbd", [P, 4, 4, T])
        sm, mx, pr = pair("sm", [P, 16, T]), pair("mx", [P, 16]), pair("pr", [P, 8, P])
        pt, vbd = pair("pt", [P, 8, P]), pair("vbd", [P, 2, GROUPS, 2, HD + 1])
        rc, yn, yT = pair("rc", [P, 16]), pair("yn", [P, 16, HD]), pair("yT", [P, KD, P])
        ln = LayerNorm(k, "a", sb)
        qkv_ps, tr = k.ps("a_qkv", [P, 512], F32, ctx), k.ps("a_tr", [P, 4, P], F32, ctx)
        s_ps, pt_ps = k.ps("a_s", [P, 2, 512], F32, ctx), k.ps("a_pt", [P, 8, P], F32, ctx)
        y_ps, o_ps = k.ps("a_y", [P, 512], F32, ctx), k.ps("a_o", [P, 512], F32, ctx)

        const, resid_in, x_in = sem("a_const_in"), sem("a_resid_in"), [sem(f"a_x{u}_in") for u in range(2)]
        qkv_full, qk_out, v_out = sem("a_qkv_full"), sem("a_qk_out"), sem("a_v_out")
        summed, normed, rotated, repeated = sem("a_summed"), sem("a_normed"), sem("a_rotated"), sem("a_repeated")
        tr_full, tr_out, kbd_done = sem("a_tr_full"), sem("a_tr_out"), sem("a_kbd_done")
        s_full, s_out, shifted, exped = sem("a_s_full"), sem("a_s_out"), sem("a_shifted"), sem("a_exped")
        pt_full, pt_out, y_full, y_out = sem("a_pt_full"), sem("a_pt_out"), sem("a_y_full"), sem("a_y_out")
        o_full, o_out = sem("a_o_full"), sem("a_o_out")
        steps, vbd_set = sem("a_vector_steps"), sem("a_vbd_set")
        ITERS, TR_USES = TILES // 2, 3 * 2
        consts = ((wqkv, "a_wqkv"), (biasrow, "a_bias"), (factor, "a_factor"), (cos, "cos"), (sin, "sin"),
                  (causal, "causal"), (wo, "a_wo"), (borow, "a_bo"), (k.headmask, "headmask"))

        with nc.Block() as block:
            @block.sync
            def _(sp):
                for dst, src in consts:
                    sp.dma_start(dst[:], io[src]).then_inc(const, 16)
                sp.dma_start(k.resid[:], io["x"]).then_inc(resid_in, 16)
                with sp.Fori(0, ITERS) as i:
                    sp.wait_ge(qkv_full, 2 * i)
                    for u in range(2):
                        sp.dma_start(x[u][:], io["xT"][:, :, ds((2 * i + u) * P, P)]).then_inc(x_in[u], 16)
                        for b in range(2):
                            for copy in range(2):
                                sp.dma_start(twice[u][:, :, b, copy, :],
                                             io["xT"][:, :, ds((2 * i + u) * P + b * T, T)]).then_inc(x_in[u], 16)
                    ln.store(sp, i)
                sp.wait_ge(ln.stored, 16 * TILES)

            @block.gpsimd
            def _(gp):
                for u in range(2):
                    gp.memset(vbd[u][:], 0.0).then_inc(vbd_set, 1)
                gp.wait_ge(vbd_set, 2)
                for u in range(2):
                    for h2 in range(2):
                        gp.memset(vbd[u][h2 * T:(h2 + 1) * T, :, :, h2, HD:], 1.0).then_inc(vbd_set, 1)
                with gp.Fori(0, ITERS) as i:
                    for u in range(2):
                        gp.wait_ge(summed, 2 * i + u + 1)
                        gp.tensor_tensor(nrm[u][:], ss[u][:], k.phalf[:, 0:H20], ALU.pow).then_inc(normed, 1)
                    ln.variance_power(gp, i)

            @block.scalar
            def _(act):
                act.wait_ge(vbd_set, 6)
                with act.Fori(0, ITERS) as i:
                    for u in range(2):
                        act.wait_ge(qkv_full, 2 * i + u + 1)
                        flat = qkv_ps[:, 0:NQK].rearrange("p (h d) -> p h d", d=HD)
                        act.activation(qk[u][:], flat, ACT.Copy)
                        act.activation(sq[u][:], flat, ACT.Square).then_inc(qk_out, 1)
                        v4 = qkv_ps[:, NQK:NQK + 2 * NV].rearrange("p (b g d) -> p b g d", b=2, g=GROUPS)
                        for h2 in range(2):
                            rows = slice(h2 * T, (h2 + 1) * T)
                            act.activation(vbd[u][rows, :, :, h2, 0:HD], v4[rows], ACT.Copy).then_inc(v_out, 1)
                    for u in range(2):
                        act.wait_ge(rotated, 2 * i + u + 1)
                        act.activation(krep[u][:], rot[u][:, HEADS:H20, :].unsqueeze(2)
                                       .broadcast_to([P, GROUPS, 4, HD]), ACT.Copy).then_inc(repeated, 1)
                    for u in range(2):
                        act.wait_ge(tr_full, TR_USES * i + u + 1)
                        act.activation(qkT[u][:], tr[:], ACT.Copy).then_inc(tr_out, 1)
                    for u in range(2):
                        act.wait_ge(shifted, 2 * i + u + 1)
                        act.activation(pr[u][:].rearrange("p a b -> p (a b)"),
                                       sm[u][:].rearrange("p a b -> p (a b)"), ACT.Exp).then_inc(exped, 1)
                    for u in range(2):
                        act.wait_ge(pt_full, 2 * i + u + 1)
                        act.activation(pt[u][:], pt_ps[:], ACT.Copy).then_inc(pt_out, 1)
                    for u in range(2):
                        act.wait_ge(tr_full, TR_USES * i + 2 + u + 1)
                        act.activation(yT[u][:], tr[:, 0:KD, :], ACT.Copy).then_inc(tr_out, 1)
                    for u in range(2):
                        act.wait_ge(tr_full, TR_USES * i + 4 + u + 1)
                        act.activation(k.residT[:, :, ds((2 * i + u) * P, P)], tr[:, 0:KD, :],
                                       ACT.Copy).then_inc(tr_out, 1)

            @block.vector
            def _(dve):
                dve.wait_ge(const, 16 * len(consts))
                dve.wait_ge(resid_in, 16)
                with dve.Fori(0, ITERS) as i:
                    st = Steps(dve, steps, 16, i)
                    for u in range(2):
                        dve.wait_ge(qk_out, 2 * i + u + 1)
                        dve.tensor_reduce(ss[u][:], sq[u][:], AX.X, ALU.add).then_inc(summed, 1)
                    for u in range(2):
                        dve.wait_ge(normed, 2 * i + u + 1)
                        st.done(dve.tensor_scalar(nrm[u][:], nrm[u][:], 1e-6, None, ALU.add))
                    for u in range(2):
                        st.wait(1)
                        st.done(dve.reciprocal(sc[u][:], nrm[u][:]))
                    for u in range(2):
                        st.wait(1)
                        st.done(dve.tensor_tensor(sc[u][:], sc[u][:], factor[:], ALU.mult))
                    for u in range(2):
                        st.wait(1)
                        st.done(dve.tensor_tensor(qk[u][:], qk[u][:], sc[u][:].unsqueeze(2)
                                                  .broadcast_to([P, H20, HD]), ALU.mult))
                    for u in range(2):
                        st.wait(1)
                        half = [slice(0, HALF), slice(HALF, HD)]
                        for a in range(2):
                            dve.tensor_tensor(turned[u][:, :, half[a]], qk[u][:, :, half[1 - a]],
                                              sin[:, half[a]].unsqueeze(1).broadcast_to([P, H20, HALF]), ALU.mult)
                        st.done(dve.tensor_tensor(rot[u][:], qk[u][:], cos[:].unsqueeze(1)
                                                  .broadcast_to([P, H20, HD]), ALU.mult))
                    for u in range(2):
                        st.wait(1 - u)
                        dve.tensor_tensor(rot[u][:], rot[u][:], turned[u][:], ALU.add).then_inc(rotated, 1)
                    for u in range(2):
                        dve.wait_ge(tr_out, TR_USES * i + u + 1)
                        kT = qkT[u][:, 2:4, :].rearrange("p h (b s) -> p (h b) s", b=2)
                        dve.tensor_tensor(kbd[u][:], kT.unsqueeze(2).broadcast_to([P, 4, 4, T]),
                                          k.headmask[:].unsqueeze(1).unsqueeze(3).broadcast_to([P, 4, 4, T]),
                                          ALU.mult).then_inc(kbd_done, 1)
                    for u in range(2):
                        dve.wait_ge(s_full, 2 * i + u + 1)
                        dve.tensor_tensor(sm[u][:], s_ps[:].rearrange("p r (h s) -> p (r h) s", s=T),
                                          causal[:].unsqueeze(1).broadcast_to([P, 16, T]), ALU.add).then_inc(s_out, 1)
                    for u in range(2):
                        dve.wait_ge(s_out, 2 * i + u + 1)
                        st.done(dve.tensor_reduce(mx[u][:], sm[u][:], AX.X, ALU.max))
                    for u in range(2):
                        st.wait(1 - u)
                        dve.tensor_tensor(sm[u][:], sm[u][:], mx[u][:].unsqueeze(2).broadcast_to([P, 16, T]),
                                          ALU.subtract).then_inc(shifted, 1)
                    for u in range(2):
                        dve.wait_ge(y_full, 2 * i + u + 1)
                        y = y_ps[:, 0:16 * (HD + 1)].rearrange("p (h d) -> p h d", d=HD + 1)
                        st.done(dve.reciprocal(rc[u][:], y[:, :, HD]))
                        st.wait()
                        dve.tensor_tensor(yn[u][:], y[:, :, 0:HD], rc[u][:].unsqueeze(2).broadcast_to([P, 16, HD]),
                                          ALU.mult).then_inc(y_out, 1)
                    for u in range(2):
                        dve.wait_ge(o_full, 2 * i + u + 1)
                        dve.tensor_tensor(ln.r[u][:].unsqueeze(1), o_ps[:, 0:D].unsqueeze(1),
                                          k.resid[:, ds(2 * i + u, 1), :], ALU.add).then_inc(o_out, 1)
                    for u in range(2):
                        dve.wait_ge(o_out, 2 * i + u + 1)
                        ln.statistics(dve, st, u)
                    for u in range(2):
                        st.wait(1 - u)
                        dve.sem_inc(k.passed, 1)
                        ln.aggregate(dve, u)
                    for u in range(2):
                        ln.apply(dve, i, u)
                    st.close()

            @block.tensor
            def _(pe):
                pe.wait_ge(const, 16 * len(consts))
                with pe.Fori(0, ITERS) as i:
                    for u in range(2):
                        pe.wait_ge(x_in[u], 80 * (i + 1))
                        pe.wait_ge(v_out, 2 * (2 * i + u))
                        for kd in range(KD):
                            pe.matmul(qkv_ps[:, 0:NQK], x[u][:, kd, :], wqkv[:, kd, 0:NQK], start=(kd == 0), stop=False)
                        pe.matmul(qkv_ps[:, 0:NQK], k.ones[0:1, :], biasrow[0:1, 0:NQK], start=False, stop=True)
                        for b in range(2):
                            v = qkv_ps[:, NQK + b * NV:NQK + (b + 1) * NV]
                            for kd in range(KD):
                                pe.matmul(v, twice[u][:, kd, b, :, :].rearrange("p c t -> p (c t)"), wqkv[:, kd, NQK:NQK + NV], start=(kd == 0), stop=False)
                            ins = pe.matmul(v, k.ones[0:1, :], biasrow[0:1, NQK:NQK + NV], start=False, stop=True)
                        ins.then_inc(qkv_full, 1)
                    for u in range(2):
                        pe.wait_ge(rotated, 2 * i + u + 1)
                        pe.wait_ge(repeated, 2 * i + u + 1)
                        pe.wait_ge(tr_out, TR_USES * i + u)
                        q = rot[u][:, 0:HEADS, :].rearrange("p h d -> p (h d)")
                        kr = krep[u][:].rearrange("p g j d -> p (g j d)")
                        for c in range(2):
                            pe.transpose(tr[:, c, :], q[:, c * P:(c + 1) * P], k.ident[:])
                        for c in range(2):
                            ins = pe.transpose(tr[:, 2 + c, :], kr[:, c * P:(c + 1) * P], k.ident[:])
                        ins.then_inc(tr_full, 1)
                    for u in range(2):
                        pe.wait_ge(tr_out, TR_USES * i + u + 1)
                        pe.wait_ge(kbd_done, 2 * i + u + 1)
                        pe.wait_ge(s_out, 2 * i + u)
                        pe.sem_inc(k.passed, 1)
                        for r in range(2):
                            rows = slice(r * 64, r * 64 + 64)
                            for hh in range(2):
                                for b in range(2):
                                    ins = pe.matmul(s_ps[b * T:(b + 1) * T, r, hh * 256:(hh + 1) * 256],
                                                    qkT[u][rows, hh, b * T:(b + 1) * T],
                                                    kbd[u][rows, hh * 2 + b, :, :].rearrange("p h s -> p (h s)"),
                                                    start=True, stop=True)
                        ins.then_inc(s_full, 1)
                    for u in range(2):
                        pe.wait_ge(exped, 2 * i + u + 1)
                        pe.wait_ge(pt_out, 2 * i + u)
                        for c in range(8):
                            ins = pe.transpose(pt_ps[:, c, :], pr[u][:, c, :], k.ident[:])
                        ins.then_inc(pt_full, 1)
                    for u in range(2):
                        pe.wait_ge(pt_out, 2 * i + u + 1)
                        pe.wait_ge(v_out, 4 * i + 2 * u + 2)
                        pe.wait_ge(y_out, 2 * i + u)
                        for c in range(8):
                            g = (c // 2 % 2) * 2 + c // 4
                            for b in range(2):
                                ins = pe.matmul(y_ps[b * T:(b + 1) * T, c * 34:(c + 1) * 34],
                                                pt[u][:, c, b * T:(b + 1) * T],
                                                vbd[u][:, b, g, :, :].rearrange("p h d -> p (h d)"),
                                                start=True, stop=True)
                        ins.then_inc(y_full, 1)
                    for u in range(2):
                        pe.wait_ge(y_out, 2 * i + u + 1)
                        pe.wait_ge(tr_out, TR_USES * i + 2 + u)
                        y = yn[u][:].rearrange("p h d -> p (h d)")
                        for c in range(KD):
                            ins = pe.transpose(tr[:, c, :], y[:, c * P:(c + 1) * P], k.ident[:])
                        ins.then_inc(tr_full, 1)
                    for u in range(2):
                        pe.wait_ge(tr_out, TR_USES * i + 2 + u + 1)
                        pe.wait_ge(o_out, 2 * i + u)
                        pe.matmul(o_ps[:, 0:D], k.ones[0:1, :], borow[:], start=True, stop=False)
                        for c in range(KD):
                            ins = pe.matmul(o_ps[:, 0:D], yT[u][:, c, :], wo[:, c, :], start=False, stop=(c == KD - 1))
                        ins.then_inc(o_full, 1)
                    for u in range(2):
                        pe.wait_ge(tr_out, TR_USES * i + 4 + u)
                        ln.transpose(pe, i, u, tr).then_inc(tr_full, 1)


def context_parts(k):
    nc, io, sem = k.nc, k.io, k.sem
    k.kparts = nc.dram_tensor("kparts", (TILES, 3, 3, 8, P // 8, D), BF16, kind="Internal").ap()
    with ExitStack() as ctx:
        c = k.sb("cp_c", [P, TILES, D], F32, ctx)
        part = [k.sb(f"cp_part{j}", [P, TILES, D], BF16, ctx) for j in range(3)]
        loaded, split, written, steps = sem("cp_loaded"), sem("cp_split"), sem("cp_written"), sem("cp_steps")
        with nc.Block() as block:
            @block.sync
            def _(sp):
                sp.dma_start(c[:], io["ctx_dg"]).then_inc(loaded, 16)
                for j in range(3):
                    sp.wait_ge(split, j + 1)
                    for i in range(3):
                        sp.dma_start(k.kparts[:, j, i].rearrange("t d g f -> (d g) t f"), part[j][:]).then_inc(written, 16)
                sp.wait_ge(written, 16 * 9)

            @block.vector
            def _(dve):
                st = Steps(dve, steps, 0)
                dve.wait_ge(loaded, 16)
                for j in range(3):
                    if j:
                        st.wait()
                    dve.tensor_copy(part[j][:], c[:]).then_inc(split, 1)
                    if j < 2:
                        dve.wait_ge(split, j + 1)
                        st.done(dve.tensor_tensor(c[:], c[:], part[j][:], ALU.subtract))


class Tile:

    def __init__(self, i, c):
        self.i, self.c, self.v = i, c, c % 3
        self.t = c if i is None else 3 * i + c
        self.n = c // 3 + 1 if i is None else i + (c // 3 + 1)
        self.live = i is not None or 0 <= c < TILES

    def plus(self, d):
        return Tile(self.i, self.c + d)


def slots(eng, slot, end=TILES + 2):
    for c in range(4):
        slot(Tile(None, c))
    with eng.Fori(0, (TILES - 4) // 3) as i:
        for w in range(3):
            slot(Tile(i, 4 + w))
    for c in range(TILES, end):
        slot(Tile(None, c))


def wait(eng, sem, value):
    if not isinstance(value, int) or value > 0:
        eng.wait_ge(sem, value)


def layer0_cross_attention(k):
    nc, io, sem = k.nc, k.io, k.sem
    G, DT, L = P // 8, 8, D
    ROWS = 9 * DT
    SCALE = float(DT) ** -0.5
    qparts = nc.dram_tensor("qparts", (TILES, 3, DT, G, L), BF16, kind="Internal").ap()
    with ExitStack() as ctx:
        def sb(name, shape, dt=F32):
            return k.sb("b_" + name, shape, dt, ctx)

        def three(name, shape, dt=F32):
            return [sb(f"{name}{v}", shape, dt) for v in range(3)]

        gamma = sb("gamma", [P, 1])
        xp, rest = three("xp", [P, 3, L], BF16), sb("rest", [P, L])
        qs, ks = three("qs", [P, G, L], BF16), three("ks", [P, G, L], BF16)
        vt = three("vt", [P, KD, G, 32])
        nm, nrest, mp = three("nm", [P, 2 * G]), three("nrest", [P, 2 * G]), three("mp", [P, 3, 2 * G], BF16)
        mt = three("mt", [96, P], BF16)
        pr = [sb(f"pr{n}", [P, KD, L]) for n in range(8)]
        os_ = three("os", [P, 4, L])
        nd = three("nd", [P, 4, L])
        rec, r, rn = three("rec", [P, L]), three("r", [P, L]), three("rn", [P, L])
        stats, mv, rstd = three("stats", [P, 6]), three("mv", [P, 2]), three("rstd", [P, 1])
        s1 = [k.ps(f"b_s1{n}", [P, 2, 2, L], F32, ctx) for n in range(2)]
        s2 = [k.ps(f"b_s2{n}", [P, KD, L], F32, ctx) for n in range(2)]
        o_ps, tr = k.ps("b_o", [P, 2, L], F32, ctx), k.ps("b_tr", [P, 4, P], F32, ctx)
        trb = tr[:, 0, :].bitcast(BF16)[:, 0:P]

        const, preset, gp_steps = sem("b_const_in"), sem("b_preset"), sem("b_gp_steps")
        split, vt_done = sem("b_split"), sem("b_vt_done")
        written = [sem(f"b_q_written{v}") for v in range(3)]
        placed = [sem(f"b_qk_placed{v}") for v in range(3)]
        s1_full, s1_out, m_split, steps = sem("b_s1_full"), sem("b_s1_out"), sem("b_m_split"), sem("b_steps")
        mp_turned, mt_out = sem("b_mp_turned"), sem("b_mt_out")
        rn_turned, rT_out, eps_done, m_steps = sem("b_rn_turned"), sem("b_rT_out"), sem("b_eps_done"), sem("b_m_steps")
        m_placed = [sem(f"b_m_placed{v}") for v in range(3)]
        s2_full, s2_out, pv_done, o_out = sem("b_s2_full"), sem("b_s2_out"), sem("b_pv_done"), sem("b_o_out")
        nd_in = [sem(f"b_nd_in{v}") for v in range(3)]
        mv_done, rstd_done, rn_done = sem("b_mv_done"), sem("b_rstd_done"), sem("b_rn_done")
        stored = [sem(f"b_stored{v}") for v in range(3)]
        LAG = 3

        with nc.Block() as block:
            @block.sync
            def _(sp):
                sp.dma_start(gamma[:], io["b_gamma"]).then_inc(const, 16)
                sp.dma_start(k.ctxT[:], io["ctxT"]).then_inc(const, 16)
                sp.wait_ge(preset, 6)

                def load(x):
                    wait(sp, pv_done, 4 * (x.t - 2))
                    sp.dma_start(ks[x.v][0:ROWS, :, :].rearrange("r g f -> r (g f)"),
                                 k.kparts[ds(x.t, 1)].rearrange("t j i d g f -> (t j i d) (g f)")).then_inc(placed[x.v], 16)
                    sp.wait_ge(split, x.t + 1)
                    for i in range(3):
                        sp.dma_start(qparts[ds(x.t, 1), i].rearrange("t d g f -> (t g) d f"), xp[x.v][:, i, :]
                                     ).then_inc(written[x.v], 16)
                    sp.wait_ge(written[x.v], 48 * x.n)
                    sp.dma_start(qs[x.v][0:ROWS, :, :].rearrange("r g f -> r (g f)"),
                                 qparts[ds(x.t, 1)].rearrange("t i d g f -> (t i d) (g f)").partition_broadcast(3)
                                 ).then_inc(placed[x.v], 16)

                def numerators(x, q):
                    if q % 2 == 0:
                        sp.wait_ge(o_out, 2 * x.t + q // 2 + 1)
                    if q == 0:
                        wait(sp, mv_done, x.t - 2)
                    sp.dma_start(nd[x.v][32 * q:32 * q + 32, :, :], os_[x.v][:, q, :]).then_inc(nd_in[x.v], 16)

                def slot(s):
                    if s.live:
                        load(s)
                    x, m = s.plus(-2), s.plus(-1)
                    if x.live:
                        numerators(x, 0)
                        numerators(x, 1)
                    if m.live:
                        sp.wait_ge(mt_out, m.t + 1)
                        for part in range(3):
                            sp.dma_start(qs[m.v][ROWS + part:ROWS + part + 1, :, :].rearrange("r g (h f) -> r (g h) f", h=2),
                                         mt[m.v][32 * part:32 * part + 32, :]).then_inc(m_placed[m.v], 16)
                    if x.live:
                        numerators(x, 2)
                        numerators(x, 3)
                    x = s.plus(-3)
                    if x.live:
                        sp.wait_ge(rn_done, x.t + 1)
                        sp.dma_start(k.resid[:, ds(x.t, 1), :], rn[x.v][:].unsqueeze(1)).then_inc(stored[x.v], 16)

                slots(sp, slot, TILES + 3)
                for v in range(3):
                    sp.wait_ge(stored[v], 16 * len(range(v, TILES, 3)))

            @block.gpsimd
            def _(gp):
                gp.wait_ge(preset, 6)
                gp.wait_ge(const, 32)

                def slot(s):
                    x = s
                    if x.live:
                        xs = k.resid[:, ds(x.t, 1), :].rearrange("p t f -> p (t f)")
                        gp.wait_ge(written[x.v], 48 * (x.n - 1))
                        st = Steps(gp, gp_steps, 4, x.t)
                        gp.sem_inc(k.passed, 1)
                        st.done(gp.tensor_copy(xp[x.v][:, 0, :], xs))
                        st.wait()
                        gp.sem_inc(k.passed, 1)
                        st.done(gp.tensor_tensor(rest[:], xs, xp[x.v][:, 0, :], ALU.subtract))
                        st.wait()
                        gp.sem_inc(k.passed, 1)
                        st.done(gp.tensor_copy(xp[x.v][:, 1, :], rest[:]))
                        st.wait()
                        st.done(gp.tensor_tensor(rest[:], rest[:], xp[x.v][:, 1, :], ALU.subtract))
                        st.wait()
                        gp.sem_inc(k.passed, 1)
                        gp.tensor_copy(xp[x.v][:, 2, :], rest[:]).then_inc(split, 1)
                        wait(gp, pv_done, 4 * (x.t - 2))
                        gp.sem_inc(k.passed, 1)
                        for lh in range(KD):
                            gp.tensor_copy(vt[x.v][:, lh, :, 0:32:4],
                                           k.ctxT[:, lh, ds(x.t * P, P)].rearrange("p (g d) -> p g d", d=DT)
                                           ).then_inc(vt_done, 1)
                        st.close()
                    x = s.plus(-2)
                    if x.live:
                        gp.wait_ge(mv_done, x.t + 1)
                        gp.sem_inc(k.passed, 1)
                        gp.tensor_scalar(rstd[x.v][:], mv[x.v][:, 1:2], EPS, None, ALU.add).then_inc(eps_done, 1)
                        gp.wait_ge(eps_done, x.t + 1)
                        gp.tensor_tensor(rstd[x.v][:], rstd[x.v][:], k.mhalf[:, 0:1], ALU.pow).then_inc(rstd_done, 1)

                slots(gp, slot)

            @block.vector
            def _(dve):
                for v in range(3):
                    dve.memset(ks[v][64:96, :, :], 1.0).then_inc(preset, 1)
                    dve.memset(vt[v][:], 1.0).then_inc(preset, 1)
                dve.wait_ge(const, 32)

                def finish(x):
                    st = Steps(dve, steps, 4, x.t)
                    dve.wait_ge(nd_in[x.v], 64 * x.n)
                    st.done(dve.reciprocal(rec[x.v][:], nd[x.v][:, 1, :]))
                    st.wait()
                    st.done(dve.tensor_tensor(rec[x.v][:], rec[x.v][:], nd[x.v][:, 0, :], ALU.mult))
                    st.wait()
                    st.done(dve.scalar_tensor_tensor(out=r[x.v][:], in0=rec[x.v][:], scalar=gamma[:],
                                                     in1=k.resid[:, ds(x.t, 1), :].rearrange("p t f -> p (t f)"),
                                                     op0=ALU.mult, op1=ALU.add))
                    st.wait()
                    st.done(dve.bn_stats(stats[x.v][:], r[x.v][:]))
                    st.wait()
                    dve.sem_inc(k.passed, 1)
                    dve.bn_aggr(mv[x.v][:], stats[x.v][:]).then_inc(mv_done, 1)

                def slot(s):
                    if s.live:
                        for gp in range(8):
                            dve.wait_ge(s1_full, 8 * s.t + gp + 1)
                            dve.tensor_reduce(nm[s.v][:, 4 * gp:4 * gp + 4].rearrange("p (g h) -> p g h", h=2),
                                              s1[gp % 2][:], AX.X, ALU.max, negate=True).then_inc(s1_out, 1)
                        st = Steps(dve, m_steps, 4, s.t)
                        dve.wait_ge(s1_out, 8 * s.t + 8)
                        st.done(dve.tensor_copy(mp[s.v][:, 0, :], nm[s.v][:]))
                        st.wait()
                        st.done(dve.tensor_tensor(nrest[s.v][:], nm[s.v][:], mp[s.v][:, 0, :], ALU.subtract))
                        st.wait()
                        st.done(dve.tensor_copy(mp[s.v][:, 1, :], nrest[s.v][:]))
                        st.wait()
                        st.done(dve.tensor_tensor(nrest[s.v][:], nrest[s.v][:], mp[s.v][:, 1, :], ALU.subtract))
                        st.wait()
                        dve.tensor_copy(mp[s.v][:, 2, :], nrest[s.v][:]).then_inc(m_split, 1)
                        st.close()
                    x = s.plus(-2)
                    if x.live:
                        finish(x)
                        dve.wait_ge(rstd_done, x.t + 1)
                        dve.wait_ge(stored[x.v], 16 * (x.n - 1))
                        wait(dve, rn_turned, x.t - 2)
                        dve.tensor_scalar(rn[x.v][:], r[x.v][:], mv[x.v][:, 0:1], rstd[x.v][:], ALU.subtract,
                                          ALU.mult).then_inc(rn_done, 1)

                slots(dve, slot)

            @block.scalar
            def _(act):
                act.sem_inc(s2_out, 2)

                def slot(s):
                    x = s.plus(-1)
                    for g in range(G):
                        if x.live:
                            act.wait_ge(s2_full, G * x.t + g + 1)
                            if g % 4 == 0:
                                wait(act, pv_done, 4 * x.t + g // 4 - 1)
                            act.activation(pr[g % 8][:], s2[g % 2][:], ACT.Exp, scale=SCALE).then_inc(s2_out, 1)
                        if x.live and g in (9, 15):
                            if g == 9:
                                act.wait_ge(pv_done, 4 * x.t + 2)
                            else:
                                act.wait_ge(pv_done, 4 * x.t + 4)
                            act.wait_ge(nd_in[x.v], 64 * (x.n - 1))
                            act.activation(os_[x.v][:, 2 * (g // 15):2 * (g // 15) + 2, :], o_ps[:], ACT.Copy).then_inc(o_out, 1)
                        if g == 13 and s.live:
                            act.wait_ge(mp_turned, s.t + 1)
                            act.wait_ge(m_placed[s.v], 48 * (s.n - 1))
                            act.activation(mt[s.v][:], trb[0:96, :], ACT.Copy).then_inc(mt_out, 1)
                    x = s.plus(-2)
                    if x.live:
                        act.wait_ge(rn_turned, x.t + 1)
                        act.activation(k.residT[:, :, ds(x.t * P, P)], tr[:, 0:KD, :], ACT.Copy).then_inc(rT_out, 1)

                slots(act, slot)

            @block.tensor
            def _(pe):
                def first_pass(x, gp):
                    wait(pe, s1_out, 8 * x.t + gp - 1)
                    for g in (2 * gp, 2 * gp + 1):
                        for qh in range(2):
                            ins = pe.matmul(s1[gp % 2][:, g % 2, qh, :], qs[x.v][0:ROWS, g, qh * P:(qh + 1) * P],
                                            ks[x.v][0:ROWS, g, :], start=True, stop=True)
                    ins.then_inc(s1_full, 1)

                def second_pass(x, gp):
                    for g in (2 * gp, 2 * gp + 1):
                        pe.wait_ge(s2_out, G * x.t + g + 1)
                        for lh in range(KD):
                            ins = pe.matmul(s2[g % 2][:, lh, :], ks[x.v][0:ROWS + 3, g, lh * P:(lh + 1) * P],
                                            qs[x.v][0:ROWS + 3, g, :], start=True, stop=True)
                        ins.then_inc(s2_full, 1)

                def values(x, q):
                    pe.wait_ge(s2_out, G * x.t + 4 * q + 4 + 2)
                    if q % 2 == 0:
                        wait(pe, o_out, 2 * x.t + q // 2)
                    for lh in range(KD):
                        for j in range(4):
                            g = 4 * q + j
                            ins = pe.matmul(o_ps[32 * j:32 * j + 32, q % 2, :], vt[x.v][:, lh, g, :], pr[g % 8][:, lh, :],
                                            start=(lh == 0), stop=(lh == KD - 1))
                    ins.then_inc(pv_done, 1)

                def slot(s):
                    x = s.plus(-1)
                    if s.live:
                        pe.wait_ge(placed[s.v], 32 * s.n)
                    for n in range(8 + LAG):
                        if s.live and n < 8:
                            first_pass(s, n)
                        gp = n - LAG
                        if gp < 0:
                            continue
                        if x.live:
                            if gp == 0:
                                pe.wait_ge(m_placed[x.v], 48 * x.n)
                                pe.wait_ge(vt_done, 2 * x.t + 2)
                            second_pass(x, gp)
                            if gp in (2, 4, 6):
                                values(x, gp // 2 - 1)
                        if gp == 6 and s.live:
                            pe.wait_ge(m_split, s.t + 1)
                            wait(pe, rT_out, s.t - 2)
                            pe.transpose(trb[0:96, :], mp[s.v][:].rearrange("p a n -> p (a n)"), k.identb[:]).then_inc(mp_turned, 1)
                    if x.live:
                        values(x, 3)
                    x = s.plus(-2)
                    if x.live:
                        pe.wait_ge(rn_done, x.t + 1)
                        wait(pe, rT_out, x.t)
                        if s.live:
                            pe.wait_ge(mt_out, s.t + 1)
                        for kd in range(KD):
                            ins = pe.transpose(tr[:, kd, :], rn[x.v][:, kd * P:(kd + 1) * P], k.ident[:])
                        ins.then_inc(rn_turned, 1)

                slots(pe, slot)


class ChunkNorm:

    def __init__(self, k, name, sb):
        self.k = k
        self.r = [sb(f"r{u}", [P, TPC, D]) for u in range(2)]
        self.stats = [sb(f"stats{u}", [P, TPC, 6]) for u in range(2)]
        self.mv = [sb(f"mv{u}", [P, TPC, 2]) for u in range(2)]
        self.rstd = [sb(f"rstd{u}", [P, TPC]) for u in range(2)]
        self.rn = [sb(f"rn{u}", [P, TPC, D]) for u in range(2)]
        self.r_done, self.mv_done, self.rstd_done = k.sem(name + "_r_done"), k.sem(name + "_mv_done"), k.sem(name + "_rstd_done")
        self.rn_done, self.stored = k.sem(name + "_rn_done"), k.sem(name + "_resid_stored")
        self.stats_done, self.eps_done = k.sem(name + "_stats_done"), k.sem(name + "_eps_done")

    def statistics(self, dve, c, u):
        dve.wait_ge(self.r_done, c + 1)
        for t in range(TPC):
            ins = dve.bn_stats(self.stats[u][:, t, :], self.r[u][:, t, :])
        ins.then_inc(self.stats_done, 1)
        dve.wait_ge(self.stats_done, c + 1)
        dve.sem_inc(self.k.passed, 1)
        for t in range(TPC):
            ins = dve.bn_aggr(self.mv[u][:, t, :], self.stats[u][:, t, :])
        ins.then_inc(self.mv_done, 1)

    def variance_power(self, gp, c, u):
        gp.wait_ge(self.mv_done, c + 1)
        gp.sem_inc(self.k.passed, 1)
        gp.tensor_scalar(self.rstd[u][:], self.mv[u][:, :, 1], EPS, None, ALU.add).then_inc(self.eps_done, 1)
        gp.wait_ge(self.eps_done, c + 1)
        gp.tensor_tensor(self.rstd[u][:], self.rstd[u][:], self.k.mhalf[:, 0:TPC], ALU.pow).then_inc(self.rstd_done, 1)

    def apply(self, dve, c, u, i):
        dve.wait_ge(self.rstd_done, c + 1)
        dve.wait_ge(self.stored, 32 * i)
        for t in range(TPC):
            ins = dve.tensor_scalar(self.rn[u][:, t, :], self.r[u][:, t, :], self.mv[u][:, t, 0:1],
                                    self.rstd[u][:, t:t + 1], ALU.subtract, ALU.mult)
        ins.then_inc(self.rn_done, 1)

    def store(self, sp, c, u):
        sp.wait_ge(self.rn_done, c + 1)
        sp.dma_start(self.k.resid[:, ds(TPC * c, TPC), :], self.rn[u][:]).then_inc(self.stored, 16)

    def transpose(self, pe, c, u, tr):
        pe.wait_ge(self.rn_done, c + 1)
        for t in range(TPC):
            for kd in range(KD):
                ins = pe.transpose(tr[:, t, kd, :], self.rn[u][:, t, kd * P:(kd + 1) * P], self.k.ident[:])
        return ins

    def copy_turned(self, act, c, tr):
        for t in range(TPC):
            ins = act.activation(self.k.residT[:, :, ds(CHUNK * c + t * P, P)], tr[:, t, :, :], ACT.Copy)
        return ins


def choose_two(dve, st, logits, best, cand, top, masks, maxima, descending):
    E = logits.shape[-1]
    full = [P, TILES, E]
    for n in range(2):
        st.wait()
        st.done(dve.tensor_reduce(maxima[n][:], (logits if n == 0 else best)[:], AX.X, ALU.max))
        st.wait()
        st.done(dve.tensor_tensor(cand[:], (logits if n == 0 else best)[:],
                                  maxima[n][:].unsqueeze(2).broadcast_to(full), ALU.is_equal))
        st.wait()
        st.done(dve.tensor_tensor(cand[:], cand[:], descending[:].unsqueeze(1).broadcast_to(full), ALU.mult))
        st.wait()
        st.done(dve.tensor_reduce(top[:], cand[:], AX.X, ALU.max))
        st.wait()
        st.done(dve.tensor_tensor(masks[n][:], cand[:], top[:].unsqueeze(2).broadcast_to(full), ALU.is_equal))
        if n == 0:
            st.wait()
            st.done(dve.scalar_tensor_tensor(out=best[:], in0=masks[0][:], scalar=-BIG, in1=logits[:],
                                             op0=ALU.mult, op1=ALU.add))


def three_parts(dve, st, parts, value):
    for j in range(3):
        st.wait()
        st.done(dve.tensor_copy(parts[j], value))
        if j < 2:
            st.wait()
            st.done(dve.tensor_tensor(value, value, parts[j], ALU.subtract))


def layer0_experts(k):
    nc, io, sem = k.nc, k.io, k.sem
    E, F, FS = 8, 176, 352
    HID = E * F + FS
    HT, RT = -(-HID // P), E * F // P
    LAST = HID - (HT - 1) * P
    rows = [P] * (HT - 1) + [LAST]
    with ExitStack() as ctx:
        def sb(name, shape, dt=F32):
            return k.sb("c_" + name, shape, dt, ctx)

        wr, wg, wu, wd = sb("wr", [P, KD, E]), sb("wg", [P, KD, HID]), sb("wu", [P, KD, HID]), sb("wd", [P, HT, D])
        spread = sb("spread", [3 * E, RT, P], BF16)
        wT = sb("wT", [3 * E, NTOK], BF16)
        const, logits_full, logit_steps = sem("c_const_in"), sem("c_logits_full"), sem("c_logit_steps")
        exped, w_turned, wT_out = sem("c_exped"), sem("c_w_turned"), sem("c_wT_out")
        consts = ((wr, "c_wr"), (wg, "c_wg"), (wu, "c_wu"), (wd, "c_wd"), (descending := sb("desc", [P, E]), "descending"))
        with ExitStack() as routing:
            def rb(name, shape, dt=F32):
                return k.sb("cr_" + name, shape, dt, routing)

            lg, best, cand = rb("lg", [P, TILES, E]), rb("best", [P, TILES, E]), rb("cand", [P, TILES, E])
            masks = [rb(f"mask{n}", [P, TILES, E]) for n in range(2)]
            maxima = [rb(f"max{n}", [P, TILES]) for n in range(2)]
            top, total, ex = rb("top", [P, TILES]), rb("total", [P, TILES]), rb("ex", [P, TILES, E])
            w = rb("w", [P, TILES, E])
            wp = rb("wp", [P, TILES, 3, E], BF16)
            lg_ps = k.ps("cps_lg", [P, TILES, E], F32, routing)
            wT_ps = k.ps("cps_wT", [3 * E, NTOK], BF16, routing)
            with nc.Block() as block:
                @block.sync
                def _(sp):
                    for dst, src in consts:
                        sp.dma_start(dst[:], io[src]).then_inc(const, 16)
                    sp.dma_start(spread[:], io["c_spread"]).then_inc(const, 16)

                @block.tensor
                def _(pe):
                    pe.wait_ge(const, 16 * 6)
                    for t in range(TILES):
                        for kd in range(KD):
                            ins = pe.matmul(lg_ps[:, t, :], k.residT[:, kd, t * P:(t + 1) * P], wr[:, kd, :],
                                            start=(kd == 0), stop=(kd == KD - 1))
                    ins.then_inc(logits_full, 1)
                    pe.wait_ge(w_turned, 1)
                    for t in range(TILES):
                        ins = pe.transpose(wT_ps[:, t * P:(t + 1) * P], wp[:, t].rearrange("p a e -> p (a e)"), k.identb[:])
                    ins.then_inc(w_turned, 1)

                @block.scalar
                def _(act):
                    act.wait_ge(exped, 1)
                    act.activation(ex[:], w[:], ACT.Exp).then_inc(exped, 1)

                @block.vector
                def _(dve):
                    full = [P, TILES, E]
                    st = Steps(dve, logit_steps, 0)
                    dve.wait_ge(logits_full, 1)
                    st.done(dve.tensor_copy(lg[:], lg_ps[:]))
                    choose_two(dve, st, lg, best, cand, top, masks, maxima, descending)
                    st.wait()
                    dve.tensor_tensor(w[:], lg[:], maxima[0][:].unsqueeze(2).broadcast_to(full), ALU.subtract).then_inc(exped, 1)
                    dve.wait_ge(exped, 2)
                    st.done(dve.tensor_reduce(total[:], ex[:], AX.X, ALU.add))
                    st.wait()
                    st.done(dve.reciprocal(total[:], total[:]))
                    st.done(dve.tensor_tensor(w[:], masks[0][:], masks[1][:], ALU.add))
                    st.wait()
                    st.done(dve.tensor_tensor(w[:], w[:], ex[:], ALU.mult))
                    st.wait()
                    st.done(dve.tensor_tensor(w[:], w[:], total[:].unsqueeze(2).broadcast_to(full), ALU.mult))
                    three_parts(dve, st, [wp[:, :, j, :] for j in range(3)], w[:])
                    st.wait()
                    dve.sem_inc(w_turned, 1)
                    dve.wait_ge(w_turned, 2)
                    dve.tensor_copy(wT[:], wT_ps[:]).then_inc(wT_out, 1)

        with ExitStack() as main:
            def mb(name, shape, dt=F32):
                return k.sb("cm_" + name, shape, dt, main)

            hid = [mb(f"hid{u}", [P, HT, CHUNK]) for u in range(2)]
            sg, prod = [mb(f"sg{n}", [P, CHUNK]) for n in range(2)], [mb(f"prod{n}", [P, CHUNK]) for n in range(2)]
            ln = ChunkNorm(k, "c", mb)
            g_ps = [k.ps(f"cps_g{n}", [P, CHUNK], F32, main) for n in range(2)]
            u_ps = [k.ps(f"cps_u{n}", [P, CHUNK], F32, main) for n in range(2)]
            w_ps = [k.ps(f"cps_w{n}", [P, CHUNK], F32, main) for n in range(2)]
            o_ps = k.ps("cps_o", [P, TPC, D], F32, main)
            turned = o_ps[:].rearrange("p t (kd n) -> p t kd n", kd=KD)
            up_full, silu_done, prod_done, h_done = sem("c_up_full"), sem("c_silu_done"), sem("c_prod_done"), sem("c_h_done")
            o_full, tr_full, tr_out = sem("c_o_full"), sem("c_tr_full"), sem("c_tr_out")
            with nc.Block() as block:
                @block.sync
                def _(sp):
                    with sp.Fori(0, NCHUNK // 2) as i:
                        for u in range(2):
                            ln.store(sp, 2 * i + u, u)
                    sp.wait_ge(ln.stored, 16 * NCHUNK)

                @block.gpsimd
                def _(gp):
                    with gp.Fori(0, NCHUNK // 2) as i:
                        for u in range(2):
                            ln.variance_power(gp, 2 * i + u, u)

                @block.scalar
                def _(act):
                    with act.Fori(0, NCHUNK // 2) as i:
                        for u in range(2):
                            for m in range(HT):
                                n = (2 * i + u) * HT + m
                                act.wait_ge(up_full, n + 1)
                                act.wait_ge(h_done, n + 1)
                                act.activation(sg[m % 2][0:rows[m]], g_ps[m % 2][0:rows[m]], ACT.Silu).then_inc(silu_done, 1)
                            if u == 1:
                                act.wait_ge(tr_full, 2 * i + 1)
                                ln.copy_turned(act, 2 * i, turned).then_inc(tr_out, 1)
                        act.wait_ge(tr_full, 2 * i + 2)
                        ln.copy_turned(act, 2 * i + 1, turned).then_inc(tr_out, 1)

                @block.vector
                def _(dve):
                    dve.sem_inc(h_done, 2)

                    def sums(i, u):
                        dve.wait_ge(o_full, 2 * i + u + 1)
                        dve.tensor_tensor(ln.r[u][:], o_ps[:], k.resid[:, ds(TPC * (2 * i + u), TPC), :], ALU.add
                                          ).then_inc(ln.r_done, 1)
                        ln.statistics(dve, 2 * i + u, u)

                    with dve.Fori(0, NCHUNK // 2) as i:
                        for u in range(2):
                            for m in range(HT):
                                n, rm = (2 * i + u) * HT + m, rows[m]
                                dve.wait_ge(silu_done, n + 1)
                                if m < RT:
                                    dve.tensor_tensor(prod[m % 2][:], sg[m % 2][:], u_ps[m % 2][:], ALU.mult).then_inc(prod_done, 1)
                                    dve.wait_ge(prod_done, (2 * i + u) * RT + m + 1)
                                    dve.tensor_tensor(hid[u][:, m, :], prod[m % 2][:], w_ps[m % 2][:], ALU.mult).then_inc(h_done, 1)
                                else:
                                    dve.tensor_tensor(hid[u][0:rm, m, :], sg[m % 2][0:rm], u_ps[m % 2][0:rm], ALU.mult).then_inc(h_done, 1)
                                if u == 1 and m == 11:
                                    sums(i, 0)
                                if u == 1 and m == 12:
                                    ln.apply(dve, 2 * i, 0, i)
                        sums(i, 1)
                        ln.apply(dve, 2 * i + 1, 1, i)

                @block.tensor
                def _(pe):
                    pe.wait_ge(wT_out, 1)

                    def down(i, u, t):
                        if t == 0:
                            pe.wait_ge(h_done, (2 * i + u + 1) * HT + 2)
                            pe.wait_ge(tr_out, 2 * i + u)
                        for m in range(HT):
                            ins = pe.matmul(o_ps[:, t, :], hid[u][0:rows[m], m, t * P:(t + 1) * P], wd[0:rows[m], m, :],
                                            start=(m == 0), stop=(m == HT - 1))
                        if t == TPC - 1:
                            ins.then_inc(o_full, 1)

                    with pe.Fori(0, NCHUNK // 2) as i:
                        for u in range(2):
                            for m in range(HT):
                                pe.wait_ge(h_done, (2 * i + u) * HT + m + 1)
                                tok = ds((2 * i + u) * CHUNK, CHUNK)
                                for w_, bank in ((wg, g_ps), (wu, u_ps)):
                                    for kd in range(KD):
                                        ins = pe.matmul(bank[m % 2][0:rows[m], :], w_[:, kd, m * P:m * P + rows[m]],
                                                        k.residT[:, kd, tok], start=(kd == 0), stop=(kd == KD - 1))
                                if m < RT:
                                    ins = pe.matmul(w_ps[m % 2][:], spread[:, m, :], wT[:, tok], start=True, stop=True)
                                ins.then_inc(up_full, 1)
                                if u == 1 and 3 <= m < 3 + 2 * TPC and m % 2 == 1:
                                    down(i, 0, (m - 3) // 2)
                        ln.transpose(pe, 2 * i, 0, turned).then_inc(tr_full, 1)
                        for t in range(TPC):
                            down(i, 1, t)
                        ln.transpose(pe, 2 * i + 1, 1, turned).then_inc(tr_full, 1)


def layer1_state_space(k):
    nc, io, sem = k.nc, k.io, k.sem
    NH, G, CW = 8, 4, 4
    XT, ZT = 6, 4
    MT = XT + ZT
    SPC = CHUNK // T
    with ExitStack() as ctx:
        def sb(name, shape, dt=F32):
            return k.sb("d_" + name, shape, dt, ctx)

        def pair(name, shape, dt=F32):
            return [sb(f"{name}{u}", shape, dt) for u in range(2)]

        win, wout, nw = sb("win", [P, KD, MT * P]), sb("wout", [P, G, D]), sb("nw", [P, G])
        wdt, cw, cb = sb("wdt", [P, KD, NH]), sb("cw", [P, XT, CW]), sb("cb", [P, XT])
        bias, alog, dd = sb("bias", [P, NH]), sb("alog", [P, NH]), sb("dd", [P, NH])
        later, upto, eye = sb("later", [P, P]), sb("upto", [P, T]), sb("eye", [P, T])
        dt, an, ddiag = sb("dt", [P, TILES, NH]), sb("an", [P, NH]), sb("ddiag", [P, NH, T])
        consts = ((win, "d_win"), (wout, "d_wout"), (nw, "d_nw"), (wdt, "d_wdt"), (cw, "d_cw"), (cb, "d_cb"),
                  (bias, "d_bias"), (alog, "d_alog"), (dd, "d_dd"), (later, "d_later"), (upto, "d_upto"), (eye, "d_eye"))
        const, dt_full, pre, pre_act = sem("d_const_in"), sem("d_dt_full"), sem("d_pre_steps"), sem("d_pre_act")
        with ExitStack() as first:
            def fb(name):
                return k.sb("df_" + name, [P, TILES, NH], F32, first)

            x, ab, e, s, q, p = (fb(n) for n in ("x", "ab", "e", "s", "q", "p"))
            dt_ps = k.ps("dps_dt", [P, TILES, NH], F32, first)
            with nc.Block() as block:
                @block.sync
                def _(sp):
                    for dst, src in consts:
                        sp.dma_start(dst[:], io[src]).then_inc(const, 16)

                @block.tensor
                def _(pe):
                    pe.wait_ge(const, 16 * len(consts))
                    for t in range(TILES):
                        for kd in range(KD):
                            ins = pe.matmul(dt_ps[:, t, :], k.residT[:, kd, t * P:(t + 1) * P], wdt[:, kd, :],
                                            start=(kd == 0), stop=(kd == KD - 1))
                    ins.then_inc(dt_full, 1)

                @block.scalar
                def _(act):
                    act.wait_ge(const, 16 * len(consts))
                    act.activation(an[:], alog[:], ACT.Exp).then_inc(pre_act, 1)
                    act.wait_ge(pre_act, 2)
                    act.activation(e[:], ab[:], ACT.Exp, scale=-1.0).then_inc(pre_act, 1)

                @block.vector
                def _(dve):
                    st = Steps(dve, pre, 0)
                    dve.wait_ge(const, 16 * len(consts))
                    dve.wait_ge(dt_full, 1)
                    st.done(dve.tensor_tensor(x[:], dt_ps[:], bias[:].unsqueeze(1).broadcast_to([P, TILES, NH]), ALU.add))
                    st.wait()
                    st.done(dve.tensor_scalar(q[:], x[:], -1.0, None, ALU.mult))
                    st.wait()
                    dve.wait_ge(pre_act, 1)
                    dve.tensor_tensor(ab[:], x[:], q[:], ALU.max).then_inc(pre_act, 1)
                    st.done(dve.tensor_scalar(an[:], an[:], -1.0, None, ALU.mult))
                    dve.wait_ge(pre_act, 3)
                    st.done(dve.tensor_scalar(s[:], e[:], 2.0, None, ALU.add))
                    st.wait()
                    st.done(dve.reciprocal(s[:], s[:]))
                    st.wait()
                    st.done(dve.tensor_tensor(s[:], s[:], e[:], ALU.mult))
                    st.wait()
                    st.done(dve.tensor_tensor(q[:], s[:], s[:], ALU.mult))
                    st.wait()
                    st.done(dve.tensor_scalar(p[:], q[:], 1.0 / 15, None, ALU.mult))
                    for odd in (13, 11, 9, 7, 5, 3):
                        st.wait()
                        st.done(dve.scalar_tensor_tensor(out=p[:], in0=p[:], scalar=1.0 / odd, in1=q[:], op0=ALU.add, op1=ALU.mult))
                    st.wait()
                    st.done(dve.scalar_tensor_tensor(out=p[:], in0=p[:], scalar=1.0, in1=s[:], op0=ALU.add, op1=ALU.mult))
                    st.done(dve.tensor_scalar(x[:], x[:], 0.0, None, ALU.max))
                    st.wait()
                    st.done(dve.scalar_tensor_tensor(out=dt[:], in0=p[:], scalar=2.0, in1=x[:], op0=ALU.mult, op1=ALU.add))
                    st.done(dve.tensor_tensor(ddiag[:], dd[:].unsqueeze(2).broadcast_to([P, NH, T]),
                                              eye[:].unsqueeze(1).broadcast_to([P, NH, T]), ALU.mult))
                    for g in range(G):
                        st.done(dve.tensor_scalar(wout[:, g, :], wout[:, g, :], nw[:, g:g + 1], None, ALU.mult))

        xc, bT, cT = pair("xc", [P, CHUNK]), pair("bT", [P, CHUNK]), pair("cT", [P, G, CHUNK])
        zs, yz, sq = pair("zs", [P, G, CHUNK]), pair("yz", [P, G, CHUNK]), sb("sq", [P, G, CHUNK])
        pad, acc = pair("pad", [P, SPC, CW - 1 + T]), pair("acc", [P, SPC, T])
        dtm, dam, es = pair("dtm", [P, NH, T]), pair("dam", [P, NH, T]), pair("es", [P, NH, T])
        xt, ms, rs = pair("xt", [P, P]), pair("ms", [P, TPC, G]), pair("rs", [P, TPC, G])
        ln = ChunkNorm(k, "d", sb)
        ip = k.ps("dps_ip", [P, 2, CHUNK], F32, ctx)
        tr = k.ps("dps_tr", [P, CHUNK], F32, ctx)
        g_ps, seg_ps = k.ps("dps_g", [P, CHUNK], F32, ctx), k.ps("dps_seg", [P, NH, T], F32, ctx)
        y_ps = k.ps("dps_y", [P, 2, CHUNK], F32, ctx)
        turned = ip[:].rearrange("p b (t kd n) -> p (b t) kd n", kd=KD, n=P)
        outs = [a[:].rearrange("p b (g f) -> p (b g) f", f=D) for a in (ip, y_ps)]

        ip_full, ip_out, taps, conv_done = sem("d_ip_full"), sem("d_ip_out"), sem("d_taps"), sem("d_conv_done")
        conv_in, activated, padded = sem("d_conv_in"), sem("d_activated"), sem("d_padded")
        xt_full, xt_out, dam_done = sem("d_xt_full"), sem("d_xt_out"), sem("d_dam_done")
        g_full, g_out, seg_full, seg_out = sem("d_g_full"), sem("d_g_out"), sem("d_seg_full"), sem("d_seg_out")
        w_done, w_steps, y_full, y_out, sq_done = sem("d_w_done"), sem("d_w_steps"), sem("d_y_full"), sem("d_y_out"), sem("d_sq_done")
        ss_full, ss_out, rs_done = sem("d_ss_full"), sem("d_ss_out"), sem("d_rs_done")
        p_full, p_out, p_steps = sem("d_p_full"), sem("d_p_out"), sem("d_p_steps")
        tr_full, tr_out = sem("d_tr_full"), sem("d_tr_out")

        with nc.Block() as block:
            @block.sync
            def _(sp):
                with sp.Fori(0, NCHUNK // 2) as i:
                    for u in range(2):
                        ln.store(sp, 2 * i + u, u)
                sp.wait_ge(ln.stored, 16 * NCHUNK)

            @block.gpsimd
            def _(gp):
                for n in range(2):
                    gp.memset(pad[n][:, :, 0:CW - 1], 0.0).then_inc(padded, 1)
                with gp.Fori(0, NCHUNK // 2) as i:
                    for u in range(2):
                        gp.wait_ge(ss_out, 2 * i + u + 1)
                        gp.tensor_tensor(rs[u][:].rearrange("p t g -> p (t g)"), ms[u][:].rearrange("p t g -> p (t g)"),
                                         k.mhalf[:, 0:TPC * G], ALU.pow).then_inc(rs_done, 1)
                    for u in range(2):
                        ln.variance_power(gp, 2 * i + u, u)

            @block.scalar
            def _(act):
                act.wait_ge(padded, 2)
                with act.Fori(0, NCHUNK // 2) as i:
                    for u in range(2):
                        c = 2 * i + u
                        dest = [xc[u][:], bT[u][:]] + [cT[u][:, g, :] for g in range(G)]

                        def activate(m):
                            act.wait_ge(conv_done, c * XT + m + 1)
                            act.activation(dest[m], acc[m % 2][:].rearrange("p s t -> p (s t)"), ACT.Silu).then_inc(activated, 1)

                        for m in range(XT):
                            act.wait_ge(ip_full, c * MT + m + 1)
                            src = ip[:, m % 2, :].rearrange("p (s t) -> p s t", t=T)
                            act.wait_ge(activated, c * XT + max(m - 1, 0))
                            act.activation(pad[m % 2][:, :, CW - 1:], src, ACT.Copy)
                            act.activation(acc[m % 2][:], src, ACT.Identity, bias=cb[:, m:m + 1],
                                           scale=cw[:, m, CW - 1:CW]).then_inc(ip_out, 1)
                            if m:
                                activate(m - 1)
                        activate(XT - 1)
                        for m in range(ZT):
                            act.wait_ge(ip_full, c * MT + XT + m + 1)
                            act.activation(zs[u][:, m, :], ip[:, (XT + m) % 2, :], ACT.Silu).then_inc(ip_out, 1)
                    for u in range(2):
                        c = 2 * i + u

                        def square(t):
                            act.wait_ge(y_out, c * TPC + t + 1)
                            act.wait_ge(ss_full, c)
                            cols = slice(t * P, (t + 1) * P)
                            act.activation(sq[:, :, cols], yz[u][:, :, cols], ACT.Square).then_inc(sq_done, 1)

                        for t in range(TPC):
                            act.wait_ge(xt_full, c * TPC + t + 1)
                            act.activation(xt[t % 2][:], tr[:, 0:P], ACT.Copy).then_inc(xt_out, 1)
                            act.wait_ge(seg_full, c * TPC + t + 1)
                            act.activation(es[t % 2][:], seg_ps[:], ACT.Exp).then_inc(seg_out, 1)
                            if t and u == 0:
                                square(t - 1)
                        if u == 0:
                            square(TPC - 1)
                        else:
                            for t in range(TPC):
                                square(t)
                    for u in range(2):
                        act.wait_ge(tr_full, 2 * i + u + 1)
                        ln.copy_turned(act, 2 * i + u, turned).then_inc(tr_out, 1)

            @block.vector
            def _(dve):
                with dve.Fori(0, NCHUNK // 2) as i:
                    for u in range(2):
                        c = 2 * i + u
                        st = Steps(dve, taps, XT * (CW - 2), c)
                        for m in range(XT):
                            dve.wait_ge(ip_out, c * MT + m + 1)
                            for tap in range(CW - 1):
                                ins = dve.scalar_tensor_tensor(out=acc[m % 2][:], in0=pad[m % 2][:, :, tap:tap + T],
                                                               scalar=cw[:, m, tap:tap + 1], in1=acc[m % 2][:],
                                                               op0=ALU.mult, op1=ALU.add)
                                if tap == CW - 2:
                                    ins.then_inc(conv_done, 1)
                                else:
                                    st.done(ins)
                                    st.wait()
                        st.close()
                    for u in range(2):
                        c = 2 * i + u
                        st = Steps(dve, w_steps, 2 * TPC, c)

                        def decays(t):
                            st.done(dve.tensor_tensor(dtm[t % 2][:], dt[:, ds(c * TPC + t, 1), :].rearrange("p t h -> p (t h)")
                                                      .unsqueeze(2).broadcast_to([P, NH, T]),
                                                      upto[:].unsqueeze(1).broadcast_to([P, NH, T]), ALU.mult))
                            st.wait()
                            dve.tensor_tensor(dam[t % 2][:], dtm[t % 2][:], an[:].unsqueeze(2).broadcast_to([P, NH, T]),
                                              ALU.mult).then_inc(dam_done, 1)

                        def weights(t):
                            n = c * TPC + t
                            dve.wait_ge(seg_out, n + 1)
                            dve.wait_ge(g_full, n + 1)
                            w = es[t % 2][:].rearrange("p (g a) l -> p g a l", a=2)
                            cols = g_ps[:, 0:G * T].rearrange("p (g l) -> p g l", l=T)
                            dve.tensor_tensor(w, w, cols.unsqueeze(2).broadcast_to([P, G, 2, T]), ALU.mult).then_inc(g_out, 1)
                            dve.wait_ge(g_out, n + 1)
                            st.done(dve.tensor_tensor(es[t % 2][:], es[t % 2][:], dtm[t % 2][:], ALU.mult))
                            st.wait()
                            dve.tensor_tensor(es[t % 2][:], es[t % 2][:], ddiag[:], ALU.add).then_inc(w_done, 1)

                        def gated(t):
                            dve.wait_ge(y_full, c * TPC + t + 1)
                            view = [a[:, :, t * P:(t + 1) * P].rearrange("p g (b l) -> p b g l", b=2) for a in (yz[u], zs[u])]
                            y = y_ps[:, :, 0:G * T].rearrange("p b (g l) -> p b g l", l=T)
                            dve.tensor_tensor(view[0], y, view[1], ALU.mult).then_inc(y_out, 1)

                        decays(0)
                        for t in range(TPC):
                            if t + 1 < TPC:
                                decays(t + 1)
                            weights(t)
                            if t:
                                gated(t - 1)
                        gated(TPC - 1)
                        st.close()
                        dve.wait_ge(ss_full, c + 1)
                        dve.tensor_scalar(ms[u][:].rearrange("p t g -> p (t g)"), tr[:, 0:TPC * G], 1.0 / P, EPS,
                                          ALU.mult, ALU.add).then_inc(ss_out, 1)
                    for u in range(2):
                        c = 2 * i + u
                        st = Steps(dve, p_steps, TPC * (G - 1), c)
                        dve.wait_ge(rs_done, c + 1)
                        for t in range(TPC):
                            dve.wait_ge(p_full, c * TPC + t + 1)
                            r = ln.r[u][:, t, :]
                            for g in range(G):
                                acc_in = r if g else k.resid[:, ds(c * TPC + t, 1), :].rearrange("p t f -> p (t f)")
                                ins = dve.scalar_tensor_tensor(out=r, in0=outs[t % 2][:, g, :], scalar=rs[u][:, t, g:g + 1],
                                                               in1=acc_in, op0=ALU.mult, op1=ALU.add)
                                if g < G - 1:
                                    st.done(ins)
                                    st.wait()
                                else:
                                    ins.then_inc(p_out, 1)
                        st.close()
                        dve.wait_ge(p_out, (c + 1) * TPC)
                        dve.sem_inc(ln.r_done, 1)
                        ln.statistics(dve, c, u)
                    for u in range(2):
                        ln.apply(dve, 2 * i + u, u, i)

            @block.tensor
            def _(pe):
                with pe.Fori(0, NCHUNK // 2) as i:
                    for u in range(2):
                        c = 2 * i + u
                        tok = ds(c * CHUNK, CHUNK)
                        if u == 0:
                            pe.wait_ge(tr_out, 2 * i)
                        for m in range(MT):
                            pe.wait_ge(ip_out, c * MT + max(m - 1, 0))
                            for kd in range(KD):
                                ins = pe.matmul(ip[:, m % 2, :], win[:, kd, m * P:(m + 1) * P], k.residT[:, kd, tok],
                                                start=(kd == 0), stop=(kd == KD - 1))
                            ins.then_inc(ip_full, 1)
                    for u in range(2):
                        c = 2 * i + u

                        def front(t):
                            n = c * TPC + t
                            cols = slice(t * P, (t + 1) * P)
                            if t == 0:
                                pe.wait_ge(activated, (c + 1) * XT)
                                pe.wait_ge(ss_out, c)
                            pe.wait_ge(xt_out, n)
                            pe.transpose(tr[:, 0:P], xc[u][:, cols], k.ident[:]).then_inc(xt_full, 1)
                            pe.wait_ge(g_out, n)
                            pe.sem_inc(k.passed, 1)
                            for b in range(2):
                                seq = slice(t * P + b * T, t * P + (b + 1) * T)
                                ins = pe.matmul(g_ps[b * T:(b + 1) * T, 0:G * T], bT[u][:, seq], cT[u][:, :, seq],
                                                start=True, stop=True)
                            ins.then_inc(g_full, 1)
                            pe.wait_ge(dam_done, n + 1)
                            pe.wait_ge(seg_out, n)
                            pe.matmul(seg_ps[:], later[:], dam[t % 2][:], start=True, stop=True).then_inc(seg_full, 1)

                        def mix(t):
                            n = c * TPC + t
                            pe.wait_ge(w_done, n + 1)
                            pe.wait_ge(xt_out, n + 1)
                            pe.wait_ge(y_out, n)
                            pe.sem_inc(k.passed, 1)
                            for b in range(2):
                                seq = slice(b * T, (b + 1) * T)
                                for a in range(2):
                                    ins = pe.matmul(y_ps[a * 64:(a + 1) * 64, b, 0:G * T], xt[t % 2][seq, a * 64:(a + 1) * 64],
                                                    es[t % 2][seq, a::2, :], start=True, stop=True)
                            ins.then_inc(y_full, 1)

                        front(0)
                        for t in range(TPC):
                            if t + 1 < TPC:
                                front(t + 1)
                            mix(t)
                        pe.wait_ge(sq_done, (c + 1) * TPC)
                        pe.wait_ge(xt_out, (c + 1) * TPC)
                        for t in range(TPC):
                            for g in range(G):
                                ins = pe.matmul(tr[:, t * G + g:t * G + g + 1], sq[:, g, t * P:(t + 1) * P], k.ones[:, 0:1],
                                                start=True, stop=True)
                        ins.then_inc(ss_full, 1)
                    for u in range(2):
                        c = 2 * i + u
                        for t in range(TPC):
                            if t < 2:
                                pe.wait_ge(y_out, 2 * TPC * (i + 1))
                                pe.wait_ge(p_out, c * TPC)
                            else:
                                pe.wait_ge(p_out, c * TPC + t - 1)
                            for g in range(G):
                                ins = pe.matmul(outs[t % 2][:, g, :], yz[u][:, g, t * P:(t + 1) * P], wout[:, g, :],
                                                start=True, stop=True)
                            ins.then_inc(p_full, 1)
                    for u in range(2):
                        pe.wait_ge(p_out, 2 * TPC * (i + 1))
                        pe.wait_ge(tr_out, 2 * i + u)
                        ln.transpose(pe, 2 * i + u, u, turned).then_inc(tr_full, 1)


def layer1_cross_attention(k):
    nc, io, sem = k.nc, k.io, k.sem
    W, RMS_EPS, FLOOR, TINY = 4, 1e-6, -1e20, 1e-30
    PAIRS, GD = HEADS // 2, 2 * (HD + 1)
    PROJ, COPIED = 4 + W, 2 + W
    with ExitStack() as ctx:
        def sb(name, shape, dt=F32):
            return k.sb("e_" + name, shape, dt, ctx)

        def many(name, shape, dt=F32):
            return [sb(f"{name}{u}", shape, dt) for u in range(W)]

        wq, wk, wv, wo, wg = (sb(n, [P, KD, D]) for n in ("wq", "wk", "wv", "wo", "wg"))
        nw, neg = sb("nw", [P, KD]), sb("neg", [P, TILES, T])
        rs, factors = sb("rs", [P, TILES]), sb("factors", [P, TILES, 2])
        loaded, squared, powered, pre = sem("e_weights_in"), sem("e_squared"), sem("e_powered"), sem("e_pre_steps")
        consts = [(wq, "e_wq"), (wk, "e_wk"), (wv, "e_wv"), (wo, "e_wo"), (wg, "e_wg"), (nw, "e_nw")]
        with ExitStack() as first:
            mask8, junk = k.sb("ef_mask", [P, TILES, T], mybir.dt.uint8, first), k.sb("ef_junk", [P, D], F32, first)
            consts.append((mask8, "e_mask"))
            with nc.Block() as block:
                @block.sync
                def _(sp):
                    for dst, src in consts:
                        sp.dma_start(dst[:], io[src]).then_inc(loaded, 16)

                @block.scalar
                def _(act):
                    for t in range(TILES):
                        if t:
                            act.wait_ge(squared, t)
                        act.activation(junk[:], k.resid[:, t, :], ACT.Square, accum_out=rs[:, t:t + 1]).then_inc(squared, 1)

                @block.gpsimd
                def _(gp):
                    gp.wait_ge(powered, 1)
                    gp.tensor_tensor(rs[:], rs[:], k.mhalf[:, 0:TILES], ALU.pow).then_inc(powered, 1)

                @block.vector
                def _(dve):
                    st = Steps(dve, pre, 0)
                    dve.wait_ge(squared, TILES)
                    dve.tensor_scalar(rs[:], rs[:], 1.0 / D, RMS_EPS, ALU.mult, ALU.add).then_inc(powered, 1)
                    dve.wait_ge(loaded, 16 * len(consts))
                    for w in (wq, wg):
                        for kd in range(KD):
                            dve.tensor_scalar(w[:, kd, :], w[:, kd, :], nw[:, kd:kd + 1], None, ALU.mult)
                    dve.tensor_scalar(neg[:], mask8[:], -1.0, BIG, ALU.add, ALU.mult)
                    dve.wait_ge(powered, 2)
                    dve.tensor_scalar(factors[:, :, 0], rs[:], HD ** -0.5, None, ALU.mult)
                    dve.tensor_scalar(factors[:, :, 1], rs[:], -1.0, None, ALU.mult)

        xs, cs = sb("xs", [P, KD, W * P]), sb("cs", [P, KD, W * P])
        qT = sb("qT", [P, 2, W * P])
        fac, kbd, vbd = many("fac", [P, 2]), many("kbd", [P, 4, 4, T]), many("vbd", [P, 2, PAIRS, 2, HD + 1])
        sm, mx, pr, pt = many("sm", [P, 16, T]), many("mx", [P, 16]), many("pr", [P, 8, P]), many("pt", [P, 8, P])
        gate, total, yn, yT = many("gate", [P, D]), many("total", [P, 16]), many("yn", [P, 16, HD]), many("yT", [P, KD, P])
        ln = LayerNorm(k, "e", sb, W)
        pj = k.ps("eps_pj", [P, 2, 512], F32, ctx)
        s_ps, pt_ps = k.ps("eps_s", [P, 2, 512], F32, ctx), k.ps("eps_pt", [P, 8, P], F32, ctx)
        y_ps, o_ps = k.ps("eps_y", [P, 512], F32, ctx), k.ps("eps_o", [P, 512], F32, ctx)

        tiles_in, vbd_set = sem("e_tiles_in"), sem("e_vbd_set")
        pj_full, pj_out, kbd_done = sem("e_pj_full"), sem("e_pj_out"), sem("e_kbd_done")
        s_full, s_out, shifted, exped = sem("e_s_full"), sem("e_s_out"), sem("e_shifted"), sem("e_exped")
        pt_full, pt_out, y_full, y_out = sem("e_pt_full"), sem("e_pt_out"), sem("e_y_full"), sem("e_y_out")
        o_full, o_out, r_done, steps = sem("e_o_full"), sem("e_o_out"), sem("e_r_done"), sem("e_vector_steps")
        ITERS = TILES // W

        with nc.Block() as block:
            @block.sync
            def _(sp):
                with sp.Fori(0, ITERS) as i:
                    sp.wait_ge(pj_full, PROJ * i)
                    sp.dma_start(xs[:], k.residT[:, :, ds(W * P * i, W * P)]).then_inc(tiles_in, 16)
                    sp.dma_start(cs[:], k.ctxT[:, :, ds(W * P * i, W * P)]).then_inc(tiles_in, 16)
                    ln.store(sp, i)
                sp.wait_ge(ln.stored, 16 * TILES)

            @block.gpsimd
            def _(gp):
                for u in range(W):
                    gp.memset(vbd[u][:], 0.0).then_inc(vbd_set, 1)
                gp.wait_ge(vbd_set, W)
                for u in range(W):
                    for h2 in range(2):
                        gp.memset(vbd[u][h2 * T:(h2 + 1) * T, :, :, h2, HD:], 1.0).then_inc(vbd_set, 1)
                with gp.Fori(0, ITERS) as i:
                    ln.variance_power(gp, i)

            @block.scalar
            def _(act):
                act.wait_ge(vbd_set, 3 * W)
                with act.Fori(0, ITERS) as i:
                    for hh in range(2):
                        act.wait_ge(pj_full, PROJ * i + hh + 1)
                        act.activation(qT[:, hh, :], pj[:, hh, :], ACT.Copy).then_inc(pj_out, 1)
                    for u in range(W):
                        act.wait_ge(pj_full, PROJ * i + 4 + u + 1)
                        v = pj[:, u % 2, 0:D].rearrange("p (b q d) -> p b q d", b=2, d=HD)
                        for h2 in range(2):
                            rows = slice(h2 * T, (h2 + 1) * T)
                            act.activation(vbd[u][rows, :, :, h2, 0:HD], v[rows], ACT.Copy)
                        act.activation(gate[u][:], pj[:, u % 2, D:2 * D], ACT.Exp, scale=fac[u][:, 1:2]).then_inc(pj_out, 1)
                    for u in range(W):
                        act.wait_ge(shifted, W * i + u + 1)
                        act.activation(pr[u][:].rearrange("p a b -> p (a b)"), sm[u][:].rearrange("p a b -> p (a b)"),
                                       ACT.Exp, scale=fac[u][:, 0:1]).then_inc(exped, 1)
                    for u in range(W):
                        act.wait_ge(pt_full, 3 * W * i + u + 1)
                        act.activation(pt[u][:], pt_ps[:], ACT.Copy).then_inc(pt_out, 1)
                    for u in range(W):
                        act.wait_ge(pt_full, 3 * W * i + W + u + 1)
                        act.activation(yT[u][:], pt_ps[:, 4 * (u % 2):4 * (u % 2) + KD, :], ACT.Copy).then_inc(pt_out, 1)
                    for u in range(W):
                        act.wait_ge(pt_full, 3 * W * i + 2 * W + u + 1)
                        act.activation(k.residT[:, :, ds((W * i + u) * P, P)], pt_ps[:, 4 * (u % 2):4 * (u % 2) + KD, :],
                                       ACT.Copy).then_inc(pt_out, 1)

            @block.vector
            def _(dve):
                with dve.Fori(0, ITERS) as i:
                    st = Steps(dve, steps, 8 * W, i)
                    for u in range(W):
                        st.done(dve.tensor_copy(fac[u][:], factors[:, ds(W * i + u, 1), :].rearrange("p t c -> p (t c)")))
                    for hh in range(2):
                        dve.wait_ge(pj_full, PROJ * i + 2 + hh + 1)
                        for u in range(W):
                            kT = pj[:, hh, u * P:(u + 1) * P].rearrange("p (b s) -> p b s", b=2)
                            ins = dve.tensor_tensor(kbd[u][:, 2 * hh:2 * hh + 2], kT.unsqueeze(2).broadcast_to([P, 2, 4, T]),
                                                    k.headmask[:].unsqueeze(1).unsqueeze(3).broadcast_to([P, 2, 4, T]),
                                                    ALU.mult)
                        ins.then_inc(kbd_done, 1)
                    for u in range(W):
                        dve.wait_ge(s_full, W * i + u + 1)
                        dve.tensor_tensor(sm[u][:], s_ps[:].rearrange("p r (h s) -> p (r h) s", s=T),
                                          neg[:, ds(W * i + u, 1), :].broadcast_to([P, 16, T]), ALU.add).then_inc(s_out, 1)
                        dve.wait_ge(s_out, W * i + u + 1)
                        st.done(dve.tensor_reduce(mx[u][:], sm[u][:], AX.X, ALU.max))
                        st.wait()
                        st.done(dve.tensor_scalar(mx[u][:], mx[u][:], FLOOR, None, ALU.max))
                        st.wait()
                        dve.tensor_tensor(sm[u][:], sm[u][:], mx[u][:].unsqueeze(2).broadcast_to([P, 16, T]),
                                          ALU.subtract).then_inc(shifted, 1)
                    for u in range(W):
                        dve.wait_ge(pj_out, COPIED * i + 2 + u + 1)
                        st.done(dve.tensor_scalar(gate[u][:], gate[u][:], 1.0, None, ALU.add))
                        st.wait()
                        st.done(dve.reciprocal(gate[u][:], gate[u][:]))
                    for u in range(W):
                        dve.wait_ge(y_full, W * i + u + 1)
                        y = y_ps[:, 0:16 * (HD + 1)].rearrange("p (h d) -> p h d", d=HD + 1)
                        st.done(dve.tensor_scalar(total[u][:], y[:, :, HD], TINY, None, ALU.max))
                        st.wait()
                        st.done(dve.reciprocal(total[u][:], total[u][:]))
                        st.wait()
                        dve.tensor_tensor(yn[u][:], y[:, :, 0:HD], total[u][:].unsqueeze(2).broadcast_to([P, 16, HD]),
                                          ALU.mult).then_inc(y_out, 1)
                    for u in range(W):
                        dve.wait_ge(o_full, W * i + u + 1)
                        dve.tensor_tensor(ln.r[u][:], o_ps[:, 0:D], gate[u][:], ALU.mult).then_inc(o_out, 1)
                        dve.wait_ge(o_out, W * i + u + 1)
                        dve.tensor_tensor(ln.r[u][:].unsqueeze(1), ln.r[u][:].unsqueeze(1),
                                          k.resid[:, ds(W * i + u, 1), :], ALU.add).then_inc(r_done, 1)
                        dve.wait_ge(r_done, W * i + u + 1)
                        ln.statistics(dve, st, u)
                        st.wait()
                        dve.sem_inc(k.passed, 1)
                        ln.aggregate(dve, u)
                    for u in range(W):
                        ln.apply(dve, i, u)
                    st.close()

            @block.tensor
            def _(pe):
                with pe.Fori(0, ITERS) as i:
                    pe.wait_ge(tiles_in, 32 * (i + 1))
                    for n, (w, src) in enumerate(((wq, xs), (wq, xs), (wk, cs), (wk, cs))):
                        hh = n % 2
                        if n < 2:
                            pe.wait_ge(pj_out, COPIED * i)
                        else:
                            pe.wait_ge(pj_out, COPIED * i + n - 1)
                        for kd in range(KD):
                            ins = pe.matmul(pj[:, hh, :], w[:, kd, hh * P:(hh + 1) * P], src[:, kd, :],
                                            start=(kd == 0), stop=(kd == KD - 1))
                        ins.then_inc(pj_full, 1)
                    for u in range(W):
                        if u < 2:
                            pe.wait_ge(kbd_done, 2 * i + u + 1)
                        else:
                            pe.wait_ge(pj_out, COPIED * i + 2 + u - 1)
                        pe.sem_inc(k.passed, 1)
                        for b in range(2):
                            for h2 in range(2):
                                for kd in range(KD):
                                    pe.matmul(pj[h2 * T:(h2 + 1) * T, u % 2, b * P:(b + 1) * P],
                                              cs[:, kd, u * P + b * T:u * P + (b + 1) * T],
                                              wv[:, kd, h2 * P:(h2 + 1) * P], start=(kd == 0), stop=(kd == KD - 1))
                        for kd in range(KD):
                            ins = pe.matmul(pj[:, u % 2, D:2 * D], xs[:, kd, u * P:(u + 1) * P], wg[:, kd, :],
                                            start=(kd == 0), stop=(kd == KD - 1))
                        ins.then_inc(pj_full, 1)
                    for u in range(W):
                        pe.wait_ge(pj_out, COPIED * i + 2)
                        pe.wait_ge(kbd_done, 2 * (i + 1))
                        pe.wait_ge(s_out, W * i + u)
                        pe.sem_inc(k.passed, 1)
                        for r in range(2):
                            rows = slice(r * 64, r * 64 + 64)
                            for hh in range(2):
                                for b in range(2):
                                    ins = pe.matmul(s_ps[b * T:(b + 1) * T, r, hh * 256:(hh + 1) * 256],
                                                    qT[rows, hh, u * P + b * T:u * P + (b + 1) * T],
                                                    kbd[u][rows, hh * 2 + b, :, :].rearrange("p h s -> p (h s)"),
                                                    start=True, stop=True)
                        ins.then_inc(s_full, 1)
                    for u in range(W):
                        pe.wait_ge(exped, W * i + u + 1)
                        pe.wait_ge(pt_out, 3 * W * i + u)
                        for c in range(8):
                            ins = pe.transpose(pt_ps[:, c, :], pr[u][:, c, :], k.ident[:])
                        ins.then_inc(pt_full, 1)
                    for u in range(W):
                        pe.wait_ge(pt_out, 3 * W * i + u + 1)
                        pe.wait_ge(y_out, W * i + u)
                        for c in range(8):
                            q = (c // 2 % 2) * 4 + (c // 4) * 2 + c % 2
                            for b in range(2):
                                ins = pe.matmul(y_ps[b * T:(b + 1) * T, c * GD:(c + 1) * GD],
                                                pt[u][:, c, b * T:(b + 1) * T],
                                                vbd[u][:, b, q, :, :].rearrange("p h d -> p (h d)"),
                                                start=True, stop=True)
                        ins.then_inc(y_full, 1)
                    for u in range(W):
                        pe.wait_ge(y_out, W * i + u + 1)
                        pe.wait_ge(pt_out, 3 * W * i + W + max(u - 1, 0))
                        y = yn[u][:].rearrange("p h d -> p (h d)")
                        for c in range(KD):
                            ins = pe.transpose(pt_ps[:, 4 * (u % 2) + c, :], y[:, c * P:(c + 1) * P], k.ident[:])
                        ins.then_inc(pt_full, 1)
                    for u in range(W):
                        pe.wait_ge(pt_out, 3 * W * i + W + u + 1)
                        pe.wait_ge(o_out, W * i + u)
                        for c in range(KD):
                            ins = pe.matmul(o_ps[:, 0:D], yT[u][:, c, :], wo[:, c, :], start=(c == 0), stop=(c == KD - 1))
                        ins.then_inc(o_full, 1)
                    for u in range(W):
                        pe.wait_ge(pt_out, 3 * W * i + 2 * W + max(u - 1, 0))
                        ln.transpose(pe, i, u, pt_ps[:, 4 * (u % 2):4 * (u % 2) + KD, :]).then_inc(pt_full, 1)


def layer1_experts(k):
    nc, io, sem = k.nc, k.io, k.sem
    E, R, F, LORA_SCALE = 8, 16, 704, 32.0 / 16.0
    HT = -(-F // P)
    rows = [P] * (HT - 1) + [F - (HT - 1) * P]
    STACK = 2 * E + 2 * 3
    with ExitStack() as ctx:
        def sb(name, shape, dt=F32):
            return k.sb("f_" + name, shape, dt, ctx)

        gw, w1, w3, w2 = sb("gw", [P, KD, E]), sb("w1", [P, KD, F]), sb("w3", [P, KD, F]), sb("w2", [P, HT, D])
        a1, a3, b1, b3 = sb("a1", [P, KD, P]), sb("a3", [P, KD, P]), sb("b1", [P, F]), sb("b3", [P, F])
        a2, b2, desc = sb("a2", [P, HT, P]), sb("b2", [P, D]), sb("desc", [P, E])
        select = sb("select", [STACK, 4, P], BF16)
        stack = sb("stack", [STACK, NTOK], BF16)
        const, logits_full, logit_steps = sem("f_const_in"), sem("f_logits_full"), sem("f_logit_steps")
        exped, turning, stack_out = sem("f_exped"), sem("f_turning"), sem("f_stack_out")
        first_consts = ((gw, "f_gw"), (desc, "descending"))
        consts = ((select, "f_select"), (a1, "f_a1"), (a3, "f_a3"), (w1, "f_w1"), (w3, "f_w3"), (b1, "f_b1"),
                  (b3, "f_b3"), (a2, "f_a2"), (w2, "f_w2"), (b2, "f_b2"))
        with ExitStack() as routing:
            def rb(name, shape, dt=F32):
                return k.sb("fr_" + name, shape, dt, routing)

            lg, best, cand = rb("lg", [P, TILES, E]), rb("best", [P, TILES, E]), rb("cand", [P, TILES, E])
            masks, maxima = [rb(f"mask{n}", [P, TILES, E]) for n in range(2)], [rb(f"max{n}", [P, TILES]) for n in range(2)]
            top, e2, w = rb("top", [P, TILES]), rb("e2", [P, TILES]), rb("w", [P, TILES, 2])
            pieces = rb("pieces", [P, TILES, STACK], BF16)
            lg_ps = k.ps("fps_lg", [P, TILES, E], F32, routing)
            stack_ps = k.ps("fps_stack", [STACK, NTOK], BF16, routing)
            with nc.Block() as block:
                @block.sync
                def _(sp):
                    for dst, src in first_consts:
                        sp.dma_start(dst[:], io[src]).then_inc(logits_full, 16)
                    for dst, src in consts:
                        sp.dma_start(dst[:], io[src]).then_inc(const, 16)

                @block.tensor
                def _(pe):
                    pe.wait_ge(logits_full, 32)
                    for t in range(TILES):
                        for kd in range(KD):
                            ins = pe.matmul(lg_ps[:, t, :], k.residT[:, kd, t * P:(t + 1) * P], gw[:, kd, :],
                                            start=(kd == 0), stop=(kd == KD - 1))
                    ins.then_inc(logits_full, 1)
                    pe.wait_ge(turning, 1)
                    for t in range(TILES):
                        ins = pe.transpose(stack_ps[:, t * P:(t + 1) * P], pieces[:, t, :], k.identb[:])
                    ins.then_inc(turning, 1)

                @block.scalar
                def _(act):
                    act.wait_ge(exped, 1)
                    act.activation(e2[:], top[:], ACT.Exp).then_inc(exped, 1)

                @block.vector
                def _(dve):
                    st = Steps(dve, logit_steps, 0)
                    dve.wait_ge(logits_full, 33)
                    st.done(dve.tensor_copy(lg[:], lg_ps[:]))
                    choose_two(dve, st, lg, best, cand, top, masks, maxima, desc)
                    st.wait()
                    for n in range(2):
                        st.done(dve.tensor_copy(pieces[:, :, n * E:(n + 1) * E], masks[n][:]))
                    st.wait()
                    dve.tensor_tensor(top[:], maxima[1][:], maxima[0][:], ALU.subtract).then_inc(exped, 1)
                    dve.wait_ge(exped, 2)
                    st.done(dve.tensor_scalar(top[:], e2[:], 1.0, None, ALU.add))
                    st.wait()
                    st.done(dve.reciprocal(w[:, :, 0], top[:]))
                    st.wait()
                    st.done(dve.tensor_tensor(w[:, :, 1], w[:, :, 0], e2[:], ALU.mult))
                    parts = pieces[:, :, 2 * E:].rearrange("p t (n j) -> p t n j", n=2)
                    three_parts(dve, st, [parts[:, :, :, j] for j in range(3)], w[:])
                    st.wait()
                    dve.sem_inc(turning, 1)
                    dve.wait_ge(turning, 2)
                    dve.tensor_copy(stack[:], stack_ps[:]).then_inc(stack_out, 1)

        hid = [sb(f"hid{u}", [P, HT, CHUNK]) for u in range(2)]
        sg, prod = [sb(f"sg{n}", [P, CHUNK]) for n in range(2)], [sb(f"prod{n}", [P, CHUNK]) for n in range(2)]
        aw = [[sb(f"aw{s}{n}", [P, CHUNK]) for n in range(2)] for s in range(3)]
        kept = [[sb(f"kept{s}{n}", [P, CHUNK]) for n in range(2)] for s in range(2)]
        both = [[sb(f"both{s}{n}", [P, CHUNK]) for n in range(2)] for s in range(2)]
        mask, weight, change = [sb(f"mask{n}", [P, CHUNK]) for n in range(2)], [sb(f"weight{n}", [P, CHUNK]) for n in range(2)], sb("change", [P, CHUNK])
        inner = [[sb(f"inner{a}{n}", [P, CHUNK]) for n in range(2)] for a in range(2)]
        z = [sb(f"z{n}", [P, CHUNK]) for n in range(2)]
        ln = ChunkNorm(k, "f", sb)
        h_ps = [[k.ps(f"fps_h{s}{n}", [P, CHUNK], F32, ctx) for n in range(2)] for s in range(2)]
        front = [k.ps(f"fps_front{n}", [P, CHUNK], F32, ctx) for n in range(2)]
        o_ps = k.ps("fps_o", [P, TPC, D], F32, ctx)
        front_full, front_out, changed = sem("f_front_full"), sem("f_front_out"), sem("f_changed")
        h_full, silu_done, h_read, aw_done = sem("f_h_full"), sem("f_silu_done"), sem("f_h_read"), sem("f_aw_done")
        prod_done = sem("f_prod_done")
        hid_done, low_out, z_done = sem("f_hid_done"), sem("f_low_out"), sem("f_z_done")
        o_full, low_used = sem("f_o_full"), sem("f_low_used")
        JOBS = 2 * HT
        order = [(0, 0)] + [j for m in range(1, HT) for j in ((m, 0), (m - 1, 1))] + [(HT - 1, 1)]
        place = {job: n for n, job in enumerate(order)}
        step = {job: place[job] + (job[1] if place[job] + 1 < JOBS else 0) for job in order}
        ready = sorted(order, key=lambda job: (step[job], job[1], job[0]))
        rank = {job: n for n, job in enumerate(ready)}
        y = io["out"].rearrange("(t p) d -> p t d", p=P)

        with nc.Block() as block:
            @block.sync
            def _(sp):
                with sp.Fori(0, NCHUNK // 2) as i:
                    for u in range(2):
                        c = 2 * i + u
                        sp.wait_ge(ln.rn_done, c + 1)
                        sp.dma_start(y[:, ds(TPC * c, TPC), :], ln.rn[u][:]).then_inc(ln.stored, 16)
                sp.wait_ge(ln.stored, 16 * NCHUNK)

            @block.gpsimd
            def _(gp):
                with gp.Fori(0, NCHUNK // 2) as i:
                    for u in range(2):
                        c = 2 * i + u
                        for m in range(HT):
                            gp.wait_ge(aw_done, c * JOBS + rank[m, 1] + 1)
                            if m == 0:
                                gp.wait_ge(o_full, 2 * i)
                            rm = rows[m]
                            gp.tensor_tensor(hid[u][0:rm, m, :], aw[m % 3][0][0:rm], aw[m % 3][1][0:rm], ALU.add).then_inc(hid_done, 1)
                        if u == 1:
                            ln.variance_power(gp, 2 * i, 0)
                    ln.variance_power(gp, 2 * i + 1, 1)

            @block.scalar
            def _(act):
                with act.Fori(0, NCHUNK // 2) as i:
                    for u in range(2):
                        c = 2 * i + u
                        for n, dst in enumerate((mask, weight)):
                            act.wait_ge(front_full, 3 * c + n + 1)
                            act.activation(dst[0][:], front[0][:], ACT.Copy)
                            act.activation(dst[1][:], front[1][:], ACT.Copy).then_inc(front_out, 1)
                        for n, (m, choice) in enumerate(order):
                            rm, s = rows[m], m % 2
                            act.wait_ge(prod_done, c * JOBS + (rank[order[n - 2]] + 1 if n >= 2 else 0))
                            if choice == 0:
                                act.wait_ge(h_full, c * JOBS + n + 1)
                                act.activation(sg[n % 2][0:rm], h_ps[n % 2][0][0:rm], ACT.Silu)
                                act.wait_ge(h_read, c * JOBS + (place[m - 2, 1] + 3 if m >= 2 else 2))
                                act.activation(kept[s][0][0:rm], h_ps[n % 2][0][0:rm], ACT.Copy)
                                act.activation(kept[s][1][0:rm], h_ps[n % 2][1][0:rm], ACT.Copy).then_inc(silu_done, 1)
                            else:
                                act.wait_ge(h_read, c * JOBS + n + 3)
                                act.activation(sg[n % 2][0:rm], both[s][0][0:rm], ACT.Silu).then_inc(silu_done, 1)

            @block.vector
            def _(dve):
                dve.sem_inc(h_read, 2)

                def sums(c, u):
                    dve.wait_ge(o_full, c + 1)
                    dve.tensor_tensor(ln.r[u][:], o_ps[:], k.resid[:, ds(TPC * c, TPC), :], ALU.add).then_inc(ln.r_done, 1)
                    ln.statistics(dve, c, u)

                with dve.Fori(0, NCHUNK // 2) as i:
                    for u in range(2):
                        c = 2 * i + u
                        dve.wait_ge(front_out, 3 * c + 1)
                        dve.tensor_tensor(change[:], mask[1][:], mask[0][:], ALU.subtract).then_inc(changed, 1)
                        dve.wait_ge(changed, c + 1)
                        dve.wait_ge(front_full, 3 * c + 3)
                        for n, by in enumerate((mask[0], change)):
                            for a in range(2):
                                ins = dve.tensor_tensor(inner[a][n][:], front[a][:], by[:], ALU.mult)
                        ins.then_inc(front_out, 1)
                        def take(m, choice):
                            rm, n = rows[m], place[m, choice]
                            dve.wait_ge(silu_done, c * JOBS + n + 1)
                            if choice == 0:
                                dve.tensor_tensor(prod[n % 2][0:rm], sg[n % 2][0:rm], h_ps[n % 2][1][0:rm], ALU.mult).then_inc(prod_done, 1)
                                dve.wait_ge(prod_done, c * JOBS + rank[m, choice] + 1)
                                dve.sem_inc(h_read, 1)
                            else:
                                dve.tensor_tensor(prod[n % 2][0:rm], sg[n % 2][0:rm], both[m % 2][1][0:rm], ALU.mult).then_inc(prod_done, 1)
                                dve.wait_ge(prod_done, c * JOBS + rank[m, choice] + 1)
                            dve.wait_ge(hid_done, c * HT + max(m - 2, 0))
                            dve.wait_ge(low_used, c * JOBS + (rank[m - 3, choice] + 1 if m >= 3 else 0))
                            dve.tensor_tensor(aw[m % 3][choice][0:rm], prod[n % 2][0:rm], weight[choice][0:rm], ALU.mult).then_inc(aw_done, 1)

                        for n, (m, choice) in enumerate(order):
                            if choice == 1:
                                rm = rows[m]
                                dve.wait_ge(h_full, c * JOBS + n + 1)
                                for j in range(2):
                                    ins = dve.tensor_tensor(both[m % 2][j][0:rm], kept[m % 2][j][0:rm], h_ps[n % 2][j][0:rm], ALU.add)
                                ins.then_inc(h_read, 1)
                            for job in ready:
                                if step[job] == n:
                                    take(*job)
                            if u == 1 and n == 3:
                                sums(2 * i, 0)
                        dve.wait_ge(low_used, (c + 1) * JOBS)
                        for n in range(2):
                            ins = dve.tensor_tensor(z[n][:], front[n][:], mask[n][:], ALU.mult)
                        ins.then_inc(low_out, 1)
                        dve.wait_ge(low_out, c + 1)
                        dve.tensor_tensor(z[0][:], z[0][:], z[1][:], ALU.add).then_inc(z_done, 1)
                        if u == 1:
                            ln.apply(dve, 2 * i, 0, i)
                    sums(2 * i + 1, 1)
                    ln.apply(dve, 2 * i + 1, 1, i)

            @block.tensor
            def _(pe):
                pe.wait_ge(const, 16 * len(consts))
                pe.wait_ge(stack_out, 1)

                def lead(c, n):
                    if n == 0:
                        pe.wait_ge(low_out, c)
                    else:
                        pe.wait_ge(front_out, 3 * c + n)
                    pe.sem_inc(k.passed, 1)
                    tok = ds(c * CHUNK, CHUNK)
                    for j in range(2):
                        if n < 2:
                            ins = pe.matmul(front[j][:], select[:, 2 * n + j, :], stack[:, tok], start=True, stop=True)
                        else:
                            for kd in range(KD):
                                ins = pe.matmul(front[j][:], (a1, a3)[j][:, kd, :], k.residT[:, kd, tok],
                                                start=(kd == 0), stop=(kd == KD - 1))
                    ins.then_inc(front_full, 1)

                def hidden(c, n, m, choice):
                    rm, cols = rows[m], slice(m * P, m * P + rows[m])
                    pe.wait_ge(h_read, c * JOBS + n + 1)
                    pe.sem_inc(k.passed, 1)
                    for j, (w, b) in enumerate(((w1, b1), (w3, b3))):
                        bank = h_ps[n % 2][j][0:rm, :]
                        if choice == 0:
                            for kd in range(KD):
                                pe.matmul(bank, w[:, kd, cols], k.residT[:, kd, ds(c * CHUNK, CHUNK)], start=(kd == 0), stop=False)
                        ins = pe.matmul(bank, b[:, cols], inner[j][choice][:], start=(choice == 1), stop=True)
                    ins.then_inc(h_full, 1)

                def low(c, m, choice):
                    pe.wait_ge(aw_done, c * JOBS + rank[m, choice] + 1)
                    rm = rows[m]
                    pe.matmul(front[choice][:], a2[0:rm, m, :], aw[m % 3][choice][0:rm], start=(m == 0),
                              stop=(m == HT - 1)).then_inc(low_used, 1)

                def down(c, u, t):
                    if t == 0:
                        pe.wait_ge(hid_done, (c + 1) * HT)
                        pe.wait_ge(ln.r_done, c)
                        pe.wait_ge(z_done, c + 1)
                    for m in range(HT):
                        pe.matmul(o_ps[:, t, :], hid[u][0:rows[m], m, t * P:(t + 1) * P], w2[0:rows[m], m, :],
                                  start=(m == 0), stop=False)
                    ins = pe.matmul(o_ps[:, t, :], z[0][:, t * P:(t + 1) * P], b2[:], start=False, stop=True)
                    if t == TPC - 1:
                        ins.then_inc(o_full, 1)

                with pe.Fori(0, NCHUNK // 2) as i:
                    for u in range(2):
                        c = 2 * i + u
                        for n in range(3):
                            lead(c, n)
                            if u == 1:
                                down(c - 1, 0, n)
                        if u == 1:
                            down(c - 1, 0, 3)
                        pe.wait_ge(front_out, 3 * c + 3)
                        for n, (m, choice) in enumerate(order):
                            hidden(c, n, m, choice)
                            for job in ready:
                                if step[job] == n - 1:
                                    low(c, *job)
                        for job in ready:
                            if step[job] == JOBS - 1:
                                low(c, *job)
                    for t in range(TPC):
                        down(2 * i + 1, 1, t)


def experts_layout(f, out, rows_to_parts):
    def padded(a):
        full = np.zeros((-(-a.shape[0] // P) * P, a.shape[1]), a.dtype)
        full[:a.shape[0]] = a
        return rows_to_parts(full)

    E, F = 8, 176
    out["c_wr"] = rows_to_parts(f["L0_ffn_Wr"].T)
    out["c_wg"] = rows_to_parts(np.concatenate([f["L0_ffn_Wg"].reshape(E * F, D), f["L0_ffn_Wsg"]]).T)
    out["c_wu"] = rows_to_parts(np.concatenate([f["L0_ffn_Wu"].reshape(E * F, D), f["L0_ffn_Wsu"]]).T)
    out["c_wd"] = padded(np.concatenate([f["L0_ffn_Wd"].transpose(0, 2, 1).reshape(E * F, D), f["L0_ffn_Wsd"].T]))
    unit = np.arange(E * F).reshape(-1, P) // F
    out["c_spread"] = np.tile(unit[None] == np.arange(E)[:, None, None], (3, 1, 1)).astype(mybir.dt.np(BF16))
    out["descending"] = np.tile(np.arange(E, 0, -1, dtype=np.float32)[None], (P, 1))


def state_space_layout(f, out, rows_to_parts):
    NH, G = 8, 4
    W = f["L1_attn_W_in"]
    DI, CONV = 512, 768
    out["d_win"] = rows_to_parts(np.concatenate([W[DI:DI + CONV], W[:DI]]).T)
    out["d_wdt"] = rows_to_parts(W[DI + CONV:].T)
    out["d_wout"] = rows_to_parts(f["L1_attn_W_out"].T)
    out["d_nw"] = f["L1_attn_norm_weight"].reshape(G, P).T
    out["d_cw"] = rows_to_parts(f["L1_attn_conv_w"])
    out["d_cb"] = f["L1_attn_conv_b"].reshape(-1, P).T
    for name, src in (("d_bias", "dt_bias"), ("d_alog", "A_log"), ("d_dd", "D")):
        out[name] = np.tile(f["L1_attn_" + src][None], (P, 1))
    row = np.arange(P)
    same = row[:, None] // T == row[None, :] // T
    out["d_later"] = (same & (row[:, None] > row[None, :])).astype(np.float32)
    out["d_upto"] = (row[:, None] % T <= np.arange(T)[None, :]).astype(np.float32)
    out["d_eye"] = (row[:, None] % T == np.arange(T)[None, :]).astype(np.float32)


def cross_layout(f, out, rows_to_parts, order):
    wq, wk, wv, wo, wg = (f["L1_xattn_" + n].T for n in ("wq", "wk", "wv", "wo", "wg"))
    for name, w in (("wq", wq), ("wk", wk), ("wg", wg)):
        out["e_" + name] = rows_to_parts(w)
    out["e_wv"] = rows_to_parts(wv.reshape(D, HEADS // 2, 2, HD).transpose(0, 2, 1, 3).reshape(D, D))
    out["e_wo"] = rows_to_parts(wo.reshape(HEADS, HD, D)[order].reshape(D, D))
    out["e_nw"] = f["L1_xattn_norm_w"].reshape(KD, P).T
    mask = f["mask_BxS2_bk0"].reshape(TILES, 2, T)
    out["e_mask"] = np.repeat(mask.transpose(1, 0, 2), T, axis=0)



def lora_layout(f, out, rows_to_parts):
    E, R, F = 8, 16, 704

    def padded(a):
        full = np.zeros((-(-a.shape[0] // P) * P, a.shape[1]), a.dtype)
        full[:a.shape[0]] = a
        return rows_to_parts(full)

    g = {n: f["L1_ffn_" + n] for n in ("gate_w", "w1", "w3", "w2", "a1", "b1", "a3", "b3", "a2", "b2")}
    out["f_gw"] = rows_to_parts(g["gate_w"].T)
    for n in ("w1", "w3"):
        out["f_" + n] = rows_to_parts(g[n].T)
    out["f_w2"] = padded(g["w2"].T)
    for n in ("a1", "a3"):
        out["f_" + n] = rows_to_parts(g[n].reshape(E * R, D).T)
    for n in ("b1", "b3", "b2"):
        out["f_" + n] = g[n].transpose(0, 2, 1).reshape(E * R, -1)
    out["f_a2"] = padded(g["a2"].reshape(E * R, F).T)
    select = np.zeros((2 * E + 6, 4, P), np.float32)
    for n in range(2):
        for e in range(E):
            select[n * E + e, n, e * R:(e + 1) * R] = 32.0 / 16.0
        select[2 * E + 3 * n:2 * E + 3 * n + 3, 2 + n, :] = 1.0
    out["f_select"] = select.astype(mybir.dt.np(BF16))


def layout(inputs):
    f = {n: np.asarray(a) for n, a in inputs.items()}

    def rows_to_parts(a):
        return np.ascontiguousarray(a.reshape(-1, P, a.shape[1]).transpose(1, 0, 2))

    def halves(a):
        return a.reshape(a.shape[0], -1, HALF, 2).transpose(0, 1, 3, 2).reshape(a.shape[0], -1)

    out = {}
    x = f["x"].reshape(NTOK, D)
    out["x"] = rows_to_parts(x)
    out["xT"] = rows_to_parts(x.T)
    out["a_wqkv"] = rows_to_parts(np.concatenate([halves(f["L0_attn_Wq"]), halves(f["L0_attn_Wk"]), f["L0_attn_Wv"]], 1))
    out["a_bias"] = np.concatenate([halves(f["L0_attn_bq"][None]), halves(f["L0_attn_bk"][None]),
                                    f["L0_attn_bv"][None], f["L0_attn_bv"][None]], 1)
    out["a_factor"] = np.tile(np.concatenate([f["L0_attn_alpha"], np.ones(GROUPS, np.float32)])[None], (P, 1))
    order = [hh * 8 + r * 4 + hq * 2 + h2 for r in range(2) for hh in range(2) for hq in range(2) for h2 in range(2)]
    out["a_wo"] = rows_to_parts(f["L0_attn_Wo"].reshape(HEADS, HD, D)[order].reshape(D, D))
    out["a_bo"] = f["L0_attn_bo"][None]
    inv_freq = np.float32(1.0) / np.float32(10000.0) ** (np.arange(0, HD, 2, dtype=np.float32) / np.float32(HD))
    freqs = np.arange(T, dtype=np.float32)[:, None] * inv_freq[None, :]
    cos, sin = np.cos(freqs), np.sin(freqs)
    out["cos"] = np.tile(np.concatenate([cos, cos], 1), (2, 1)).astype(np.float32)
    out["sin"] = np.tile(np.concatenate([-sin, sin], 1), (2, 1)).astype(np.float32)
    pos = np.arange(P) % T
    out["causal"] = np.where(np.arange(T)[None, :] <= pos[:, None], 0.0, -BIG).astype(np.float32)
    out["headmask"] = (np.arange(4)[None, :] == (np.arange(P)[:, None] % 64) // HD).astype(np.float32)
    ctx = f["ctx_2048"].reshape(NTOK, D)
    out["ctxT"] = rows_to_parts(ctx.T)
    out["ctx_dg"] = ctx.reshape(TILES, P // 8, 8, D).transpose(2, 1, 0, 3).reshape(P, TILES, D)
    out["b_gamma"] = np.full((P, 1), f["L0_xattn_gamma"], np.float32)
    more_layout(f, out, rows_to_parts, order)
    return {n: np.ascontiguousarray(a) for n, a in out.items()}


def more_layout(f, out, rows_to_parts, order):
    experts_layout(f, out, rows_to_parts)
    state_space_layout(f, out, rows_to_parts)
    cross_layout(f, out, rows_to_parts, order)
    lora_layout(f, out, rows_to_parts)


def decoder(nc, io):
    with ExitStack() as ctx:
        k = Kernel(nc, ctx, io)
        setup(k)
        layer0_attention(k)
        context_parts(k)
        layer0_cross_attention(k)
        layer0_experts(k)
        k.recycle()
        layer1_state_space(k)
        layer1_cross_attention(k)
        layer1_experts(k)


def kernel(**inputs):
    import concourse.bacc as _bacc
    from concourse.bass_utils import run_bass_kernel_spmd as _run

    nc = _bacc.Bacc("TRN2", target_bir_lowering=False, num_devices=1)
    arrays = {f"in_{name}": a for name, a in layout(inputs).items()}
    io = {name[3:]: nc.dram_tensor(name, a.shape, mybir.dt.from_np(a.dtype), kind="ExternalInput").ap()
          for name, a in arrays.items()}
    io["out"] = nc.dram_tensor("out", (NTOK, D), F32, kind="ExternalOutput").ap()
    decoder(nc, io)
    r = _run(nc, [arrays], core_ids=[0])
    return r.results[0]["out"].reshape(B, T, D)
```

```python
from contextlib import ExitStack

import numpy as np

import concourse.bass as bass
from concourse import mybir

F32 = mybir.dt.float32
BF16 = mybir.dt.bfloat16
ALU = mybir.AluOpType
ACT = mybir.ActivationFunctionType
AX = mybir.AxisListType
ds = bass.ds

P = 128
B, T, D = 32, 64, 256
NTOK = B * T
TILES = NTOK // P
SEQS = P // T
KD = D // P
CHUNK = 512
NCHUNK = NTOK // CHUNK
TPC = CHUNK // P
EPS = 1e-5
BIG = 1e30

HEADS, HD = 16, 16
GROUPS = 4
HALF = HD // 2


class Steps:

    def __init__(self, eng, sem, per, it=0):
        self.eng, self.sem, self.per, self.it, self.n = eng, sem, per, it, 0

    def done(self, ins):
        self.n += 1
        return ins.then_inc(self.sem, 1)

    def wait(self, back=0):
        self.eng.wait_ge(self.sem, self.it * self.per + self.n - back)

    def close(self):
        assert self.n == self.per, (self.n, self.per)


class Kernel:

    def __init__(self, nc, ctx, io):
        self.nc, self.ctx, self.io, self.sems = nc, ctx, io, []
        self.resid = self.sb("resid", [P, TILES, D])
        self.residT = self.sb("residT", [P, KD, NTOK])
        self.ctxT = self.sb("ctxT_all", [P, KD, NTOK])
        self.ident = self.sb("ident", [P, P])
        self.identb = self.sb("identb", [P, P], BF16)
        self.mhalf = self.sb("mhalf", [P, 64])
        self.phalf = self.sb("phalf", [P, 32])
        self.ones = self.sb("ones", [P, P])
        self.built = ctx.enter_context(nc.semaphore("consts_built"))
        self.passed = ctx.enter_context(nc.semaphore("passed"))
        self.headmask = self.sb("headmask", [P, 4])

    def sb(self, name, shape, dt=F32, ctx=None):
        return (ctx or self.ctx).enter_context(self.nc.sbuf_tensor(name, shape, dt))

    def ps(self, name, shape, dt=F32, ctx=None):
        return (ctx or self.ctx).enter_context(self.nc.psum_tensor(name, shape, dt))

    def sem(self, name):
        self.sems.append(self.nc.alloc_semaphore(name=name))
        return self.sems[-1]

    def recycle(self):
        self.nc.all_engine_barrier()
        self.nc.clear_and_free_semaphores(self.sems)
        self.nc.all_engine_barrier()
        self.sems = []


class Tile:

    def __init__(self, i, c):
        self.i, self.c, self.v = i, c, c % 3
        self.t = c if i is None else 3 * i + c
        self.n = c // 3 + 1 if i is None else i + (c // 3 + 1)
        self.live = i is not None or 0 <= c < TILES

    def plus(self, d):
        return Tile(self.i, self.c + d)


def slots(eng, slot, end=TILES + 2):
    for c in range(4):
        slot(Tile(None, c))
    with eng.Fori(0, (TILES - 4) // 3) as i:
        for w in range(3):
            slot(Tile(i, 4 + w))
    for c in range(TILES, end):
        slot(Tile(None, c))


def wait(eng, sem, value):
    if not isinstance(value, int) or value > 0:
        eng.wait_ge(sem, value)


class TileNorm:

    def __init__(self, k, name, sb):
        self.k = k
        self.r, self.rn = ([sb(f"{n}{v}", [P, D]) for v in range(3)] for n in ("r", "rn"))
        self.stats, self.mv, self.rstd = ([sb(f"{n}{v}", [P, w]) for v in range(3)] for n, w in (("stats", 6), ("mv", 2), ("rstd", 1)))
        self.stats_done, self.mv_done, self.eps_done = k.sem(name + "_stats_done"), k.sem(name + "_mv_done"), k.sem(name + "_eps_done")
        self.rstd_done, self.rn_done = k.sem(name + "_rstd_done"), k.sem(name + "_rn_done")
        self.turned, self.copied = k.sem(name + "_rn_turned"), k.sem(name + "_residT_copied")
        self.stored = [k.sem(f"{name}_resid_stored{v}") for v in range(3)]

    def statistics(self, dve, x):
        dve.bn_stats(self.stats[x.v][:], self.r[x.v][:]).then_inc(self.stats_done, 1)
        dve.wait_ge(self.stats_done, x.t + 1)
        dve.sem_inc(self.k.passed, 1)
        dve.bn_aggr(self.mv[x.v][:], self.stats[x.v][:]).then_inc(self.mv_done, 1)

    def variance_power(self, gp, x):
        gp.wait_ge(self.mv_done, x.t + 1)
        gp.sem_inc(self.k.passed, 1)
        gp.tensor_scalar(self.rstd[x.v][:], self.mv[x.v][:, 1:2], EPS, None, ALU.add).then_inc(self.eps_done, 1)
        gp.wait_ge(self.eps_done, x.t + 1)
        gp.tensor_tensor(self.rstd[x.v][:], self.rstd[x.v][:], self.k.mhalf[:, 0:1], ALU.pow).then_inc(self.rstd_done, 1)

    def apply(self, dve, x):
        dve.wait_ge(self.rstd_done, x.t + 1)
        dve.wait_ge(self.stored[x.v], 16 * (x.n - 1))
        dve.tensor_scalar(self.rn[x.v][:], self.r[x.v][:], self.mv[x.v][:, 0:1], self.rstd[x.v][:], ALU.subtract,
                          ALU.mult).then_inc(self.rn_done, 1)

    def store(self, sp, x):
        sp.wait_ge(self.rn_done, x.t + 1)
        sp.dma_start(self.k.resid[:, ds(x.t, 1), :], self.rn[x.v][:].unsqueeze(1)).then_inc(self.stored[x.v], 16)

    def wait_stored(self, sp):
        for v in range(3):
            sp.wait_ge(self.stored[v], 16 * len(range(v, TILES, 3)))

    def transpose(self, pe, x, tr):
        pe.wait_ge(self.rn_done, x.t + 1)
        for kd in range(KD):
            ins = pe.transpose(tr[:, kd, :], self.rn[x.v][:, kd * P:(kd + 1) * P], self.k.ident[:])
        ins.then_inc(self.turned, 1)

    def copy_turned(self, act, x, tr):
        act.wait_ge(self.turned, x.t + 1)
        act.activation(self.k.residT[:, :, ds(x.t * P, P)], tr, ACT.Copy).then_inc(self.copied, 1)


def setup(k):
    with k.nc.Block() as block:
        @block.gpsimd
        def _(gp):
            gp.memset(k.ident[:], 0.0).then_inc(k.built, 1)
            gp.memset(k.identb[:], 0.0).then_inc(k.built, 1)
            gp.memset(k.mhalf[:], -0.5).then_inc(k.built, 1)
            gp.memset(k.phalf[:], 0.5).then_inc(k.built, 1)
            gp.memset(k.ones[:], 1.0).then_inc(k.built, 1)
            gp.wait_ge(k.built, 2)
            for m in (k.ident, k.identb):
                gp.affine_select(out=m[:], in_=m[:], compare_op=ALU.not_equal, fill=1.0, base=0,
                                 pattern=[[-1, P]], channel_multiplier=1).then_inc(k.built, 1)


def layer0_attention(k):
    nc, io, sem = k.nc, k.io, k.sem
    k.kparts = nc.dram_tensor("kparts", (TILES, 3, 3, 8, P // 8, D), BF16, kind="Internal").ap()
    with ExitStack() as ctx:
        def sb(name, shape, dt=F32):
            return k.sb("a_" + name, shape, dt, ctx)

        def three(name, shape, dt=F32):
            return [sb(f"{name}{v}", shape, dt) for v in range(3)]

        NQK, NV, H20 = (HEADS + GROUPS) * HD, GROUPS * HD, HEADS + GROUPS
        wqkv, wo = sb("wqkv", [P, KD, NQK + NV]), sb("wo", [P, KD, D])
        biasrow, borow = sb("biasrow", [1, NQK + NV]), sb("borow", [1, D])
        factor, cos, sin = sb("factor", [P, H20]), sb("cos", [P, HD]), sb("sin", [P, HD])
        causal = sb("causal", [P, T])
        x_sb = three("x", [P, KD, P])
        qk, sq = three("qk", [P, H20, HD]), three("sq", [P, H20, HD])
        ss, nrm, sc = three("ss", [P, H20]), three("nrm", [P, H20]), three("sc", [P, H20])
        turned, rot = three("turned", [P, H20, HD]), three("rot", [P, H20, HD])
        krep, qkT, kbd = three("krep", [P, GROUPS, 4, HD]), three("qkT", [P, 4, P]), three("kbd", [P, 4, 4, T])
        sm, mx, pr = three("sm", [P, 16, T]), three("mx", [P, 16]), three("pr", [P, 8, P])
        pt, vbd = three("pt", [P, 8, P]), three("vbd", [P, 2, GROUPS, 2, HD + 1])
        rc, yn, yT = three("rc", [P, 16]), three("yn", [P, 16, HD]), three("yT", [P, KD, P])
        c_in, c_parts = three("c", [P, D]), three("cparts", [P, 3, D], BF16)
        ln = TileNorm(k, "a", sb)
        qkv_ps, tr = k.ps("a_qkv", [P, 512], F32, ctx), k.ps("a_tr", [P, 4, P], F32, ctx)
        s_ps, pt_ps = k.ps("a_s", [P, 2, 512], F32, ctx), k.ps("a_pt", [P, 8, P], F32, ctx)
        y_ps, o_all = k.ps("a_y", [P, 512], F32, ctx), k.ps("a_o", [P, 4, P], F32, ctx)
        o_ps, o_tr = o_all[:, 0:KD, :].rearrange("p a b -> p (a b)"), o_all[:, KD:2 * KD, :]

        const, resid_in = sem("a_const_in"), sem("a_resid_in")
        x_in, c_loaded, c_written = ([sem(f"a_{n}{v}") for v in range(3)] for n in ("x_in", "context_in", "parts_written"))
        qk_full, v_full, qk_out, v_out = sem("a_qk_full"), sem("a_v_full"), sem("a_qk_out"), sem("a_v_out")
        summed, normed, rotated, repeated = sem("a_summed"), sem("a_normed"), sem("a_rotated"), sem("a_repeated")
        qk_turned, qkT_out, kbd_done = sem("a_qk_turned"), sem("a_qkT_out"), sem("a_kbd_done")
        s_full, s_out, shifted, exped = sem("a_s_full"), sem("a_s_out"), sem("a_shifted"), sem("a_exped")
        pt_full, pt_out, y_full, y_out = sem("a_pt_full"), sem("a_pt_out"), sem("a_y_full"), sem("a_y_out")
        y_turned, yT_out, o_full, o_out = sem("a_y_turned"), sem("a_yT_out"), sem("a_o_full"), sem("a_o_out")
        rot_steps, max_done, rc_done = sem("a_rotation_steps"), sem("a_max_done"), sem("a_rc_done")
        vbd_set, parts_steps, split = sem("a_vbd_set"), sem("a_parts_steps"), sem("a_context_split")
        consts = ((wqkv, "a_wqkv"), (biasrow, "a_bias"), (factor, "a_factor"), (cos, "cos"), (sin, "sin"),
                  (causal, "causal"), (wo, "a_wo"), (borow, "a_bo"), (k.headmask, "headmask"))

        with nc.Block() as block:
            @block.sync
            def _(sp):
                for dst, src in consts:
                    sp.dma_start(dst[:], io[src]).then_inc(const, 16)
                sp.dma_start(k.resid[:], io["x"]).then_inc(resid_in, 16)
                sp.dma_start(k.ctxT[:], io["ctxT"]).then_inc(resid_in, 16)

                def slot(s):
                    if s.live:
                        wait(sp, v_full, s.t - 2)
                        sp.dma_start(x_sb[s.v][:], io["xT"][:, :, ds(s.t * P, P)]).then_inc(x_in[s.v], 16)
                        wait(sp, split, s.t - 2)
                        sp.dma_start(c_in[s.v][:].unsqueeze(1), io["ctx_dg"][:, ds(s.t, 1), :]).then_inc(c_loaded[s.v], 16)
                    x = s.plus(-2)
                    if x.live:
                        sp.wait_ge(split, x.t + 1)
                        for j in range(3):
                            sp.dma_start(k.kparts[ds(x.t, 1), j].rearrange("t i d g f -> (t d g) i f"),
                                         c_parts[x.v][:, j, :].unsqueeze(1).broadcast_to([P, 3, D])).then_inc(c_written[x.v], 16)
                    x = s.plus(-4)
                    if x.live:
                        ln.store(sp, x)

                slots(sp, slot, TILES + 4)
                ln.wait_stored(sp)
                for v in range(3):
                    sp.wait_ge(c_written[v], 48 * len(range(v, TILES, 3)))

            @block.gpsimd
            def _(gp):
                for v in range(3):
                    gp.memset(vbd[v][:], 0.0).then_inc(vbd_set, 1)
                gp.wait_ge(vbd_set, 3)
                for v in range(3):
                    for h2 in range(2):
                        gp.memset(vbd[v][h2 * T:(h2 + 1) * T, :, :, h2, HD:], 1.0).then_inc(vbd_set, 1)

                def slot(s):
                    x = s.plus(-3)
                    if x.live:
                        ln.variance_power(gp, x)
                    if s.live:
                        gp.wait_ge(summed, s.t + 1)
                        gp.tensor_tensor(nrm[s.v][:], ss[s.v][:], k.phalf[:, 0:H20], ALU.pow).then_inc(normed, 1)
                    if s.live:
                        gp.wait_ge(c_loaded[s.v], 16 * s.n)
                        gp.wait_ge(c_written[s.v], 48 * (s.n - 1))
                        gp.sem_inc(k.passed, 1)
                        st, c, parts = Steps(gp, parts_steps, 4, s.t), c_in[s.v], c_parts[s.v]
                        for j in range(3):
                            if j:
                                st.wait()
                                gp.sem_inc(k.passed, 1)
                            ins = gp.tensor_copy(parts[:, j, :], c[:])
                            if j < 2:
                                st.done(ins)
                                st.wait()
                                st.done(gp.tensor_tensor(c[:], c[:], parts[:, j, :], ALU.subtract))
                            else:
                                ins.then_inc(split, 1)
                        st.close()

                slots(gp, slot, TILES + 3)

            @block.scalar
            def _(act):
                act.wait_ge(resid_in, 32)
                for dst, src in k.ahead:
                    act.dma_start(dst[:], src).then_inc(k.ahead_in, 16)
                act.wait_ge(vbd_set, 9)

                def slot(s):
                    m, x, l = s.plus(-1), s.plus(-2), s.plus(-3)
                    if x.live:
                        act.wait_ge(pt_full, x.t + 1)
                        act.activation(pt[x.v][:], pt_ps[:], ACT.Copy).then_inc(pt_out, 1)
                    if m.live:
                        act.wait_ge(rotated, m.t + 1)
                        act.activation(krep[m.v][:], rot[m.v][:, HEADS:H20, :].unsqueeze(2)
                                       .broadcast_to([P, GROUPS, 4, HD]), ACT.Copy).then_inc(repeated, 1)
                        act.wait_ge(qk_turned, m.t + 1)
                        act.activation(qkT[m.v][:], tr[:], ACT.Copy).then_inc(qkT_out, 1)
                    if s.live:
                        act.wait_ge(qk_full, s.t + 1)
                        flat = qkv_ps[:, 0:NQK].rearrange("p (h d) -> p h d", d=HD)
                        act.activation(sq[s.v][:], flat, ACT.Square).then_inc(qk_out, 1)
                        act.activation(qk[s.v][:], flat, ACT.Copy).then_inc(qk_out, 1)
                    if l.live:
                        ln.copy_turned(act, l, o_tr)
                    if x.live:
                        act.wait_ge(y_turned, x.t + 1)
                        act.activation(yT[x.v][:], o_tr, ACT.Copy).then_inc(yT_out, 1)
                    if s.live:
                        act.wait_ge(v_full, s.t + 1)
                        v4 = qkv_ps[:, NQK:NQK + 2 * NV].rearrange("p (b g d) -> p b g d", b=2, g=GROUPS)
                        for h2 in range(2):
                            rows = slice(h2 * T, (h2 + 1) * T)
                            act.activation(vbd[s.v][rows, :, :, h2, 0:HD], v4[rows], ACT.Copy).then_inc(v_out, 1)
                    if m.live:
                        act.wait_ge(shifted, m.t + 1)
                        act.activation(pr[m.v][:].rearrange("p a b -> p (a b)"),
                                       sm[m.v][:].rearrange("p a b -> p (a b)"), ACT.Exp).then_inc(exped, 1)

                slots(act, slot, TILES + 3)

            @block.vector
            def _(dve):
                dve.wait_ge(const, 16 * len(consts))
                dve.wait_ge(resid_in, 32)

                def rotate(x):
                    v, full = x.v, [P, H20, HD]
                    st = Steps(dve, rot_steps, 5, x.t)
                    dve.wait_ge(normed, x.t + 1)
                    st.done(dve.tensor_scalar(nrm[v][:], nrm[v][:], 1e-6, None, ALU.add))
                    st.wait()
                    st.done(dve.reciprocal(sc[v][:], nrm[v][:]))
                    st.wait()
                    st.done(dve.tensor_tensor(sc[v][:], sc[v][:], factor[:], ALU.mult))
                    st.wait()
                    dve.wait_ge(qk_out, 2 * x.t + 2)
                    st.done(dve.tensor_tensor(qk[v][:], qk[v][:], sc[v][:].unsqueeze(2).broadcast_to(full), ALU.mult))
                    st.wait()
                    half = [slice(0, HALF), slice(HALF, HD)]
                    for a in range(2):
                        dve.tensor_tensor(turned[v][:, :, half[a]], qk[v][:, :, half[1 - a]],
                                          sin[:, half[a]].unsqueeze(1).broadcast_to([P, H20, HALF]), ALU.mult)
                    st.done(dve.tensor_tensor(rot[v][:], qk[v][:], cos[:].unsqueeze(1).broadcast_to(full), ALU.mult))
                    st.wait()
                    dve.tensor_tensor(rot[v][:], rot[v][:], turned[v][:], ALU.add).then_inc(rotated, 1)
                    st.close()

                def slot(s):
                    m, x, l = s.plus(-1), s.plus(-2), s.plus(-3)
                    if m.live:
                        rotate(m)
                    if l.live:
                        ln.apply(dve, l)
                    if m.live:
                        dve.wait_ge(qkT_out, m.t + 1)
                        kT = qkT[m.v][:, 2:4, :].rearrange("p h (b s) -> p (h b) s", b=2)
                        dve.tensor_tensor(kbd[m.v][:], kT.unsqueeze(2).broadcast_to([P, 4, 4, T]),
                                          k.headmask[:].unsqueeze(1).unsqueeze(3).broadcast_to([P, 4, 4, T]),
                                          ALU.mult).then_inc(kbd_done, 1)
                    if x.live:
                        dve.wait_ge(y_full, x.t + 1)
                        y = y_ps[:, 0:16 * (HD + 1)].rearrange("p (h d) -> p h d", d=HD + 1)
                        dve.reciprocal(rc[x.v][:], y[:, :, HD]).then_inc(rc_done, 1)
                        dve.wait_ge(rc_done, x.t + 1)
                        dve.tensor_tensor(yn[x.v][:], y[:, :, 0:HD], rc[x.v][:].unsqueeze(2).broadcast_to([P, 16, HD]),
                                          ALU.mult).then_inc(y_out, 1)
                    if s.live:
                        dve.wait_ge(qk_out, 2 * s.t + 1)
                        dve.tensor_reduce(ss[s.v][:], sq[s.v][:], AX.X, ALU.add).then_inc(summed, 1)
                    if m.live:
                        dve.wait_ge(s_full, m.t + 1)
                        dve.tensor_tensor(sm[m.v][:], s_ps[:].rearrange("p r (h s) -> p (r h) s", s=T),
                                          causal[:].unsqueeze(1).broadcast_to([P, 16, T]), ALU.add).then_inc(s_out, 1)
                        dve.wait_ge(s_out, m.t + 1)
                        dve.tensor_reduce(mx[m.v][:], sm[m.v][:], AX.X, ALU.max).then_inc(max_done, 1)
                        dve.wait_ge(max_done, m.t + 1)
                        dve.tensor_tensor(sm[m.v][:], sm[m.v][:], mx[m.v][:].unsqueeze(2).broadcast_to([P, 16, T]),
                                          ALU.subtract).then_inc(shifted, 1)
                    if x.live:
                        dve.wait_ge(o_full, x.t + 1)
                        dve.tensor_tensor(ln.r[x.v][:].unsqueeze(1), o_ps.unsqueeze(1),
                                          k.resid[:, ds(x.t, 1), :], ALU.add).then_inc(o_out, 1)
                        dve.wait_ge(o_out, x.t + 1)
                        ln.statistics(dve, x)

                slots(dve, slot, TILES + 3)

            @block.tensor
            def _(pe):
                pe.wait_ge(const, 16 * len(consts))

                def project(x):
                    pe.wait_ge(x_in[x.v], 16 * x.n)
                    wait(pe, v_out, 2 * x.t)
                    for kd in range(KD):
                        pe.matmul(qkv_ps[:, 0:NQK], x_sb[x.v][:, kd, :], wqkv[:, kd, 0:NQK], start=(kd == 0), stop=False)
                    pe.matmul(qkv_ps[:, 0:NQK], k.ones[0:1, :], biasrow[0:1, 0:NQK], start=False, stop=True).then_inc(qk_full, 1)

                def values(x):
                    pe.wait_ge(qk_out, 2 * x.t + 2)
                    pe.sem_inc(k.passed, 1)
                    for b in range(2):
                        for h2 in range(2):
                            v = qkv_ps[h2 * T:(h2 + 1) * T, NQK + b * NV:NQK + (b + 1) * NV]
                            for kd in range(KD):
                                pe.matmul(v, x_sb[x.v][:, kd, b * T:(b + 1) * T], wqkv[:, kd, NQK:NQK + NV], start=(kd == 0), stop=False)
                            ins = pe.matmul(v, k.ones[0:1, 0:T], biasrow[0:1, NQK:NQK + NV], start=False, stop=True)
                    ins.then_inc(v_full, 1)

                def scores(x):
                    pe.wait_ge(kbd_done, x.t + 1)
                    pe.wait_ge(qkT_out, x.t + 1)
                    wait(pe, s_out, x.t)
                    pe.sem_inc(k.passed, 1)
                    for r in range(2):
                        rows = slice(r * 64, r * 64 + 64)
                        for hh in range(2):
                            for b in range(2):
                                ins = pe.matmul(s_ps[b * T:(b + 1) * T, r, hh * 256:(hh + 1) * 256],
                                                qkT[x.v][rows, hh, b * T:(b + 1) * T],
                                                kbd[x.v][rows, hh * 2 + b, :, :].rearrange("p h s -> p (h s)"),
                                                start=True, stop=True)
                    ins.then_inc(s_full, 1)

                def mix(x):
                    pe.wait_ge(pt_out, x.t + 1)
                    pe.wait_ge(v_out, 2 * x.t + 2)
                    wait(pe, y_out, x.t)
                    pe.sem_inc(k.passed, 1)
                    for c in range(8):
                        g = (c // 2 % 2) * 2 + c // 4
                        for b in range(2):
                            ins = pe.matmul(y_ps[b * T:(b + 1) * T, c * 34:(c + 1) * 34],
                                            pt[x.v][:, c, b * T:(b + 1) * T],
                                            vbd[x.v][:, b, g, :, :].rearrange("p h d -> p (h d)"),
                                            start=True, stop=True)
                    ins.then_inc(y_full, 1)

                def turn(dst, src, blocks, signal):
                    for c in range(blocks):
                        ins = pe.transpose(dst[:, c, :], src[:, c * P:(c + 1) * P], k.ident[:])
                    ins.then_inc(signal, 1)

                def slot(s):
                    m, x, l = s.plus(-1), s.plus(-2), s.plus(-3)
                    if s.live:
                        project(s)
                    if x.live:
                        pe.wait_ge(exped, x.t + 1)
                        wait(pe, pt_out, x.t)
                        turn(pt_ps, pr[x.v][:].rearrange("p c n -> p (c n)"), 8, pt_full)
                    if m.live:
                        pe.wait_ge(rotated, m.t + 1)
                        wait(pe, qkT_out, m.t)
                        turn(tr, rot[m.v][:, 0:HEADS, :].rearrange("p h d -> p (h d)"), 2, k.passed)
                        pe.wait_ge(repeated, m.t + 1)
                        turn(tr[:, 2:4, :], krep[m.v][:].rearrange("p g j d -> p (g j d)"), 2, qk_turned)
                    if x.live:
                        mix(x)
                    if l.live:
                        ln.transpose(pe, l, o_tr)
                    if s.live:
                        values(s)
                    if m.live:
                        scores(m)
                    if x.live:
                        pe.wait_ge(y_out, x.t + 1)
                        if l.live:
                            pe.wait_ge(ln.copied, l.t + 1)
                        turn(o_tr, yn[x.v][:].rearrange("p h d -> p (h d)"), KD, y_turned)
                    if x.live:
                        pe.wait_ge(yT_out, x.t + 1)
                        pe.matmul(o_ps, k.ones[0:1, :], borow[:], start=True, stop=False)
                        for c in range(KD):
                            ins = pe.matmul(o_ps, yT[x.v][:, c, :], wo[:, c, :], start=False, stop=(c == KD - 1))
                        ins.then_inc(o_full, 1)

                slots(pe, slot, TILES + 3)


def layer0_cross_attention(k):
    nc, io, sem = k.nc, k.io, k.sem
    G, DT, L = P // 8, 8, D
    ROWS = 9 * DT
    SCALE = float(DT) ** -0.5
    qparts = nc.dram_tensor("qparts", (TILES, 3, DT, G, L), BF16, kind="Internal").ap()
    with ExitStack() as ctx:
        def sb(name, shape, dt=F32):
            return k.sb("b_" + name, shape, dt, ctx)

        def three(name, shape, dt=F32):
            return [sb(f"{name}{v}", shape, dt) for v in range(3)]

        gamma = sb("gamma", [P, 1])
        xp, rest = three("xp", [P, 3, L], BF16), sb("rest", [P, L])
        qs, ks = three("qs", [P, G, L], BF16), three("ks", [P, G, L], BF16)
        vt = three("vt", [P, KD, G, 32])
        nm, nrest, mp = three("nm", [P, 2 * G]), three("nrest", [P, 2 * G]), three("mp", [P, 3, 2 * G], BF16)
        mt = three("mt", [96, P], BF16)
        pr = [sb(f"pr{n}", [P, KD, L]) for n in range(8)]
        os_ = three("os", [P, 4, L])
        nd = three("nd", [P, 4, L])
        rec, r, rn = sb("rec", [P, L]), sb("r", [P, L]), three("rn", [P, L])
        stats, mv, rstd = three("stats", [P, 6]), three("mv", [P, 2]), three("rstd", [P, 1])
        s1 = [k.ps(f"b_s1{n}", [P, 2, 2, L], F32, ctx) for n in range(2)]
        s2 = [k.ps(f"b_s2{n}", [P, KD, L], F32, ctx) for n in range(2)]
        o_ps, tr = k.ps("b_o", [P, 2, L], F32, ctx), k.ps("b_tr", [P, 4, P], F32, ctx)
        trb = tr[:, 0, :].bitcast(BF16)[:, 0:P]

        const, preset, vt_set, gp_steps = sem("b_const_in"), sem("b_preset"), sem("b_vt_set"), sem("b_gp_steps")
        split, vt_done = sem("b_split"), sem("b_vt_done")
        written = [sem(f"b_q_written{v}") for v in range(3)]
        placed = [sem(f"b_qk_placed{v}") for v in range(3)]
        s1_full, s1_out, m_split, steps = sem("b_s1_full"), sem("b_s1_out"), sem("b_m_split"), sem("b_steps")
        mp_turned, mt_out = sem("b_mp_turned"), sem("b_mt_out")
        rn_turned, rT_out, eps_done, m_steps = sem("b_rn_turned"), sem("b_rT_out"), sem("b_eps_done"), sem("b_m_steps")
        m_placed = [sem(f"b_m_placed{v}") for v in range(3)]
        s2_full, s2_out, pv_done, o_out = sem("b_s2_full"), sem("b_s2_out"), sem("b_pv_done"), sem("b_o_out")
        nd_in = [sem(f"b_nd_in{v}") for v in range(3)]
        mv_done, rstd_done, rn_done = sem("b_mv_done"), sem("b_rstd_done"), sem("b_rn_done")
        stored = [sem(f"b_stored{v}") for v in range(3)]
        LAG = 2

        with nc.Block() as block:
            @block.sync
            def _(sp):
                sp.dma_start(gamma[:], io["b_gamma"]).then_inc(const, 16)

                def load(x):
                    if x.i is None and x.c < 3:
                        sp.wait_ge(preset, x.c + 1)
                    wait(sp, pv_done, 4 * (x.t - 2))
                    sp.dma_start(ks[x.v][0:ROWS, :, :].rearrange("r g f -> r (g f)"),
                                 k.kparts[ds(x.t, 1)].rearrange("t j i d g f -> (t j i d) (g f)")).then_inc(placed[x.v], 16)
                    sp.wait_ge(split, x.t + 1)
                    for i in range(3):
                        sp.dma_start(qparts[ds(x.t, 1), i].rearrange("t d g f -> (t g) d f"), xp[x.v][:, i, :]
                                     ).then_inc(written[x.v], 16)
                    sp.wait_ge(written[x.v], 48 * x.n)
                    sp.dma_start(qs[x.v][0:ROWS, :, :].rearrange("r g f -> r (g f)"),
                                 qparts[ds(x.t, 1)].rearrange("t i d g f -> (t i d) (g f)").partition_broadcast(3)
                                 ).then_inc(placed[x.v], 16)

                def numerators(x, q):
                    if q % 2 == 0:
                        sp.wait_ge(o_out, 2 * x.t + q // 2 + 1)
                    sp.dma_start(nd[x.v][32 * q:32 * q + 32, :, :], os_[x.v][:, q, :]).then_inc(nd_in[x.v], 16)

                def slot(s):
                    if s.live:
                        load(s)
                    x = s.plus(-3)
                    if x.live:
                        numerators(x, 0)
                        numerators(x, 1)
                        numerators(x, 2)
                        numerators(x, 3)
                    x = s.plus(-4)
                    if x.live:
                        sp.wait_ge(rn_done, x.t + 1)
                        sp.dma_start(k.resid[:, ds(x.t, 1), :], rn[x.v][:].unsqueeze(1)).then_inc(stored[x.v], 16)

                slots(sp, slot, TILES + 4)
                for v in range(3):
                    sp.wait_ge(stored[v], 16 * len(range(v, TILES, 3)))

            @block.gpsimd
            def _(gp):

                def slot(s):
                    x = s
                    if x.live:
                        xs = k.resid[:, ds(x.t, 1), :].rearrange("p t f -> p (t f)")
                        gp.wait_ge(written[x.v], 48 * (x.n - 1))
                        st = Steps(gp, gp_steps, 4, x.t)
                        gp.sem_inc(k.passed, 1)
                        st.done(gp.tensor_copy(xp[x.v][:, 0, :], xs))
                        st.wait()
                        gp.sem_inc(k.passed, 1)
                        st.done(gp.tensor_tensor(rest[:], xs, xp[x.v][:, 0, :], ALU.subtract))
                        st.wait()
                        gp.sem_inc(k.passed, 1)
                        st.done(gp.tensor_copy(xp[x.v][:, 1, :], rest[:]))
                        st.wait()
                        st.done(gp.tensor_tensor(rest[:], rest[:], xp[x.v][:, 1, :], ALU.subtract))
                        st.wait()
                        gp.sem_inc(k.passed, 1)
                        gp.tensor_copy(xp[x.v][:, 2, :], rest[:]).then_inc(split, 1)
                        if x.i is None and x.c < 3:
                            gp.memset(vt[x.v][:], 1.0).then_inc(vt_set, 1)
                            gp.wait_ge(vt_set, x.c + 1)
                        wait(gp, pv_done, 4 * (x.t - 2))
                        gp.sem_inc(k.passed, 1)
                        for lh in range(KD):
                            gp.tensor_copy(vt[x.v][:, lh, :, 0:32:4],
                                           k.ctxT[:, lh, ds(x.t * P, P)].rearrange("p (g d) -> p g d", d=DT)
                                           ).then_inc(vt_done, 1)
                        st.close()
                    x = s.plus(-3)
                    if x.live:
                        gp.wait_ge(mv_done, x.t + 1)
                        gp.sem_inc(k.passed, 1)
                        gp.tensor_scalar(rstd[x.v][:], mv[x.v][:, 1:2], EPS, None, ALU.add).then_inc(eps_done, 1)
                        gp.wait_ge(eps_done, x.t + 1)
                        gp.tensor_tensor(rstd[x.v][:], rstd[x.v][:], k.mhalf[:, 0:1], ALU.pow).then_inc(rstd_done, 1)

                slots(gp, slot, TILES + 3)

            @block.vector
            def _(dve):
                for v in range(3):
                    dve.memset(ks[v][64:96, :, :], 1.0).then_inc(preset, 1)
                dve.wait_ge(const, 16)

                def finish(x):
                    st = Steps(dve, steps, 4, x.t)
                    dve.wait_ge(nd_in[x.v], 64 * x.n)
                    st.done(dve.reciprocal(rec[:], nd[x.v][:, 1, :]))
                    st.wait()
                    st.done(dve.tensor_tensor(rec[:], rec[:], nd[x.v][:, 0, :], ALU.mult))
                    st.wait()
                    st.done(dve.scalar_tensor_tensor(out=r[:], in0=rec[:], scalar=gamma[:],
                                                     in1=k.resid[:, ds(x.t, 1), :].rearrange("p t f -> p (t f)"),
                                                     op0=ALU.mult, op1=ALU.add))
                    st.wait()
                    st.done(dve.bn_stats(stats[x.v][:], r[:]))
                    st.wait()
                    dve.sem_inc(k.passed, 1)
                    dve.bn_aggr(mv[x.v][:], stats[x.v][:]).then_inc(mv_done, 1)

                def slot(s):
                    if s.live:
                        for gp in range(8):
                            dve.wait_ge(s1_full, 8 * s.t + gp + 1)
                            dve.tensor_reduce(nm[s.v][:, 4 * gp:4 * gp + 4].rearrange("p (g h) -> p g h", h=2),
                                              s1[gp % 2][:], AX.X, ALU.max, negate=True).then_inc(s1_out, 1)
                        st = Steps(dve, m_steps, 4, s.t)
                        dve.wait_ge(s1_out, 8 * s.t + 8)
                        st.done(dve.tensor_copy(mp[s.v][:, 0, :], nm[s.v][:]))
                        st.wait()
                        st.done(dve.tensor_tensor(nrest[s.v][:], nm[s.v][:], mp[s.v][:, 0, :], ALU.subtract))
                        st.wait()
                        st.done(dve.tensor_copy(mp[s.v][:, 1, :], nrest[s.v][:]))
                        st.wait()
                        st.done(dve.tensor_tensor(nrest[s.v][:], nrest[s.v][:], mp[s.v][:, 1, :], ALU.subtract))
                        st.wait()
                        dve.tensor_copy(mp[s.v][:, 2, :], nrest[s.v][:]).then_inc(m_split, 1)
                        st.close()
                    x = s.plus(-2)
                    if x.live:
                        finish(x)
                        dve.wait_ge(rstd_done, x.t + 1)
                        dve.wait_ge(stored[x.v], 16 * (x.n - 1))
                        wait(dve, rn_turned, x.t - 2)
                        dve.tensor_scalar(rn[x.v][:], r[:], mv[x.v][:, 0:1], rstd[x.v][:], ALU.subtract,
                                          ALU.mult).then_inc(rn_done, 1)

                slots(dve, slot)

            @block.scalar
            def _(act):
                act.sem_inc(s2_out, 2)

                def products_out(x, half):
                    act.wait_ge(pv_done, 4 * x.t + 2 * half + 2)
                    act.wait_ge(nd_in[x.v], 64 * (x.n - 1))
                    act.activation(os_[x.v][:, 2 * half:2 * half + 2, :], o_ps[:], ACT.Copy).then_inc(o_out, 1)

                def slot(s):
                    x, last, done = s.plus(-1), s.plus(-2), s.plus(-3)
                    for g in range(G):
                        if x.live:
                            act.wait_ge(s2_full, G * x.t + g + 1)
                            if g % 4 == 0:
                                wait(act, pv_done, 4 * x.t + g // 4 - 1)
                            act.activation(pr[g % 8][:], s2[g % 2][:], ACT.Exp, scale=SCALE).then_inc(s2_out, 1)
                        if x.live and g == 9:
                            products_out(x, 0)
                        if g == 1 and last.live:
                            products_out(last, 1)
                        if g == 7 and done.live:
                            act.wait_ge(rn_turned, done.t + 1)
                            act.activation(k.residT[:, :, ds(done.t * P, P)], tr[:, 0:KD, :], ACT.Copy).then_inc(rT_out, 1)
                    if s.live:
                        act.wait_ge(mp_turned, s.t + 1)
                        act.wait_ge(m_placed[s.v], 48 * (s.n - 1))
                        act.activation(mt[s.v][:], trb[0:96, :], ACT.Copy).then_inc(mt_out, 1)
                        act.wait_ge(mt_out, s.t + 1)
                        for part in range(3):
                            act.dma_start(qs[s.v][ROWS + part:ROWS + part + 1, :, :].rearrange("r g (h f) -> r (g h) f", h=2),
                                          mt[s.v][32 * part:32 * part + 32, :]).then_inc(m_placed[s.v], 16)

                slots(act, slot, TILES + 3)

            @block.tensor
            def _(pe):
                def first_pass(x, gp):
                    wait(pe, s1_out, 8 * x.t + gp - 1)
                    for g in (2 * gp, 2 * gp + 1):
                        for qh in range(2):
                            ins = pe.matmul(s1[gp % 2][:, g % 2, qh, :], qs[x.v][0:ROWS, g, qh * P:(qh + 1) * P],
                                            ks[x.v][0:ROWS, g, :], start=True, stop=True)
                    ins.then_inc(s1_full, 1)

                def second_pass(x, gp):
                    for g in (2 * gp, 2 * gp + 1):
                        pe.wait_ge(s2_out, G * x.t + g + 1)
                        for lh in range(KD):
                            ins = pe.matmul(s2[g % 2][:, lh, :], ks[x.v][0:ROWS + 3, g, lh * P:(lh + 1) * P],
                                            qs[x.v][0:ROWS + 3, g, :], start=True, stop=True)
                        ins.then_inc(s2_full, 1)

                def values(x, q):
                    pe.wait_ge(s2_out, G * x.t + 4 * q + 4 + 2)
                    if q % 2 == 0:
                        wait(pe, o_out, 2 * x.t + q // 2)
                    for lh in range(KD):
                        for j in range(4):
                            g = 4 * q + j
                            ins = pe.matmul(o_ps[32 * j:32 * j + 32, q % 2, :], vt[x.v][:, lh, g, :], pr[g % 8][:, lh, :],
                                            start=(lh == 0), stop=(lh == KD - 1))
                    ins.then_inc(pv_done, 1)

                def slot(s):
                    x, last, done = s.plus(-1), s.plus(-2), s.plus(-3)
                    if s.live:
                        pe.wait_ge(placed[s.v], 32 * s.n)
                    for n in range(8 + LAG):
                        if s.live and n < 8:
                            first_pass(s, n)
                        gp = n - LAG
                        if n == 1 and last.live:
                            values(last, 3)
                        if n == 5 and done.live:
                            pe.wait_ge(rn_done, done.t + 1)
                            pe.wait_ge(mt_out, s.t if s.live else TILES)
                            wait(pe, rT_out, done.t)
                            for kd in range(KD):
                                ins = pe.transpose(tr[:, kd, :], rn[done.v][:, kd * P:(kd + 1) * P], k.ident[:])
                            ins.then_inc(rn_turned, 1)
                        if gp < 0:
                            continue
                        if x.live:
                            if gp == 0:
                                pe.wait_ge(m_placed[x.v], 48 * x.n)
                                pe.wait_ge(vt_done, 2 * x.t + 2)
                            second_pass(x, gp)
                            if gp in (2, 4, 6):
                                values(x, gp // 2 - 1)
                        if gp == 6 and s.live:
                            pe.wait_ge(m_split, s.t + 1)
                            wait(pe, rT_out, s.t - 2)
                            pe.transpose(trb[0:96, :], mp[s.v][:].rearrange("p a n -> p (a n)"), k.identb[:]).then_inc(mp_turned, 1)

                slots(pe, slot, TILES + 3)


class ChunkNorm:

    def __init__(self, k, name, sb):
        self.k = k
        self.r = [sb(f"r{u}", [P, TPC, D]) for u in range(2)]
        self.stats = [sb(f"stats{u}", [P, TPC, 6]) for u in range(2)]
        self.mv = [sb(f"mv{u}", [P, TPC, 2]) for u in range(2)]
        self.rstd = [sb(f"rstd{u}", [P, TPC]) for u in range(2)]
        self.rn = [sb(f"rn{u}", [P, TPC, D]) for u in range(2)]
        self.r_done, self.mv_done, self.rstd_done = k.sem(name + "_r_done"), k.sem(name + "_mv_done"), k.sem(name + "_rstd_done")
        self.rn_done, self.stored = k.sem(name + "_rn_done"), k.sem(name + "_resid_stored")
        self.stats_done, self.eps_done = k.sem(name + "_stats_done"), k.sem(name + "_eps_done")

    def statistics(self, dve, c, u):
        dve.wait_ge(self.r_done, c + 1)
        for t in range(TPC):
            ins = dve.bn_stats(self.stats[u][:, t, :], self.r[u][:, t, :])
        ins.then_inc(self.stats_done, 1)
        dve.wait_ge(self.stats_done, c + 1)
        dve.sem_inc(self.k.passed, 1)
        for t in range(TPC):
            ins = dve.bn_aggr(self.mv[u][:, t, :], self.stats[u][:, t, :])
        ins.then_inc(self.mv_done, 1)

    def variance_power(self, gp, c, u):
        gp.wait_ge(self.mv_done, c + 1)
        gp.sem_inc(self.k.passed, 1)
        gp.tensor_scalar(self.rstd[u][:], self.mv[u][:, :, 1], EPS, None, ALU.add).then_inc(self.eps_done, 1)
        gp.wait_ge(self.eps_done, c + 1)
        gp.tensor_tensor(self.rstd[u][:], self.rstd[u][:], self.k.mhalf[:, 0:TPC], ALU.pow).then_inc(self.rstd_done, 1)

    def apply(self, dve, c, u, i):
        dve.wait_ge(self.rstd_done, c + 1)
        dve.wait_ge(self.stored, 32 * i)
        for t in range(TPC):
            ins = dve.tensor_scalar(self.rn[u][:, t, :], self.r[u][:, t, :], self.mv[u][:, t, 0:1],
                                    self.rstd[u][:, t:t + 1], ALU.subtract, ALU.mult)
        ins.then_inc(self.rn_done, 1)

    def store(self, sp, c, u):
        sp.wait_ge(self.rn_done, c + 1)
        sp.dma_start(self.k.resid[:, ds(TPC * c, TPC), :], self.rn[u][:]).then_inc(self.stored, 16)

    def transpose(self, pe, c, u, tr):
        pe.wait_ge(self.rn_done, c + 1)
        for t in range(TPC):
            for kd in range(KD):
                ins = pe.transpose(tr[:, t, kd, :], self.rn[u][:, t, kd * P:(kd + 1) * P], self.k.ident[:])
        return ins

    def copy_turned(self, act, c, tr):
        for t in range(TPC):
            ins = act.activation(self.k.residT[:, :, ds(CHUNK * c + t * P, P)], tr[:, t, :, :], ACT.Copy)
        return ins


def choose_two(dve, st, logits, best, cand, top, masks, maxima, descending):
    E = logits.shape[-1]
    full = [P, TILES, E]
    for n in range(2):
        st.wait()
        st.done(dve.tensor_reduce(maxima[n][:], (logits if n == 0 else best)[:], AX.X, ALU.max))
        st.wait()
        st.done(dve.tensor_tensor(cand[:], (logits if n == 0 else best)[:],
                                  maxima[n][:].unsqueeze(2).broadcast_to(full), ALU.is_equal))
        st.wait()
        st.done(dve.tensor_tensor(cand[:], cand[:], descending[:].unsqueeze(1).broadcast_to(full), ALU.mult))
        st.wait()
        st.done(dve.tensor_reduce(top[:], cand[:], AX.X, ALU.max))
        st.wait()
        st.done(dve.tensor_tensor(masks[n][:], cand[:], top[:].unsqueeze(2).broadcast_to(full), ALU.is_equal))
        if n == 0:
            st.wait()
            st.done(dve.scalar_tensor_tensor(out=best[:], in0=masks[0][:], scalar=-BIG, in1=logits[:],
                                             op0=ALU.mult, op1=ALU.add))


def three_parts(dve, st, parts, value):
    for j in range(3):
        st.wait()
        st.done(dve.tensor_copy(parts[j], value))
        if j < 2:
            st.wait()
            st.done(dve.tensor_tensor(value, value, parts[j], ALU.subtract))


def experts_weights(k, ctx):
    E, HID, HT, RT = 8, 8 * 176 + 352, 14, 11
    k.ahead, k.ahead_in = [], k.sem("c_weights_in")
    w = {}
    for name, shape, dt in (("wr", [P, KD, E], F32), ("descending", [P, E], F32), ("spread", [3 * E, RT, P], BF16),
                            ("wg", [P, KD, HID], F32), ("wu", [P, KD, HID], F32), ("wd", [P, HT, D], F32)):
        w[name] = k.sb("c_" + name, shape, dt, ctx)
        k.ahead.append((w[name], k.io[name if name == "descending" else "c_" + name]))
    return w


def layer0_experts(k, w):
    nc, io, sem = k.nc, k.io, k.sem
    E, F, FS = 8, 176, 352
    HID = E * F + FS
    HT, RT = -(-HID // P), E * F // P
    LAST = HID - (HT - 1) * P
    rows = [P] * (HT - 1) + [LAST]
    with ExitStack() as ctx:
        def sb(name, shape, dt=F32):
            return k.sb("c_" + name, shape, dt, ctx)

        wr, wg, wu, wd, spread, descending = (w[n] for n in ("wr", "wg", "wu", "wd", "spread", "descending"))
        wT = sb("wT", [3 * E, NTOK], BF16)
        logits_full, logit_steps = sem("c_logits_full"), sem("c_logit_steps")
        exped, w_turned, wT_out = sem("c_exped"), sem("c_w_turned"), sem("c_wT_out")
        with ExitStack() as routing:
            def rb(name, shape, dt=F32):
                return k.sb("cr_" + name, shape, dt, routing)

            lg, best, cand = rb("lg", [P, TILES, E]), rb("best", [P, TILES, E]), rb("cand", [P, TILES, E])
            masks = [rb(f"mask{n}", [P, TILES, E]) for n in range(2)]
            maxima = [rb(f"max{n}", [P, TILES]) for n in range(2)]
            top, total, ex = rb("top", [P, TILES]), rb("total", [P, TILES]), rb("ex", [P, TILES, E])
            share = rb("w", [P, TILES, E])
            wp = rb("wp", [P, TILES, 3, E], BF16)
            lg_ps = k.ps("cps_lg", [P, TILES, E], F32, routing)
            wT_ps = k.ps("cps_wT", [3 * E, NTOK], BF16, routing)
            with nc.Block() as block:
                @block.tensor
                def _(pe):
                    pe.wait_ge(k.ahead_in, 16 * len(k.ahead))
                    for t in range(TILES):
                        for kd in range(KD):
                            ins = pe.matmul(lg_ps[:, t, :], k.residT[:, kd, t * P:(t + 1) * P], wr[:, kd, :],
                                            start=(kd == 0), stop=(kd == KD - 1))
                    ins.then_inc(logits_full, 1)
                    pe.wait_ge(w_turned, 1)
                    for t in range(TILES):
                        ins = pe.transpose(wT_ps[:, t * P:(t + 1) * P], wp[:, t].rearrange("p a e -> p (a e)"), k.identb[:])
                    ins.then_inc(w_turned, 1)

                @block.scalar
                def _(act):
                    act.wait_ge(exped, 1)
                    act.activation(ex[:], share[:], ACT.Exp).then_inc(exped, 1)

                @block.vector
                def _(dve):
                    full = [P, TILES, E]
                    st = Steps(dve, logit_steps, 0)
                    dve.wait_ge(logits_full, 1)
                    st.done(dve.tensor_copy(lg[:], lg_ps[:]))
                    choose_two(dve, st, lg, best, cand, top, masks, maxima, descending)
                    st.wait()
                    dve.tensor_tensor(share[:], lg[:], maxima[0][:].unsqueeze(2).broadcast_to(full), ALU.subtract).then_inc(exped, 1)
                    dve.wait_ge(exped, 2)
                    st.done(dve.tensor_reduce(total[:], ex[:], AX.X, ALU.add))
                    st.wait()
                    st.done(dve.reciprocal(total[:], total[:]))
                    st.done(dve.tensor_tensor(share[:], masks[0][:], masks[1][:], ALU.add))
                    st.wait()
                    st.done(dve.tensor_tensor(share[:], share[:], ex[:], ALU.mult))
                    st.wait()
                    st.done(dve.tensor_tensor(share[:], share[:], total[:].unsqueeze(2).broadcast_to(full), ALU.mult))
                    three_parts(dve, st, [wp[:, :, j, :] for j in range(3)], share[:])
                    st.wait()
                    dve.sem_inc(w_turned, 1)
                    dve.wait_ge(w_turned, 2)
                    dve.tensor_copy(wT[:], wT_ps[:]).then_inc(wT_out, 1)

        with ExitStack() as main:
            def mb(name, shape, dt=F32):
                return k.sb("cm_" + name, shape, dt, main)

            hid = [mb(f"hid{u}", [P, HT, CHUNK]) for u in range(2)]
            sg, prod = [mb(f"sg{n}", [P, CHUNK]) for n in range(2)], [mb(f"prod{n}", [P, CHUNK]) for n in range(2)]
            ln = ChunkNorm(k, "c", mb)
            g_ps = [k.ps(f"cps_g{n}", [P, CHUNK], F32, main) for n in range(2)]
            u_ps = [k.ps(f"cps_u{n}", [P, CHUNK], F32, main) for n in range(2)]
            w_ps = [k.ps(f"cps_w{n}", [P, CHUNK], F32, main) for n in range(2)]
            o_ps = k.ps("cps_o", [P, TPC, D], F32, main)
            turned = o_ps[:].rearrange("p t (kd n) -> p t kd n", kd=KD)
            up_full, silu_done, prod_done, h_done = sem("c_up_full"), sem("c_silu_done"), sem("c_prod_done"), sem("c_h_done")
            o_full, tr_full, tr_out = sem("c_o_full"), sem("c_tr_full"), sem("c_tr_out")
            with nc.Block() as block:
                @block.sync
                def _(sp):
                    with sp.Fori(0, NCHUNK // 2) as i:
                        for u in range(2):
                            ln.store(sp, 2 * i + u, u)
                    sp.wait_ge(ln.stored, 16 * NCHUNK)

                @block.gpsimd
                def _(gp):
                    with gp.Fori(0, NCHUNK // 2) as i:
                        for u in range(2):
                            ln.variance_power(gp, 2 * i + u, u)

                @block.scalar
                def _(act):
                    with act.Fori(0, NCHUNK // 2) as i:
                        for u in range(2):
                            for m in range(HT):
                                n = (2 * i + u) * HT + m
                                act.wait_ge(up_full, n + 1)
                                act.wait_ge(h_done, n + 1)
                                act.activation(sg[m % 2][0:rows[m]], g_ps[m % 2][0:rows[m]], ACT.Silu).then_inc(silu_done, 1)
                            if u == 1:
                                act.wait_ge(tr_full, 2 * i + 1)
                                ln.copy_turned(act, 2 * i, turned).then_inc(tr_out, 1)
                        act.wait_ge(tr_full, 2 * i + 2)
                        ln.copy_turned(act, 2 * i + 1, turned).then_inc(tr_out, 1)

                @block.vector
                def _(dve):
                    dve.sem_inc(h_done, 2)

                    def sums(i, u):
                        dve.wait_ge(o_full, 2 * i + u + 1)
                        dve.tensor_tensor(ln.r[u][:], o_ps[:], k.resid[:, ds(TPC * (2 * i + u), TPC), :], ALU.add
                                          ).then_inc(ln.r_done, 1)
                        ln.statistics(dve, 2 * i + u, u)

                    with dve.Fori(0, NCHUNK // 2) as i:
                        for u in range(2):
                            for m in range(HT):
                                n, rm = (2 * i + u) * HT + m, rows[m]
                                dve.wait_ge(silu_done, n + 1)
                                if m < RT:
                                    dve.tensor_tensor(prod[m % 2][:], sg[m % 2][:], u_ps[m % 2][:], ALU.mult).then_inc(prod_done, 1)
                                    dve.wait_ge(prod_done, (2 * i + u) * RT + m + 1)
                                    dve.tensor_tensor(hid[u][:, m, :], prod[m % 2][:], w_ps[m % 2][:], ALU.mult).then_inc(h_done, 1)
                                else:
                                    dve.tensor_tensor(hid[u][0:rm, m, :], sg[m % 2][0:rm], u_ps[m % 2][0:rm], ALU.mult).then_inc(h_done, 1)
                                if u == 1 and m == 11:
                                    sums(i, 0)
                                if u == 1 and m == 12:
                                    ln.apply(dve, 2 * i, 0, i)
                        sums(i, 1)
                        ln.apply(dve, 2 * i + 1, 1, i)

                @block.tensor
                def _(pe):
                    pe.wait_ge(wT_out, 1)

                    def down(i, u, t):
                        if t == 0:
                            pe.wait_ge(h_done, (2 * i + u + 1) * HT + 2)
                            pe.wait_ge(tr_out, 2 * i + u)
                        for m in range(HT):
                            ins = pe.matmul(o_ps[:, t, :], hid[u][0:rows[m], m, t * P:(t + 1) * P], wd[0:rows[m], m, :],
                                            start=(m == 0), stop=(m == HT - 1))
                        if t == TPC - 1:
                            ins.then_inc(o_full, 1)

                    with pe.Fori(0, NCHUNK // 2) as i:
                        for u in range(2):
                            for m in range(HT):
                                pe.wait_ge(h_done, (2 * i + u) * HT + m + 1)
                                tok = ds((2 * i + u) * CHUNK, CHUNK)
                                for w_, bank in ((wg, g_ps), (wu, u_ps)):
                                    for kd in range(KD):
                                        ins = pe.matmul(bank[m % 2][0:rows[m], :], w_[:, kd, m * P:m * P + rows[m]],
                                                        k.residT[:, kd, tok], start=(kd == 0), stop=(kd == KD - 1))
                                if m < RT:
                                    ins = pe.matmul(w_ps[m % 2][:], spread[:, m, :], wT[:, tok], start=True, stop=True)
                                ins.then_inc(up_full, 1)
                                if u == 1 and 3 <= m < 3 + 2 * TPC and m % 2 == 1:
                                    down(i, 0, (m - 3) // 2)
                        ln.transpose(pe, 2 * i, 0, turned).then_inc(tr_full, 1)
                        for t in range(TPC):
                            down(i, 1, t)
                        ln.transpose(pe, 2 * i + 1, 1, turned).then_inc(tr_full, 1)


def layer1_state_space(k):
    nc, io, sem = k.nc, k.io, k.sem
    NH, G, CW = 8, 4, 4
    XT, ZT = 6, 4
    MT = XT + ZT
    SPC = CHUNK // T
    order = [j for n in range(ZT) for j in (n, XT + n)] + list(range(ZT, XT))
    place = {m: n for n, m in enumerate(order)}
    beside = [range(0), range(0), range(0, 5), range(5, MT)]
    with ExitStack() as ctx:
        def sb(name, shape, dt=F32):
            return k.sb("d_" + name, shape, dt, ctx)

        def pair(name, shape, dt=F32):
            return [sb(f"{name}{u}", shape, dt) for u in range(2)]

        win, wout, nw = sb("win", [P, KD, MT * P]), sb("wout", [P, G, D]), sb("nw", [P, G])
        wdt, cw, cb = sb("wdt", [P, KD, NH]), sb("cw", [P, XT, CW]), sb("cb", [P, XT])
        bias, alog, dd = sb("bias", [P, NH]), sb("alog", [P, NH]), sb("dd", [P, NH])
        later, upto, eye = sb("later", [P, P]), sb("upto", [P, T]), sb("eye", [P, T])
        dt, an, ddiag = sb("dt", [P, TILES, NH]), sb("an", [P, NH]), sb("ddiag", [P, NH, T])
        dt_consts = ((wdt, "d_wdt"), (bias, "d_bias"), (alog, "d_alog"))
        consts = ((dd, "d_dd"), (eye, "d_eye"), (wout, "d_wout"), (nw, "d_nw"), (win, "d_win"), (cw, "d_cw"), (cb, "d_cb"),
                  (later, "d_later"), (upto, "d_upto"))
        dt_const, const, dt_full, pre, pre_act = sem("d_dt_const_in"), sem("d_const_in"), sem("d_dt_full"), sem("d_pre_steps"), sem("d_pre_act")
        with ExitStack() as first:
            def fb(name):
                return k.sb("df_" + name, [P, TILES, NH], F32, first)

            x, ab, e, s, q, p = (fb(n) for n in ("x", "ab", "e", "s", "q", "p"))
            dt_ps = k.ps("dps_dt", [P, TILES, NH], F32, first)
            with nc.Block() as block:
                @block.sync
                def _(sp):
                    for dst, src in dt_consts:
                        sp.dma_start(dst[:], io[src]).then_inc(dt_const, 16)
                    for dst, src in consts:
                        sp.dma_start(dst[:], io[src]).then_inc(const, 16)

                @block.tensor
                def _(pe):
                    pe.wait_ge(dt_const, 16 * len(dt_consts))
                    for t in range(TILES):
                        for kd in range(KD):
                            ins = pe.matmul(dt_ps[:, t, :], k.residT[:, kd, t * P:(t + 1) * P], wdt[:, kd, :],
                                            start=(kd == 0), stop=(kd == KD - 1))
                    ins.then_inc(dt_full, 1)

                @block.scalar
                def _(act):
                    act.wait_ge(dt_const, 16 * len(dt_consts))
                    act.activation(an[:], alog[:], ACT.Exp).then_inc(pre_act, 1)
                    act.wait_ge(pre_act, 2)
                    act.activation(e[:], ab[:], ACT.Exp, scale=-1.0).then_inc(pre_act, 1)

                @block.vector
                def _(dve):
                    st = Steps(dve, pre, 0)
                    dve.wait_ge(dt_const, 16 * len(dt_consts))
                    dve.wait_ge(dt_full, 1)
                    st.done(dve.tensor_tensor(x[:], dt_ps[:], bias[:].unsqueeze(1).broadcast_to([P, TILES, NH]), ALU.add))
                    st.wait()
                    st.done(dve.tensor_scalar(q[:], x[:], -1.0, None, ALU.mult))
                    st.wait()
                    dve.wait_ge(pre_act, 1)
                    dve.tensor_tensor(ab[:], x[:], q[:], ALU.max).then_inc(pre_act, 1)
                    st.done(dve.tensor_scalar(an[:], an[:], -1.0, None, ALU.mult))
                    dve.wait_ge(pre_act, 3)
                    st.done(dve.tensor_scalar(s[:], e[:], 2.0, None, ALU.add))
                    st.wait()
                    st.done(dve.reciprocal(s[:], s[:]))
                    st.wait()
                    st.done(dve.tensor_tensor(s[:], s[:], e[:], ALU.mult))
                    st.wait()
                    st.done(dve.tensor_tensor(q[:], s[:], s[:], ALU.mult))
                    st.wait()
                    st.done(dve.tensor_scalar(p[:], q[:], 1.0 / 15, None, ALU.mult))
                    for odd in (13, 11, 9, 7, 5, 3):
                        st.wait()
                        st.done(dve.scalar_tensor_tensor(out=p[:], in0=p[:], scalar=1.0 / odd, in1=q[:], op0=ALU.add, op1=ALU.mult))
                    st.wait()
                    st.done(dve.scalar_tensor_tensor(out=p[:], in0=p[:], scalar=1.0, in1=s[:], op0=ALU.add, op1=ALU.mult))
                    st.done(dve.tensor_scalar(x[:], x[:], 0.0, None, ALU.max))
                    st.wait()
                    st.done(dve.scalar_tensor_tensor(out=dt[:], in0=p[:], scalar=2.0, in1=x[:], op0=ALU.mult, op1=ALU.add))
                    dve.wait_ge(const, 16 * len(consts))
                    st.done(dve.tensor_tensor(ddiag[:], dd[:].unsqueeze(2).broadcast_to([P, NH, T]),
                                              eye[:].unsqueeze(1).broadcast_to([P, NH, T]), ALU.mult))
                    for g in range(G):
                        st.done(dve.tensor_scalar(wout[:, g, :], wout[:, g, :], nw[:, g:g + 1], None, ALU.mult))

        xc, bT, cT = pair("xc", [P, CHUNK]), pair("bT", [P, CHUNK]), pair("cT", [P, G, CHUNK])
        zs, yz, sq = pair("zs", [P, G, CHUNK]), pair("yz", [P, G, CHUNK]), sb("sq", [P, G, CHUNK])
        pad, acc = pair("pad", [P, SPC, CW - 1 + T]), pair("acc", [P, SPC, T])
        dtm, dam, es = pair("dtm", [P, NH, T]), pair("dam", [P, NH, T]), pair("es", [P, NH, T])
        xt, ms, rs = pair("xt", [P, P]), pair("ms", [P, TPC, G]), pair("rs", [P, TPC, G])
        ln = ChunkNorm(k, "d", sb)
        ip = k.ps("dps_ip", [P, 2, CHUNK], F32, ctx)
        tr = k.ps("dps_tr", [P, CHUNK], F32, ctx)
        g_ps, seg_ps = k.ps("dps_g", [P, CHUNK], F32, ctx), k.ps("dps_seg", [P, NH, T], F32, ctx)
        y_ps = k.ps("dps_y", [P, 2, CHUNK], F32, ctx)
        turned = ip[:].rearrange("p b (t kd n) -> p (b t) kd n", kd=KD, n=P)
        outs = [a[:].rearrange("p b (g f) -> p (b g) f", f=D) for a in (ip, y_ps)]

        def out_banks(u, t):
            return outs[t % 2 if u else 0]

        ip_full, ip_out, taps, conv_done = sem("d_ip_full"), sem("d_ip_out"), sem("d_taps"), sem("d_conv_done")
        conv_in, activated, padded = sem("d_conv_in"), sem("d_activated"), sem("d_padded")
        xt_full, xt_out, dtm_done, dam_done = sem("d_xt_full"), sem("d_xt_out"), sem("d_dtm_done"), sem("d_dam_done")
        g_full, g_out, seg_full, seg_out = sem("d_g_full"), sem("d_g_out"), sem("d_seg_full"), sem("d_seg_out")
        w_done, w_steps, y_full, y_out, sq_done = sem("d_w_done"), sem("d_w_steps"), sem("d_y_full"), sem("d_y_out"), sem("d_sq_done")
        ss_full, ss_out, rs_done = sem("d_ss_full"), sem("d_ss_out"), sem("d_rs_done")
        p_full, p_out, p_steps = sem("d_p_full"), sem("d_p_out"), sem("d_p_steps")
        tr_full, tr_out = sem("d_tr_full"), sem("d_tr_out")

        with nc.Block() as block:
            @block.sync
            def _(sp):
                for dst, src in k.ahead:
                    sp.dma_start(dst[:], src).then_inc(k.ahead_in, 16)
                with sp.Fori(0, NCHUNK // 2) as i:
                    for u in range(2):
                        ln.store(sp, 2 * i + u, u)
                sp.wait_ge(ln.stored, 16 * NCHUNK)

            @block.gpsimd
            def _(gp):
                for n in range(2):
                    gp.memset(pad[n][:, :, 0:CW - 1], 0.0).then_inc(padded, 1)
                with gp.Fori(0, NCHUNK // 2) as i:
                    def rms(u):
                        gp.wait_ge(ss_out, 2 * i + u + 1)
                        gp.tensor_tensor(rs[u][:].rearrange("p t g -> p (t g)"), ms[u][:].rearrange("p t g -> p (t g)"),
                                         k.mhalf[:, 0:TPC * G], ALU.pow).then_inc(rs_done, 1)

                    for u in range(2):
                        for t in range(TPC):
                            if u == 1 and t == 2:
                                rms(0)
                            c = 2 * i + u
                            gp.wait_ge(w_done, c * TPC + max(t - 1, 0))
                            gp.sem_inc(k.passed, 1)
                            gp.tensor_tensor(dtm[t % 2][:], dt[:, ds(c * TPC + t, 1), :].rearrange("p t h -> p (t h)")
                                             .unsqueeze(2).broadcast_to([P, NH, T]),
                                             upto[:].unsqueeze(1).broadcast_to([P, NH, T]), ALU.mult).then_inc(dtm_done, 1)
                            gp.wait_ge(dtm_done, c * TPC + t + 1)
                            gp.tensor_tensor(dam[t % 2][:], dtm[t % 2][:], an[:].unsqueeze(2).broadcast_to([P, NH, T]),
                                             ALU.mult).then_inc(dam_done, 1)
                    rms(1)
                    for u in range(2):
                        ln.variance_power(gp, 2 * i + u, u)

            @block.scalar
            def _(act):
                act.wait_ge(padded, 2)
                with act.Fori(0, NCHUNK // 2) as i:
                    def activate(u, m):
                        dest = [xc[u][:], bT[u][:]] + [cT[u][:, g, :] for g in range(G)]
                        act.wait_ge(conv_done, (2 * i + u) * XT + m + 1)
                        act.activation(dest[m], acc[m % 2][:].rearrange("p s t -> p (s t)"), ACT.Silu).then_inc(activated, 1)

                    def project(u, n):
                        c, m = 2 * i + u, order[n]
                        act.wait_ge(ip_full, c * MT + n + 1)
                        if m >= XT:
                            act.activation(zs[u][:, m - XT, :], ip[:, n % 2, :], ACT.Silu).then_inc(ip_out, 1)
                            return
                        src = ip[:, n % 2, :].rearrange("p (s t) -> p s t", t=T)
                        act.wait_ge(activated, c * XT + max(m - 1, 0))
                        act.activation(pad[m % 2][:, :, CW - 1:], src, ACT.Copy)
                        act.activation(acc[m % 2][:], src, ACT.Identity, bias=cb[:, m:m + 1],
                                       scale=cw[:, m, CW - 1:CW]).then_inc(ip_out, 1)
                        if m:
                            activate(u, m - 1)
                        if m == XT - 1:
                            activate(u, m)

                    for n in range(MT):
                        project(0, n)
                    for u in range(2):
                        c = 2 * i + u

                        def square(t):
                            act.wait_ge(y_out, c * TPC + t + 1)
                            act.wait_ge(ss_full, c)
                            cols = slice(t * P, (t + 1) * P)
                            act.activation(sq[:, :, cols], yz[u][:, :, cols], ACT.Square).then_inc(sq_done, 1)

                        for t in range(TPC):
                            act.wait_ge(xt_full, c * TPC + t + 1)
                            act.activation(xt[t % 2][:], tr[:, 0:P], ACT.Copy).then_inc(xt_out, 1)
                            act.wait_ge(seg_full, c * TPC + t + 1)
                            act.activation(es[t % 2][:], seg_ps[:], ACT.Exp).then_inc(seg_out, 1)
                            if t and u == 0:
                                square(t - 1)
                                for n in beside[t - 1]:
                                    project(1, n)
                        if u == 0:
                            square(TPC - 1)
                            for n in beside[TPC - 1]:
                                project(1, n)
                        else:
                            for t in range(TPC):
                                square(t)
                    for u in range(2):
                        act.wait_ge(tr_full, 2 * i + u + 1)
                        ln.copy_turned(act, 2 * i + u, turned).then_inc(tr_out, 1)

            @block.vector
            def _(dve):
                with dve.Fori(0, NCHUNK // 2) as i:
                    tap_st = [Steps(dve, taps, XT * (CW - 2), 2 * i + u) for u in range(2)]

                    def convolve(u, n):
                        c, m, st = 2 * i + u, order[n], tap_st[u]
                        if m >= XT:
                            return
                        dve.wait_ge(ip_out, c * MT + n + 1)
                        for tap in range(CW - 1):
                            ins = dve.scalar_tensor_tensor(out=acc[m % 2][:], in0=pad[m % 2][:, :, tap:tap + T],
                                                           scalar=cw[:, m, tap:tap + 1], in1=acc[m % 2][:],
                                                           op0=ALU.mult, op1=ALU.add)
                            if tap == CW - 2:
                                ins.then_inc(conv_done, 1)
                            else:
                                st.done(ins)
                                st.wait()
                        if m == XT - 1:
                            st.close()

                    for n in range(MT):
                        convolve(0, n)
                    p_st = [Steps(dve, p_steps, TPC * (G - 1), 2 * i + u) for u in range(2)]

                    def add_up(u, t):
                        c, st = 2 * i + u, p_st[u]
                        if t == 0:
                            dve.wait_ge(rs_done, c + 1)
                        dve.wait_ge(p_full, c * TPC + t + 1)
                        r = ln.r[u][:, t, :]
                        for g in range(G):
                            acc_in = r if g else k.resid[:, ds(c * TPC + t, 1), :].rearrange("p t f -> p (t f)")
                            ins = dve.scalar_tensor_tensor(out=r, in0=out_banks(u, t)[:, g, :], scalar=rs[u][:, t, g:g + 1],
                                                           in1=acc_in, op0=ALU.mult, op1=ALU.add)
                            if g < G - 1:
                                st.done(ins)
                                st.wait()
                            else:
                                ins.then_inc(p_out, 1)
                        if t == TPC - 1:
                            st.close()
                            dve.wait_ge(p_out, (c + 1) * TPC)
                            dve.sem_inc(ln.r_done, 1)
                            ln.statistics(dve, c, u)

                    for u in range(2):
                        c = 2 * i + u
                        st = Steps(dve, w_steps, TPC, c)

                        def weights(t):
                            n = c * TPC + t
                            dve.wait_ge(seg_out, n + 1)
                            dve.wait_ge(g_full, n + 1)
                            w = es[t % 2][:].rearrange("p (g a) l -> p g a l", a=2)
                            cols = g_ps[:, 0:G * T].rearrange("p (g l) -> p g l", l=T)
                            dve.tensor_tensor(w, w, cols.unsqueeze(2).broadcast_to([P, G, 2, T]), ALU.mult).then_inc(g_out, 1)
                            dve.wait_ge(g_out, n + 1)
                            st.done(dve.tensor_tensor(es[t % 2][:], es[t % 2][:], dtm[t % 2][:], ALU.mult))
                            st.wait()
                            dve.tensor_tensor(es[t % 2][:], es[t % 2][:], ddiag[:], ALU.add).then_inc(w_done, 1)

                        def gated(t):
                            dve.wait_ge(y_full, c * TPC + t + 1)
                            view = [a[:, :, t * P:(t + 1) * P].rearrange("p g (b l) -> p b g l", b=2) for a in (yz[u], zs[u])]
                            y = y_ps[:, :, 0:G * T].rearrange("p b (g l) -> p b g l", l=T)
                            dve.tensor_tensor(view[0], y, view[1], ALU.mult).then_inc(y_out, 1)

                        for t in range(TPC):
                            weights(t)
                            if t:
                                gated(t - 1)
                            if u == 0 and t:
                                for n in beside[t - 1]:
                                    convolve(1, n)
                            if u == 1 and t:
                                add_up(0, t - 1)
                        gated(TPC - 1)
                        if u == 0:
                            for n in beside[TPC - 1]:
                                convolve(1, n)
                        if u == 1:
                            add_up(0, TPC - 1)
                        st.close()
                        dve.wait_ge(ss_full, c + 1)
                        dve.tensor_scalar(ms[u][:].rearrange("p t g -> p (t g)"), tr[:, 0:TPC * G], 1.0 / P, EPS,
                                          ALU.mult, ALU.add).then_inc(ss_out, 1)
                    for t in range(TPC):
                        add_up(1, t)
                    for u in range(2):
                        ln.apply(dve, 2 * i + u, u, i)

            @block.tensor
            def _(pe):
                with pe.Fori(0, NCHUNK // 2) as i:
                    def project(u, n):
                        c, m = 2 * i + u, order[n]
                        pe.wait_ge(ip_out, c * MT + max(n - 1, 0))
                        for kd in range(KD):
                            ins = pe.matmul(ip[:, n % 2, :], win[:, kd, m * P:(m + 1) * P],
                                            k.residT[:, kd, ds(c * CHUNK, CHUNK)], start=(kd == 0), stop=(kd == KD - 1))
                        ins.then_inc(ip_full, 1)

                    pe.wait_ge(tr_out, 2 * i)
                    for n in range(MT):
                        project(0, n)
                    def put_out(u, t):
                        c = 2 * i + u
                        if u == 0:
                            pe.wait_ge(ip_out, 2 * MT * (i + 1))
                            pe.wait_ge(p_out, c * TPC + t)
                        elif t < 2:
                            pe.wait_ge(y_out, 2 * TPC * (i + 1))
                            pe.wait_ge(p_out, c * TPC)
                        else:
                            pe.wait_ge(p_out, c * TPC + t - 1)
                        for g in range(G):
                            ins = pe.matmul(out_banks(u, t)[:, g, :], yz[u][:, g, t * P:(t + 1) * P], wout[:, g, :],
                                            start=True, stop=True)
                        ins.then_inc(p_full, 1)

                    for u in range(2):
                        c = 2 * i + u

                        def front(t):
                            n = c * TPC + t
                            cols = slice(t * P, (t + 1) * P)
                            if t == 0:
                                pe.wait_ge(activated, (c + 1) * XT)
                                pe.wait_ge(ss_out, c)
                            pe.wait_ge(xt_out, n)
                            pe.transpose(tr[:, 0:P], xc[u][:, cols], k.ident[:]).then_inc(xt_full, 1)
                            pe.wait_ge(dam_done, n + 1)
                            pe.wait_ge(seg_out, n)
                            pe.matmul(seg_ps[:], later[:], dam[t % 2][:], start=True, stop=True).then_inc(seg_full, 1)
                            pe.wait_ge(g_out, n)
                            pe.sem_inc(k.passed, 1)
                            for b in range(2):
                                seq = slice(t * P + b * T, t * P + (b + 1) * T)
                                ins = pe.matmul(g_ps[b * T:(b + 1) * T, 0:G * T], bT[u][:, seq], cT[u][:, :, seq],
                                                start=True, stop=True)
                            ins.then_inc(g_full, 1)

                        def mix(t):
                            n = c * TPC + t
                            pe.wait_ge(w_done, n + 1)
                            pe.wait_ge(xt_out, n + 1)
                            pe.wait_ge(y_out, n)
                            pe.sem_inc(k.passed, 1)
                            for b in range(2):
                                seq = slice(b * T, (b + 1) * T)
                                for a in range(2):
                                    ins = pe.matmul(y_ps[a * 64:(a + 1) * 64, b, 0:G * T], xt[t % 2][seq, a * 64:(a + 1) * 64],
                                                    es[t % 2][seq, a::2, :], start=True, stop=True)
                            ins.then_inc(y_full, 1)

                        front(0)
                        for t in range(TPC):
                            if t + 1 < TPC:
                                front(t + 1)
                            mix(t)
                            if u == 0:
                                for n in beside[t]:
                                    project(1, n)
                            else:
                                put_out(0, t)
                        pe.wait_ge(sq_done, (c + 1) * TPC)
                        pe.wait_ge(xt_out, (c + 1) * TPC)
                        for t in range(TPC):
                            for g in range(G):
                                ins = pe.matmul(tr[:, t * G + g:t * G + g + 1], sq[:, g, t * P:(t + 1) * P], k.ones[:, 0:1],
                                                start=True, stop=True)
                        ins.then_inc(ss_full, 1)
                    for t in range(TPC):
                        put_out(1, t)
                    for u in range(2):
                        pe.wait_ge(p_out, 2 * TPC * (i + 1))
                        pe.wait_ge(tr_out, 2 * i + u)
                        ln.transpose(pe, 2 * i + u, u, turned).then_inc(tr_full, 1)


def later_weights(k, ctx):
    k.ahead, k.ahead_in = [], k.sem("later_weights_in")
    w = {}
    shapes = [(f"e_{n}", [P, KD, D], F32) for n in ("wq", "wk", "wv", "wo", "wg")]
    shapes += [("e_nw", [P, KD], F32), ("e_mask", [P, TILES, T], mybir.dt.uint8)]
    shapes += [("f_gw", [P, KD, 8], F32), ("descending", [P, 8], F32), ("f_select", [22, 4, P], BF16),
               ("f_a1", [P, KD, P], F32), ("f_a3", [P, KD, P], F32), ("f_w1", [P, KD, 704], F32),
               ("f_w3", [P, KD, 704], F32), ("f_b1", [P, 704], F32), ("f_b3", [P, 704], F32),
               ("f_a2", [P, 6, P], F32), ("f_b2", [P, D], F32)]
    for name, shape, dt in shapes:
        w[name] = k.sb("w_" + name, shape, dt, ctx)
        k.ahead.append((w[name], k.io[name]))
    return w


def layer1_cross_attention(k, w):
    nc, io, sem = k.nc, k.io, k.sem
    RMS_EPS, FLOOR, TINY = 1e-6, -1e20, 1e-30
    PAIRS, GD = HEADS // 2, 2 * (HD + 1)
    with ExitStack() as ctx:
        def sb(name, shape, dt=F32):
            return k.sb("e_" + name, shape, dt, ctx)

        def three(name, shape, dt=F32):
            return [sb(f"{name}{v}", shape, dt) for v in range(3)]

        wq, wk, wv, wo, wg, nw, mask8 = (w["e_" + n] for n in ("wq", "wk", "wv", "wo", "wg", "nw", "mask"))
        neg = sb("neg", [P, TILES, T])
        rs, factors = sb("rs", [P, TILES]), sb("factors", [P, TILES, 2])
        squared, powered, pre = sem("e_squared"), sem("e_powered"), sem("e_pre_steps")
        with ExitStack() as first:
            junk = [k.sb(f"ef_junk{n}", [P, D], F32, first) for n in range(2)]
            with nc.Block() as block:
                @block.scalar
                def _(act):
                    for t in range(TILES):
                        if t > 1:
                            act.wait_ge(squared, t - 1)
                        act.activation(junk[t % 2][:], k.resid[:, t, :], ACT.Square, accum_out=rs[:, t:t + 1]).then_inc(squared, 1)

                @block.gpsimd
                def _(gp):
                    gp.wait_ge(powered, 1)
                    gp.tensor_tensor(rs[:], rs[:], k.mhalf[:, 0:TILES], ALU.pow).then_inc(powered, 1)

                @block.vector
                def _(dve):
                    st = Steps(dve, pre, 0)
                    dve.wait_ge(k.ahead_in, 16 * len(k.ahead))
                    for weight in (wq, wg):
                        for kd in range(KD):
                            dve.tensor_scalar(weight[:, kd, :], weight[:, kd, :], nw[:, kd:kd + 1], None, ALU.mult)
                    dve.tensor_scalar(neg[:], mask8[:], -1.0, BIG, ALU.add, ALU.mult)
                    dve.wait_ge(squared, TILES)
                    dve.tensor_scalar(rs[:], rs[:], 1.0 / D, RMS_EPS, ALU.mult, ALU.add).then_inc(powered, 1)
                    dve.wait_ge(powered, 2)
                    dve.tensor_scalar(factors[:, :, 0], rs[:], HD ** -0.5, None, ALU.mult)
                    dve.tensor_scalar(factors[:, :, 1], rs[:], -1.0, None, ALU.mult)

        xs, cs, qT = three("xs", [P, KD, P]), three("cs", [P, KD, P]), three("qT", [P, 2, P])
        fac, kbd, vbd = three("fac", [P, 2]), three("kbd", [P, 4, 4, T]), three("vbd", [P, 2, PAIRS, 2, HD + 1])
        sm, mx, pr, pt = three("sm", [P, 16, T]), three("mx", [P, 16]), three("pr", [P, 8, P]), three("pt", [P, 8, P])
        gate, total, yn, yT = three("gate", [P, D]), three("total", [P, 16]), three("yn", [P, 16, HD]), three("yT", [P, KD, P])
        ln = TileNorm(k, "e", sb)
        qk_ps, vg_ps = k.ps("eps_qk", [P, 4, P], F32, ctx), k.ps("eps_vg", [P, 2, D], F32, ctx)
        s_ps, pt_ps = k.ps("eps_s", [P, 2, 512], F32, ctx), k.ps("eps_pt", [P, 8, P], F32, ctx)
        y_ps, o_all = k.ps("eps_y", [P, 512], F32, ctx), k.ps("eps_o", [P, 4, P], F32, ctx)
        o_ps, o_tr = o_all[:, 0:KD, :].rearrange("p a b -> p (a b)"), o_all[:, KD:2 * KD, :]

        tiles_in = [sem(f"e_tiles_in{v}") for v in range(3)]
        vbd_set, fac_done = sem("e_vbd_set"), sem("e_factors_copied")
        qk_full, qT_out, kbd_done = sem("e_qk_full"), sem("e_qT_out"), sem("e_kbd_done")
        vg_full, vg_out, gate_done = sem("e_vg_full"), sem("e_vg_out"), sem("e_gate_done")
        s_full, s_out, shifted, exped = sem("e_s_full"), sem("e_s_out"), sem("e_shifted"), sem("e_exped")
        pt_full, pt_out, y_full, y_out = sem("e_pt_full"), sem("e_pt_out"), sem("e_y_full"), sem("e_y_out")
        y_turned, yT_out, o_full, o_out = sem("e_y_turned"), sem("e_yT_out"), sem("e_o_full"), sem("e_o_out")
        r_done, max_done, total_done = sem("e_r_done"), sem("e_max_done"), sem("e_total_done")

        with nc.Block() as block:
            @block.sync
            def _(sp):
                def slot(s):
                    if s.live:
                        wait(sp, vg_full, s.t - 2)
                        sp.dma_start(xs[s.v][:], k.residT[:, :, ds(s.t * P, P)]).then_inc(tiles_in[s.v], 16)
                        sp.dma_start(cs[s.v][:], k.ctxT[:, :, ds(s.t * P, P)]).then_inc(tiles_in[s.v], 16)
                    x = s.plus(-4)
                    if x.live:
                        ln.store(sp, x)

                slots(sp, slot, TILES + 4)
                ln.wait_stored(sp)

            @block.gpsimd
            def _(gp):
                for v in range(3):
                    gp.memset(vbd[v][:], 0.0).then_inc(vbd_set, 1)
                gp.wait_ge(vbd_set, 3)
                for v in range(3):
                    for h2 in range(2):
                        gp.memset(vbd[v][h2 * T:(h2 + 1) * T, :, :, h2, HD:], 1.0).then_inc(vbd_set, 1)

                def slot(s):
                    x = s.plus(-3)
                    if x.live:
                        ln.variance_power(gp, x)

                slots(gp, slot, TILES + 3)

            @block.scalar
            def _(act):
                act.wait_ge(vbd_set, 9)

                def slot(s):
                    m, x, l = s.plus(-1), s.plus(-2), s.plus(-3)
                    if s.live:
                        act.wait_ge(qk_full, s.t + 1)
                        act.activation(qT[s.v][:], qk_ps[:, 0:2, :], ACT.Copy).then_inc(qT_out, 1)
                    if m.live:
                        act.wait_ge(shifted, m.t + 1)
                        act.activation(pr[m.v][:].rearrange("p a b -> p (a b)"), sm[m.v][:].rearrange("p a b -> p (a b)"),
                                       ACT.Exp, scale=fac[m.v][:, 0:1]).then_inc(exped, 1)
                    if l.live:
                        ln.copy_turned(act, l, o_tr)
                    if s.live:
                        act.wait_ge(vg_full, s.t + 1)
                        v = vg_ps[:, 0, :].rearrange("p (b q d) -> p b q d", b=2, d=HD)
                        for h2 in range(2):
                            rows = slice(h2 * T, (h2 + 1) * T)
                            act.activation(vbd[s.v][rows, :, :, h2, 0:HD], v[rows], ACT.Copy)
                        act.wait_ge(fac_done, s.t + 1)
                        act.activation(gate[s.v][:], vg_ps[:, 1, :], ACT.Exp, scale=fac[s.v][:, 1:2]).then_inc(vg_out, 1)
                    if x.live:
                        act.wait_ge(y_turned, x.t + 1)
                        act.activation(yT[x.v][:], o_tr, ACT.Copy).then_inc(yT_out, 1)
                    if m.live:
                        act.wait_ge(pt_full, m.t + 1)
                        act.activation(pt[m.v][:], pt_ps[:], ACT.Copy).then_inc(pt_out, 1)

                slots(act, slot, TILES + 3)

            @block.vector
            def _(dve):
                def slot(s):
                    m, x, l = s.plus(-1), s.plus(-2), s.plus(-3)
                    if m.live:
                        dve.wait_ge(s_full, m.t + 1)
                        dve.tensor_tensor(sm[m.v][:], s_ps[:].rearrange("p r (h s) -> p (r h) s", s=T),
                                          neg[:, ds(m.t, 1), :].broadcast_to([P, 16, T]), ALU.add).then_inc(s_out, 1)
                        dve.wait_ge(s_out, m.t + 1)
                        dve.tensor_reduce(mx[m.v][:], sm[m.v][:], AX.X, ALU.max).then_inc(max_done, 1)
                        dve.wait_ge(max_done, 2 * m.t + 1)
                        dve.tensor_scalar(mx[m.v][:], mx[m.v][:], FLOOR, None, ALU.max).then_inc(max_done, 1)
                        dve.wait_ge(max_done, 2 * m.t + 2)
                        dve.tensor_tensor(sm[m.v][:], sm[m.v][:], mx[m.v][:].unsqueeze(2).broadcast_to([P, 16, T]),
                                          ALU.subtract).then_inc(shifted, 1)
                    if l.live:
                        ln.apply(dve, l)
                    if s.live:
                        dve.tensor_copy(fac[s.v][:], factors[:, ds(s.t, 1), :].rearrange("p t c -> p (t c)")).then_inc(fac_done, 1)
                    if x.live:
                        dve.wait_ge(y_full, x.t + 1)
                        y = y_ps[:, 0:16 * (HD + 1)].rearrange("p (h d) -> p h d", d=HD + 1)
                        dve.tensor_scalar(total[x.v][:], y[:, :, HD], TINY, None, ALU.max).then_inc(total_done, 1)
                        dve.wait_ge(total_done, 2 * x.t + 1)
                        dve.reciprocal(total[x.v][:], total[x.v][:]).then_inc(total_done, 1)
                        dve.wait_ge(total_done, 2 * x.t + 2)
                        dve.tensor_tensor(yn[x.v][:], y[:, :, 0:HD], total[x.v][:].unsqueeze(2).broadcast_to([P, 16, HD]),
                                          ALU.mult).then_inc(y_out, 1)
                    if s.live:
                        dve.wait_ge(qk_full, s.t + 1)
                        dve.wait_ge(qT_out, s.t + 1)
                        kT = qk_ps[:, 2:4, :].rearrange("p h (b s) -> p (h b) s", b=2)
                        dve.tensor_tensor(kbd[s.v][:], kT.unsqueeze(2).broadcast_to([P, 4, 4, T]),
                                          k.headmask[:].unsqueeze(1).unsqueeze(3).broadcast_to([P, 4, 4, T]),
                                          ALU.mult).then_inc(kbd_done, 1)
                    if s.live:
                        dve.wait_ge(vg_out, s.t + 1)
                        dve.tensor_scalar(gate[s.v][:], gate[s.v][:], 1.0, None, ALU.add).then_inc(gate_done, 1)
                        dve.wait_ge(gate_done, 2 * s.t + 1)
                        dve.reciprocal(gate[s.v][:], gate[s.v][:]).then_inc(gate_done, 1)
                    if x.live:
                        dve.wait_ge(o_full, x.t + 1)
                        dve.wait_ge(gate_done, 2 * x.t + 2)
                        dve.tensor_tensor(ln.r[x.v][:], o_ps, gate[x.v][:], ALU.mult).then_inc(o_out, 1)
                        dve.wait_ge(o_out, x.t + 1)
                        dve.tensor_tensor(ln.r[x.v][:].unsqueeze(1), ln.r[x.v][:].unsqueeze(1),
                                          k.resid[:, ds(x.t, 1), :], ALU.add).then_inc(r_done, 1)
                        dve.wait_ge(r_done, x.t + 1)
                        ln.statistics(dve, x)

                slots(dve, slot, TILES + 3)

            @block.tensor
            def _(pe):
                def queries_keys(x):
                    pe.wait_ge(tiles_in[x.v], 32 * x.n)
                    wait(pe, kbd_done, x.t)
                    for n, (w, src) in enumerate(((wq, xs), (wq, xs), (wk, cs), (wk, cs))):
                        for kd in range(KD):
                            ins = pe.matmul(qk_ps[:, n, :], w[:, kd, n % 2 * P:(n % 2 + 1) * P], src[x.v][:, kd, :],
                                            start=(kd == 0), stop=(kd == KD - 1))
                    ins.then_inc(qk_full, 1)

                def values_gate(x):
                    wait(pe, vg_out, x.t)
                    pe.sem_inc(k.passed, 1)
                    for b in range(2):
                        for h2 in range(2):
                            for kd in range(KD):
                                pe.matmul(vg_ps[h2 * T:(h2 + 1) * T, 0, b * P:(b + 1) * P], cs[x.v][:, kd, b * T:(b + 1) * T],
                                          wv[:, kd, h2 * P:(h2 + 1) * P], start=(kd == 0), stop=(kd == KD - 1))
                    for kd in range(KD):
                        ins = pe.matmul(vg_ps[:, 1, :], xs[x.v][:, kd, :], wg[:, kd, :], start=(kd == 0), stop=(kd == KD - 1))
                    ins.then_inc(vg_full, 1)

                def scores(x):
                    pe.wait_ge(kbd_done, x.t + 1)
                    wait(pe, s_out, x.t)
                    pe.sem_inc(k.passed, 1)
                    for r in range(2):
                        rows = slice(r * 64, r * 64 + 64)
                        for hh in range(2):
                            for b in range(2):
                                ins = pe.matmul(s_ps[b * T:(b + 1) * T, r, hh * 256:(hh + 1) * 256],
                                                qT[x.v][rows, hh, b * T:(b + 1) * T],
                                                kbd[x.v][rows, hh * 2 + b, :, :].rearrange("p h s -> p (h s)"),
                                                start=True, stop=True)
                    ins.then_inc(s_full, 1)

                def mix(x):
                    pe.wait_ge(pt_out, x.t + 1)
                    wait(pe, y_out, x.t)
                    pe.sem_inc(k.passed, 1)
                    for c in range(8):
                        q = (c // 2 % 2) * 4 + (c // 4) * 2 + c % 2
                        for b in range(2):
                            ins = pe.matmul(y_ps[b * T:(b + 1) * T, c * GD:(c + 1) * GD], pt[x.v][:, c, b * T:(b + 1) * T],
                                            vbd[x.v][:, b, q, :, :].rearrange("p h d -> p (h d)"), start=True, stop=True)
                    ins.then_inc(y_full, 1)

                def turn(dst, src, blocks, signal):
                    for c in range(blocks):
                        ins = pe.transpose(dst[:, c, :], src[:, c * P:(c + 1) * P], k.ident[:])
                    ins.then_inc(signal, 1)

                def slot(s):
                    m, x, l = s.plus(-1), s.plus(-2), s.plus(-3)
                    if m.live:
                        scores(m)
                    if s.live:
                        queries_keys(s)
                    if x.live:
                        mix(x)
                    if s.live:
                        values_gate(s)
                    if l.live:
                        ln.transpose(pe, l, o_tr)
                    if x.live:
                        pe.wait_ge(y_out, x.t + 1)
                        if l.live:
                            pe.wait_ge(ln.copied, l.t + 1)
                        turn(o_tr, yn[x.v][:].rearrange("p h d -> p (h d)"), KD, y_turned)
                    if m.live:
                        pe.wait_ge(exped, m.t + 1)
                        wait(pe, pt_out, m.t)
                        turn(pt_ps, pr[m.v][:].rearrange("p c n -> p (c n)"), 8, pt_full)
                    if x.live:
                        pe.wait_ge(yT_out, x.t + 1)
                        for c in range(KD):
                            ins = pe.matmul(o_ps, yT[x.v][:, c, :], wo[:, c, :], start=(c == 0), stop=(c == KD - 1))
                        ins.then_inc(o_full, 1)

                slots(pe, slot, TILES + 3)


def layer1_experts(k, w):
    nc, io, sem = k.nc, k.io, k.sem
    E, R, F, LORA_SCALE = 8, 16, 704, 32.0 / 16.0
    HT = -(-F // P)
    rows = [P] * (HT - 1) + [F - (HT - 1) * P]
    STACK = 2 * E + 2 * 3
    with ExitStack() as ctx:
        def sb(name, shape, dt=F32):
            return k.sb("f_" + name, shape, dt, ctx)

        gw, w1, w3, a1, a3, b1, b3, a2, b2, select = (w["f_" + n] for n in (
            "gw", "w1", "w3", "a1", "a3", "b1", "b3", "a2", "b2", "select"))
        desc, w2 = w["descending"], sb("w2", [P, HT, D])
        stack = sb("stack", [STACK, NTOK], BF16)
        w2_in, logits_full, logit_steps = sem("f_w2_in"), sem("f_logits_full"), sem("f_logit_steps")
        exped, turning, stack_out = sem("f_exped"), sem("f_turning"), sem("f_stack_out")
        with ExitStack() as routing:
            def rb(name, shape, dt=F32):
                return k.sb("fr_" + name, shape, dt, routing)

            lg, best, cand = rb("lg", [P, TILES, E]), rb("best", [P, TILES, E]), rb("cand", [P, TILES, E])
            masks, maxima = [rb(f"mask{n}", [P, TILES, E]) for n in range(2)], [rb(f"max{n}", [P, TILES]) for n in range(2)]
            top, e2, wk = rb("top", [P, TILES]), rb("e2", [P, TILES]), rb("w", [P, TILES, 2])
            pieces = rb("pieces", [P, TILES, STACK], BF16)
            lg_ps = k.ps("fps_lg", [P, TILES, E], F32, routing)
            stack_ps = k.ps("fps_stack", [STACK, NTOK], BF16, routing)
            with nc.Block() as block:
                @block.sync
                def _(sp):
                    sp.dma_start(w2[:], io["f_w2"]).then_inc(w2_in, 16)

                @block.tensor
                def _(pe):
                    pe.wait_ge(k.ahead_in, 16 * len(k.ahead))
                    for t in range(TILES):
                        for kd in range(KD):
                            ins = pe.matmul(lg_ps[:, t, :], k.residT[:, kd, t * P:(t + 1) * P], gw[:, kd, :],
                                            start=(kd == 0), stop=(kd == KD - 1))
                    ins.then_inc(logits_full, 1)
                    pe.wait_ge(turning, 1)
                    for t in range(TILES):
                        ins = pe.transpose(stack_ps[:, t * P:(t + 1) * P], pieces[:, t, :], k.identb[:])
                    ins.then_inc(turning, 1)

                @block.scalar
                def _(act):
                    act.wait_ge(exped, 1)
                    act.activation(e2[:], top[:], ACT.Exp).then_inc(exped, 1)

                @block.vector
                def _(dve):
                    st = Steps(dve, logit_steps, 0)
                    dve.wait_ge(logits_full, 1)
                    st.done(dve.tensor_copy(lg[:], lg_ps[:]))
                    choose_two(dve, st, lg, best, cand, top, masks, maxima, desc)
                    st.wait()
                    for n in range(2):
                        st.done(dve.tensor_copy(pieces[:, :, n * E:(n + 1) * E], masks[n][:]))
                    st.wait()
                    dve.tensor_tensor(top[:], maxima[1][:], maxima[0][:], ALU.subtract).then_inc(exped, 1)
                    dve.wait_ge(exped, 2)
                    st.done(dve.tensor_scalar(top[:], e2[:], 1.0, None, ALU.add))
                    st.wait()
                    st.done(dve.reciprocal(wk[:, :, 0], top[:]))
                    st.wait()
                    st.done(dve.tensor_tensor(wk[:, :, 1], wk[:, :, 0], e2[:], ALU.mult))
                    parts = pieces[:, :, 2 * E:].rearrange("p t (n j) -> p t n j", n=2)
                    three_parts(dve, st, [parts[:, :, :, j] for j in range(3)], wk[:])
                    st.wait()
                    dve.sem_inc(turning, 1)
                    dve.wait_ge(turning, 2)
                    dve.tensor_copy(stack[:], stack_ps[:]).then_inc(stack_out, 1)

        hid = [sb(f"hid{u}", [P, HT, CHUNK]) for u in range(2)]
        sg, prod = [sb(f"sg{n}", [P, CHUNK]) for n in range(2)], [sb(f"prod{n}", [P, CHUNK]) for n in range(2)]
        aw = [[sb(f"aw{s}{n}", [P, CHUNK]) for n in range(2)] for s in range(3)]
        kept = [[sb(f"kept{s}{n}", [P, CHUNK]) for n in range(2)] for s in range(2)]
        both = [[sb(f"both{s}{n}", [P, CHUNK]) for n in range(2)] for s in range(2)]
        mask, weight, change = [sb(f"mask{n}", [P, CHUNK]) for n in range(2)], [sb(f"weight{n}", [P, CHUNK]) for n in range(2)], sb("change", [P, CHUNK])
        inner = [[sb(f"inner{a}{n}", [P, CHUNK]) for n in range(2)] for a in range(2)]
        z = [sb(f"z{n}", [P, CHUNK]) for n in range(2)]
        ln = ChunkNorm(k, "f", sb)
        h_ps = [[k.ps(f"fps_h{s}{n}", [P, CHUNK], F32, ctx) for n in range(2)] for s in range(2)]
        front = [k.ps(f"fps_front{n}", [P, CHUNK], F32, ctx) for n in range(2)]
        o_ps = k.ps("fps_o", [P, TPC, D], F32, ctx)
        front_full, front_out, changed = sem("f_front_full"), sem("f_front_out"), sem("f_changed")
        h_full, silu_done, h_read, aw_done = sem("f_h_full"), sem("f_silu_done"), sem("f_h_read"), sem("f_aw_done")
        prod_done = sem("f_prod_done")
        hid_done, low_out, z_done = sem("f_hid_done"), sem("f_low_out"), sem("f_z_done")
        o_full, low_used = sem("f_o_full"), sem("f_low_used")
        JOBS = 2 * HT
        order = [(0, 0)] + [j for m in range(1, HT) for j in ((m, 0), (m - 1, 1))] + [(HT - 1, 1)]
        place = {job: n for n, job in enumerate(order)}
        step = {job: place[job] + (job[1] if place[job] + 1 < JOBS else 0) for job in order}
        ready = sorted(order, key=lambda job: (step[job], job[1], job[0]))
        rank = {job: n for n, job in enumerate(ready)}
        y = io["out"].rearrange("(t p) d -> p t d", p=P)

        with nc.Block() as block:
            @block.sync
            def _(sp):
                with sp.Fori(0, NCHUNK // 2) as i:
                    for u in range(2):
                        c = 2 * i + u
                        sp.wait_ge(ln.rn_done, c + 1)
                        sp.dma_start(y[:, ds(TPC * c, TPC), :], ln.rn[u][:]).then_inc(ln.stored, 16)
                sp.wait_ge(ln.stored, 16 * NCHUNK)

            @block.gpsimd
            def _(gp):
                with gp.Fori(0, NCHUNK // 2) as i:
                    for u in range(2):
                        c = 2 * i + u
                        for m in range(HT):
                            gp.wait_ge(aw_done, c * JOBS + rank[m, 1] + 1)
                            if m == 0:
                                gp.wait_ge(o_full, 2 * i)
                            rm = rows[m]
                            gp.tensor_tensor(hid[u][0:rm, m, :], aw[m % 3][0][0:rm], aw[m % 3][1][0:rm], ALU.add).then_inc(hid_done, 1)
                        if u == 1:
                            ln.variance_power(gp, 2 * i, 0)
                    ln.variance_power(gp, 2 * i + 1, 1)

            @block.scalar
            def _(act):
                with act.Fori(0, NCHUNK // 2) as i:
                    for u in range(2):
                        c = 2 * i + u
                        for n, dst in enumerate((mask, weight)):
                            act.wait_ge(front_full, 3 * c + n + 1)
                            act.activation(dst[0][:], front[0][:], ACT.Copy)
                            act.activation(dst[1][:], front[1][:], ACT.Copy).then_inc(front_out, 1)
                        for n, (m, choice) in enumerate(order):
                            rm, s = rows[m], m % 2
                            act.wait_ge(prod_done, c * JOBS + (rank[order[n - 2]] + 1 if n >= 2 else 0))
                            if choice == 0:
                                act.wait_ge(h_full, c * JOBS + n + 1)
                                act.activation(sg[n % 2][0:rm], h_ps[n % 2][0][0:rm], ACT.Silu)
                                act.wait_ge(h_read, c * JOBS + (place[m - 2, 1] + 3 if m >= 2 else 2))
                                act.activation(kept[s][0][0:rm], h_ps[n % 2][0][0:rm], ACT.Copy)
                                act.activation(kept[s][1][0:rm], h_ps[n % 2][1][0:rm], ACT.Copy).then_inc(silu_done, 1)
                            else:
                                act.wait_ge(h_read, c * JOBS + n + 3)
                                act.activation(sg[n % 2][0:rm], both[s][0][0:rm], ACT.Silu).then_inc(silu_done, 1)

            @block.vector
            def _(dve):
                dve.sem_inc(h_read, 2)

                def sums(c, u):
                    dve.wait_ge(o_full, c + 1)
                    dve.tensor_tensor(ln.r[u][:], o_ps[:], k.resid[:, ds(TPC * c, TPC), :], ALU.add).then_inc(ln.r_done, 1)
                    ln.statistics(dve, c, u)

                with dve.Fori(0, NCHUNK // 2) as i:
                    for u in range(2):
                        c = 2 * i + u
                        dve.wait_ge(front_out, 3 * c + 1)
                        dve.tensor_tensor(change[:], mask[1][:], mask[0][:], ALU.subtract).then_inc(changed, 1)
                        dve.wait_ge(changed, c + 1)
                        dve.wait_ge(front_full, 3 * c + 3)
                        for n, by in enumerate((mask[0], change)):
                            for a in range(2):
                                ins = dve.tensor_tensor(inner[a][n][:], front[a][:], by[:], ALU.mult)
                        ins.then_inc(front_out, 1)
                        def take(m, choice):
                            rm, n = rows[m], place[m, choice]
                            dve.wait_ge(silu_done, c * JOBS + n + 1)
                            if choice == 0:
                                dve.tensor_tensor(prod[n % 2][0:rm], sg[n % 2][0:rm], h_ps[n % 2][1][0:rm], ALU.mult).then_inc(prod_done, 1)
                                dve.wait_ge(prod_done, c * JOBS + rank[m, choice] + 1)
                                dve.sem_inc(h_read, 1)
                            else:
                                dve.tensor_tensor(prod[n % 2][0:rm], sg[n % 2][0:rm], both[m % 2][1][0:rm], ALU.mult).then_inc(prod_done, 1)
                                dve.wait_ge(prod_done, c * JOBS + rank[m, choice] + 1)
                            dve.wait_ge(hid_done, c * HT + max(m - 2, 0))
                            dve.wait_ge(low_used, c * JOBS + (rank[m - 3, choice] + 1 if m >= 3 else 0))
                            dve.tensor_tensor(aw[m % 3][choice][0:rm], prod[n % 2][0:rm], weight[choice][0:rm], ALU.mult).then_inc(aw_done, 1)

                        for n, (m, choice) in enumerate(order):
                            if choice == 1:
                                rm = rows[m]
                                dve.wait_ge(h_full, c * JOBS + n + 1)
                                for j in range(2):
                                    ins = dve.tensor_tensor(both[m % 2][j][0:rm], kept[m % 2][j][0:rm], h_ps[n % 2][j][0:rm], ALU.add)
                                ins.then_inc(h_read, 1)
                            for job in ready:
                                if step[job] == n:
                                    take(*job)
                            if u == 1 and n == 3:
                                sums(2 * i, 0)
                        dve.wait_ge(low_used, (c + 1) * JOBS)
                        for n in range(2):
                            ins = dve.tensor_tensor(z[n][:], front[n][:], mask[n][:], ALU.mult)
                        ins.then_inc(low_out, 1)
                        dve.wait_ge(low_out, c + 1)
                        dve.tensor_tensor(z[0][:], z[0][:], z[1][:], ALU.add).then_inc(z_done, 1)
                        if u == 1:
                            ln.apply(dve, 2 * i, 0, i)
                    sums(2 * i + 1, 1)
                    ln.apply(dve, 2 * i + 1, 1, i)

            @block.tensor
            def _(pe):
                pe.wait_ge(stack_out, 1)
                pe.wait_ge(w2_in, 16)

                def lead(c, n):
                    if n == 0:
                        pe.wait_ge(low_out, c)
                    else:
                        pe.wait_ge(front_out, 3 * c + n)
                    pe.sem_inc(k.passed, 1)
                    tok = ds(c * CHUNK, CHUNK)
                    for j in range(2):
                        if n < 2:
                            ins = pe.matmul(front[j][:], select[:, 2 * n + j, :], stack[:, tok], start=True, stop=True)
                        else:
                            for kd in range(KD):
                                ins = pe.matmul(front[j][:], (a1, a3)[j][:, kd, :], k.residT[:, kd, tok],
                                                start=(kd == 0), stop=(kd == KD - 1))
                    ins.then_inc(front_full, 1)

                def base(c, n, m, j):
                    for kd in range(KD):
                        pe.matmul(h_ps[n % 2][j][0:rows[m], :], (w1, w3)[j][:, kd, m * P:m * P + rows[m]],
                                  k.residT[:, kd, ds(c * CHUNK, CHUNK)], start=(kd == 0), stop=False)

                def hidden(c, n, m, choice):
                    rm, cols = rows[m], slice(m * P, m * P + rows[m])
                    pe.wait_ge(h_read, c * JOBS + n + 1)
                    pe.sem_inc(k.passed, 1)
                    for j, b in enumerate((b1, b3)):
                        if choice == 0 and n > 0:
                            base(c, n, m, j)
                        ins = pe.matmul(h_ps[n % 2][j][0:rm, :], b[:, cols], inner[j][choice][:], start=(choice == 1), stop=True)
                    ins.then_inc(h_full, 1)

                def low(c, m, choice):
                    pe.wait_ge(aw_done, c * JOBS + rank[m, choice] + 1)
                    rm = rows[m]
                    pe.matmul(front[choice][:], a2[0:rm, m, :], aw[m % 3][choice][0:rm], start=(m == 0),
                              stop=(m == HT - 1)).then_inc(low_used, 1)

                def down(c, u, t):
                    if t == 0:
                        pe.wait_ge(hid_done, (c + 1) * HT)
                        pe.wait_ge(ln.r_done, c)
                        pe.wait_ge(z_done, c + 1)
                    for m in range(HT):
                        pe.matmul(o_ps[:, t, :], hid[u][0:rows[m], m, t * P:(t + 1) * P], w2[0:rows[m], m, :],
                                  start=(m == 0), stop=False)
                    ins = pe.matmul(o_ps[:, t, :], z[0][:, t * P:(t + 1) * P], b2[:], start=False, stop=True)
                    if t == TPC - 1:
                        ins.then_inc(o_full, 1)

                with pe.Fori(0, NCHUNK // 2) as i:
                    for u in range(2):
                        c = 2 * i + u
                        for n in range(3):
                            lead(c, n)
                            if n < 2:
                                if n == 0:
                                    pe.wait_ge(h_read, c * JOBS + 1)
                                base(c, 0, 0, n)
                            if u == 1:
                                down(c - 1, 0, n)
                        if u == 1:
                            down(c - 1, 0, 3)
                        pe.wait_ge(front_out, 3 * c + 3)
                        for n, (m, choice) in enumerate(order):
                            hidden(c, n, m, choice)
                            for job in ready:
                                if step[job] == n - 2:
                                    low(c, *job)
                        for job in ready:
                            if step[job] >= JOBS - 2:
                                low(c, *job)
                    for t in range(TPC):
                        down(2 * i + 1, 1, t)


def experts_layout(f, out, rows_to_parts):
    def padded(a):
        full = np.zeros((-(-a.shape[0] // P) * P, a.shape[1]), a.dtype)
        full[:a.shape[0]] = a
        return rows_to_parts(full)

    E, F = 8, 176
    out["c_wr"] = rows_to_parts(f["L0_ffn_Wr"].T)
    out["c_wg"] = rows_to_parts(np.concatenate([f["L0_ffn_Wg"].reshape(E * F, D), f["L0_ffn_Wsg"]]).T)
    out["c_wu"] = rows_to_parts(np.concatenate([f["L0_ffn_Wu"].reshape(E * F, D), f["L0_ffn_Wsu"]]).T)
    out["c_wd"] = padded(np.concatenate([f["L0_ffn_Wd"].transpose(0, 2, 1).reshape(E * F, D), f["L0_ffn_Wsd"].T]))
    unit = np.arange(E * F).reshape(-1, P) // F
    out["c_spread"] = np.tile(unit[None] == np.arange(E)[:, None, None], (3, 1, 1)).astype(mybir.dt.np(BF16))
    out["descending"] = np.tile(np.arange(E, 0, -1, dtype=np.float32)[None], (P, 1))


def state_space_layout(f, out, rows_to_parts):
    NH, G = 8, 4
    W = f["L1_attn_W_in"]
    DI, CONV = 512, 768
    out["d_win"] = rows_to_parts(np.concatenate([W[DI:DI + CONV], W[:DI]]).T)
    out["d_wdt"] = rows_to_parts(W[DI + CONV:].T)
    out["d_wout"] = rows_to_parts(f["L1_attn_W_out"].T)
    out["d_nw"] = f["L1_attn_norm_weight"].reshape(G, P).T
    out["d_cw"] = rows_to_parts(f["L1_attn_conv_w"])
    out["d_cb"] = f["L1_attn_conv_b"].reshape(-1, P).T
    for name, src in (("d_bias", "dt_bias"), ("d_alog", "A_log"), ("d_dd", "D")):
        out[name] = np.tile(f["L1_attn_" + src][None], (P, 1))
    row = np.arange(P)
    same = row[:, None] // T == row[None, :] // T
    out["d_later"] = (same & (row[:, None] > row[None, :])).astype(np.float32)
    out["d_upto"] = (row[:, None] % T <= np.arange(T)[None, :]).astype(np.float32)
    out["d_eye"] = (row[:, None] % T == np.arange(T)[None, :]).astype(np.float32)


def cross_layout(f, out, rows_to_parts, order):
    wq, wk, wv, wo, wg = (f["L1_xattn_" + n].T for n in ("wq", "wk", "wv", "wo", "wg"))
    for name, w in (("wq", wq), ("wk", wk), ("wg", wg)):
        out["e_" + name] = rows_to_parts(w)
    out["e_wv"] = rows_to_parts(wv.reshape(D, HEADS // 2, 2, HD).transpose(0, 2, 1, 3).reshape(D, D))
    out["e_wo"] = rows_to_parts(wo.reshape(HEADS, HD, D)[order].reshape(D, D))
    out["e_nw"] = f["L1_xattn_norm_w"].reshape(KD, P).T
    mask = f["mask_BxS2_bk0"].reshape(TILES, 2, T)
    out["e_mask"] = np.repeat(mask.transpose(1, 0, 2), T, axis=0)



def lora_layout(f, out, rows_to_parts):
    E, R, F = 8, 16, 704

    def padded(a):
        full = np.zeros((-(-a.shape[0] // P) * P, a.shape[1]), a.dtype)
        full[:a.shape[0]] = a
        return rows_to_parts(full)

    g = {n: f["L1_ffn_" + n] for n in ("gate_w", "w1", "w3", "w2", "a1", "b1", "a3", "b3", "a2", "b2")}
    out["f_gw"] = rows_to_parts(g["gate_w"].T)
    for n in ("w1", "w3"):
        out["f_" + n] = rows_to_parts(g[n].T)
    out["f_w2"] = padded(g["w2"].T)
    for n in ("a1", "a3"):
        out["f_" + n] = rows_to_parts(g[n].reshape(E * R, D).T)
    for n in ("b1", "b3", "b2"):
        out["f_" + n] = g[n].transpose(0, 2, 1).reshape(E * R, -1)
    out["f_a2"] = padded(g["a2"].reshape(E * R, F).T)
    select = np.zeros((2 * E + 6, 4, P), np.float32)
    for n in range(2):
        for e in range(E):
            select[n * E + e, n, e * R:(e + 1) * R] = 32.0 / 16.0
        select[2 * E + 3 * n:2 * E + 3 * n + 3, 2 + n, :] = 1.0
    out["f_select"] = select.astype(mybir.dt.np(BF16))


def layout(inputs):
    f = {n: np.asarray(a) for n, a in inputs.items()}

    def rows_to_parts(a):
        return np.ascontiguousarray(a.reshape(-1, P, a.shape[1]).transpose(1, 0, 2))

    def halves(a):
        return a.reshape(a.shape[0], -1, HALF, 2).transpose(0, 1, 3, 2).reshape(a.shape[0], -1)

    out = {}
    x = f["x"].reshape(NTOK, D)
    out["x"] = rows_to_parts(x)
    out["xT"] = rows_to_parts(x.T)
    out["a_wqkv"] = rows_to_parts(np.concatenate([halves(f["L0_attn_Wq"]), halves(f["L0_attn_Wk"]), f["L0_attn_Wv"]], 1))
    out["a_bias"] = np.concatenate([halves(f["L0_attn_bq"][None]), halves(f["L0_attn_bk"][None]),
                                    f["L0_attn_bv"][None]], 1)
    out["a_factor"] = np.tile(np.concatenate([f["L0_attn_alpha"], np.ones(GROUPS, np.float32)])[None], (P, 1))
    order = [hh * 8 + r * 4 + hq * 2 + h2 for r in range(2) for hh in range(2) for hq in range(2) for h2 in range(2)]
    out["a_wo"] = rows_to_parts(f["L0_attn_Wo"].reshape(HEADS, HD, D)[order].reshape(D, D))
    out["a_bo"] = f["L0_attn_bo"][None]
    inv_freq = np.float32(1.0) / np.float32(10000.0) ** (np.arange(0, HD, 2, dtype=np.float32) / np.float32(HD))
    freqs = np.arange(T, dtype=np.float32)[:, None] * inv_freq[None, :]
    cos, sin = np.cos(freqs), np.sin(freqs)
    out["cos"] = np.tile(np.concatenate([cos, cos], 1), (2, 1)).astype(np.float32)
    out["sin"] = np.tile(np.concatenate([-sin, sin], 1), (2, 1)).astype(np.float32)
    pos = np.arange(P) % T
    out["causal"] = np.where(np.arange(T)[None, :] <= pos[:, None], 0.0, -BIG).astype(np.float32)
    out["headmask"] = (np.arange(4)[None, :] == (np.arange(P)[:, None] % 64) // HD).astype(np.float32)
    ctx = f["ctx_2048"].reshape(NTOK, D)
    out["ctxT"] = rows_to_parts(ctx.T)
    out["ctx_dg"] = ctx.reshape(TILES, P // 8, 8, D).transpose(2, 1, 0, 3).reshape(P, TILES, D)
    out["b_gamma"] = np.full((P, 1), f["L0_xattn_gamma"], np.float32)
    more_layout(f, out, rows_to_parts, order)
    return {n: np.ascontiguousarray(a) for n, a in out.items()}


def more_layout(f, out, rows_to_parts, order):
    experts_layout(f, out, rows_to_parts)
    state_space_layout(f, out, rows_to_parts)
    cross_layout(f, out, rows_to_parts, order)
    lora_layout(f, out, rows_to_parts)


def decoder(nc, io):
    with ExitStack() as ctx:
        k = Kernel(nc, ctx, io)
        setup(k)
        with ExitStack() as weights:
            w = experts_weights(k, weights)
            layer0_attention(k)
            layer0_cross_attention(k)
            layer0_experts(k, w)
        k.recycle()
        with ExitStack() as weights:
            w = later_weights(k, weights)
            layer1_state_space(k)
            layer1_cross_attention(k, w)
            layer1_experts(k, w)


def kernel(**inputs):
    import concourse.bacc as _bacc
    from concourse.bass_utils import run_bass_kernel_spmd as _run

    nc = _bacc.Bacc("TRN2", target_bir_lowering=False, num_devices=1)
    arrays = {f"in_{name}": a for name, a in layout(inputs).items()}
    io = {name[3:]: nc.dram_tensor(name, a.shape, mybir.dt.from_np(a.dtype), kind="ExternalInput").ap()
          for name, a in arrays.items()}
    io["out"] = nc.dram_tensor("out", (NTOK, D), F32, kind="ExternalOutput").ap()
    decoder(nc, io)
    r = _run(nc, [arrays], core_ids=[0])
    return r.results[0]["out"].reshape(B, T, D)
```
